# Optimizing a Trainium2 kernel written in Bass

```python
import numpy as np
import jax
import jax.numpy as jnp

def _softmax(x, axis=-1):
    return jax.nn.softmax(x, axis=axis)

def _gelu(x):
    return jax.nn.gelu(x, approximate=True)

def _silu(x):
    return jax.nn.silu(x)

def _sigmoid(x):
    return jax.nn.sigmoid(x)

def _layernorm(x, axis=-1, eps=1e-05):
    m = jnp.mean(x, axis=axis, keepdims=True)
    v = jnp.var(x, axis=axis, keepdims=True)
    return (x - m) / jnp.sqrt(v + eps)

def _scatter_add(tgt, idx, src, axis=0):
    return tgt.at[idx].add(src)

def _segment_sum(src, seg, n):
    return jax.ops.segment_sum(src, seg, n)
kernel_name = 'mk_lm_tower_d1_tok_ids768_r4_b79e98'

def setup_inputs(seed: int=0):
    np.random.seed(seed)
    _w = jnp.asarray

    def _rec_inputs():
        import jax
        import jax.numpy as jnp
        _rk = jax.random.key(seed)
        x = jax.random.randint(jax.random.fold_in(_rk, 1), (2, 1024), 0, 250, jnp.int32)
        return x
    x = _rec_inputs()

    def _L0_tok_setup():
        import jax, jax.numpy as jnp
        import numpy as np
        TRACE_LR = 0.1
        TRACE_DECAY = 0.99
        ERASE_LR = 1.0
        N_HEADS = 8
        D_TRACE = 64

        def _layer_norm(x, gamma, beta, eps=1e-05):
            mu = jnp.mean(x, axis=-1, keepdims=True)
            var = jnp.mean(jnp.square(x - mu), axis=-1, keepdims=True)
            return (x - mu) * jax.lax.rsqrt(var + eps) * gamma + beta
        key = jax.random.key(seed)
        ks = jax.random.split(key, 8)
        B, S, V, D, HD = (8, 1024, 50257, 192, N_HEADS * D_TRACE)
        return {'input_ids': jax.random.randint(ks[0], (B, S), 0, 250), 'link_ids': jax.random.randint(ks[1], (8,), 0, 250), 'wte': jax.random.normal(ks[2], (V, D), jnp.float32), 'gamma': jnp.ones((D,), jnp.float32), 'beta': jnp.zeros((D,), jnp.float32), 'W_proj': jax.random.normal(ks[3], (HD, D), jnp.float32) * 0.02, 'W_val': jax.random.normal(ks[4], (HD, D), jnp.float32) * 0.02, 'W_out': jax.random.normal(ks[5], (D, HD), jnp.float32) * 0.02, 'value_traces': jax.random.normal(ks[6], (N_HEADS, D_TRACE, D_TRACE), jnp.float32) * 0.02}
    _L0_tok_all = _L0_tok_setup()
    _L0_tok_in = {k: v for k, v in _L0_tok_all.items() if k in ('link_ids', 'wte', 'gamma', 'beta', 'W_proj', 'W_val', 'W_out', 'value_traces')}
    del _L0_tok_all

    def _L0_attn_setup():
        import jax, jax.numpy as jnp
        import numpy as np
        DIM = 192
        GP_NUM = 49
        key = jax.random.key(seed)
        ks = jax.random.split(key, 7)
        b, n, d = (8, 512, DIM)
        s = d ** (-0.5)
        x = jax.random.normal(ks[0], (b, n, d), dtype=jnp.float32)
        W_qkv = jax.random.normal(ks[1], (d, 3 * d), dtype=jnp.float32) * s
        b_qkv = jnp.zeros((3 * d,), dtype=jnp.float32)
        W_proj = jax.random.normal(ks[2], (d, d), dtype=jnp.float32) * s
        b_proj = jnp.zeros((d,), dtype=jnp.float32)
        W_gp = jax.random.normal(ks[3], (d, GP_NUM), dtype=jnp.float32) * s
        alpha = jax.random.normal(ks[4], (), dtype=jnp.float32)
        return {'x': x, 'W_qkv': W_qkv, 'b_qkv': b_qkv, 'W_proj': W_proj, 'b_proj': b_proj, 'W_gp': W_gp, 'alpha': alpha}
    _L0_attn_all = _L0_attn_setup()
    _L0_attn_in = {k: v for k, v in _L0_attn_all.items() if k in ('W_qkv', 'b_qkv', 'W_proj', 'b_proj', 'W_gp', 'alpha')}
    del _L0_attn_all

    def _L0_ffn_setup():
        import jax, jax.numpy as jnp
        import numpy as np
        EPS_NORM = 1e-06
        EPS_LN = 1e-05

        def _layernorm(x, g, b):
            mu = jnp.mean(x, axis=-1, keepdims=True)
            var = jnp.mean(jnp.square(x - mu), axis=-1, keepdims=True)
            return (x - mu) * jax.lax.rsqrt(var + EPS_LN) * g + b
        key = jax.random.key(seed)
        ks = jax.random.split(key, 6)
        b, m, d = (8, 256, 192)
        n, p = (64, 16)
        h = 2 * d
        x = jax.random.normal(ks[0], (b, m, d), dtype=jnp.float32)
        phi = jax.random.normal(ks[1], (n, p, d), dtype=jnp.float32)
        ln_g = jnp.ones((n, d), dtype=jnp.float32)
        ln_b = jnp.zeros((n, d), dtype=jnp.float32)
        w1 = jax.random.normal(ks[2], (n, d, h), dtype=jnp.float32) * (1.0 / np.sqrt(d))
        b1 = jax.random.normal(ks[3], (n, h), dtype=jnp.float32) * 0.01
        w2 = jax.random.normal(ks[4], (n, h, d), dtype=jnp.float32) * (1.0 / np.sqrt(h))
        b2 = jax.random.normal(ks[5], (n, d), dtype=jnp.float32) * 0.01
        return {'x': x, 'phi': phi, 'ln_g': ln_g, 'ln_b': ln_b, 'w1': w1, 'b1': b1, 'w2': w2, 'b2': b2}
    _L0_ffn_all = _L0_ffn_setup()
    _L0_ffn_in = {k: v for k, v in _L0_ffn_all.items() if k in ('phi', 'ln_g', 'ln_b', 'w1', 'b1', 'w2', 'b2')}
    del _L0_ffn_all
    return {'x': x, 'L0_tok_link_ids': _L0_tok_in['link_ids'], 'L0_tok_wte': _L0_tok_in['wte'], 'L0_tok_gamma': _L0_tok_in['gamma'], 'L0_tok_beta': _L0_tok_in['beta'], 'L0_tok_W_proj': _L0_tok_in['W_proj'], 'L0_tok_W_val': _L0_tok_in['W_val'], 'L0_tok_W_out': _L0_tok_in['W_out'], 'L0_tok_value_traces': _L0_tok_in['value_traces'], 'L0_attn_W_qkv': _L0_attn_in['W_qkv'], 'L0_attn_b_qkv': _L0_attn_in['b_qkv'], 'L0_attn_W_proj': _L0_attn_in['W_proj'], 'L0_attn_b_proj': _L0_attn_in['b_proj'], 'L0_attn_W_gp': _L0_attn_in['W_gp'], 'L0_attn_alpha': _L0_attn_in['alpha'], 'L0_ffn_phi': _L0_ffn_in['phi'], 'L0_ffn_ln_g': _L0_ffn_in['ln_g'], 'L0_ffn_ln_b': _L0_ffn_in['ln_b'], 'L0_ffn_w1': _L0_ffn_in['w1'], 'L0_ffn_b1': _L0_ffn_in['b1'], 'L0_ffn_w2': _L0_ffn_in['w2'], 'L0_ffn_b2': _L0_ffn_in['b2']}

def reference(x, L0_tok_link_ids, L0_tok_wte, L0_tok_gamma, L0_tok_beta, L0_tok_W_proj, L0_tok_W_val, L0_tok_W_out, L0_tok_value_traces, L0_attn_W_qkv, L0_attn_b_qkv, L0_attn_W_proj, L0_attn_b_proj, L0_attn_W_gp, L0_attn_alpha, L0_ffn_phi, L0_ffn_ln_g, L0_ffn_ln_b, L0_ffn_w1, L0_ffn_b1, L0_ffn_w2, L0_ffn_b2):
    import jax
    import jax.numpy as jnp

    def _L0_tok_ref(input_ids, link_ids, wte, gamma, beta, W_proj, W_val, W_out, value_traces):
        import jax, jax.numpy as jnp
        import numpy as np
        TRACE_LR = 0.1
        TRACE_DECAY = 0.99
        ERASE_LR = 1.0
        N_HEADS = 8
        D_TRACE = 64

        def _layer_norm(x, gamma, beta, eps=1e-05):
            mu = jnp.mean(x, axis=-1, keepdims=True)
            var = jnp.mean(jnp.square(x - mu), axis=-1, keepdims=True)
            return (x - mu) * jax.lax.rsqrt(var + eps) * gamma + beta
        B, S = input_ids.shape
        H, dt = (N_HEADS, D_TRACE)
        tok = jax.lax.stop_gradient(wte[input_ids])
        Q = _layer_norm(tok, gamma, beta) @ W_proj.T
        Q = Q.reshape(B, S, H, dt).transpose(0, 2, 1, 3)
        V = (tok @ W_val.T).reshape(B, S, H, dt).transpose(0, 2, 1, 3)
        Q_store = Q[:, :, :-2, :]
        V_store = V[:, :, 2:, :]
        mid = input_ids[:, 1:-1]
        arrow_mask = (mid[:, :, None] == link_ids[None, None, :]).any(-1)
        Q_store = Q_store * arrow_mask[:, None, :, None].astype(Q.dtype)
        denom = jnp.maximum(arrow_mask.sum().astype(Q.dtype) * H, 1.0)
        Q_norm = jnp.clip(jnp.linalg.norm(Q_store, axis=-1, keepdims=True), 1e-08)
        Q_erase = Q_store / Q_norm
        V_old = jnp.einsum('bhip,hpq->bhiq', Q_erase, value_traces)
        erase = jnp.einsum('bhip,bhiq->hpq', Q_erase, V_old) / denom
        traces = value_traces - ERASE_LR * erase
        v_update = jnp.einsum('bhip,bhiq->hpq', Q_store, V_store) / denom
        traces = TRACE_DECAY * traces + TRACE_LR * v_update
        traces = jax.lax.stop_gradient(traces)
        Q_addr = jnp.concatenate([jnp.zeros_like(Q[:, :, :1, :]), Q[:, :, :-1, :]], axis=2)
        V_ret = jnp.einsum('bhsp,hpq->bhsq', Q_addr, traces)
        V_ret = V_ret.transpose(0, 2, 1, 3).reshape(B, S, H * dt)
        return V_ret @ W_out.T

    def _L0_attn_ref(x, W_qkv, b_qkv, W_proj, b_proj, W_gp, alpha):
        import jax, jax.numpy as jnp
        import numpy as np
        DIM = 192
        GP_NUM = 49
        d = x.shape[-1]
        scale = d ** (-0.5)
        qkv = x @ W_qkv + b_qkv
        q, k, v = jnp.split(qkv, 3, axis=-1)
        attn_scores = jnp.einsum('bnd,bmd->bnm', q, k) * scale
        gw = jax.nn.softmax(jax.nn.gelu(v @ W_gp, approximate=False), axis=-1)
        group_weight = jnp.einsum('bng,bmg->bnm', gw, gw)
        attn_scores = jax.nn.softmax(attn_scores * group_weight, axis=-1)
        a = jax.nn.sigmoid(alpha)
        attn_weights = (1.0 - a) * attn_scores + a * group_weight
        out = jnp.einsum('bnm,bmd->bnd', attn_weights, v)
        return out @ W_proj + b_proj

    def _L0_ffn_ref(x, phi, ln_g, ln_b, w1, b1, w2, b2):
        import jax, jax.numpy as jnp
        import numpy as np
        EPS_NORM = 1e-06
        EPS_LN = 1e-05

        def _layernorm(x, g, b):
            mu = jnp.mean(x, axis=-1, keepdims=True)
            var = jnp.mean(jnp.square(x - mu), axis=-1, keepdims=True)
            return (x - mu) * jax.lax.rsqrt(var + EPS_LN) * g + b
        phi_n = phi * jax.lax.rsqrt(jnp.sum(jnp.square(phi), axis=0, keepdims=True) + EPS_NORM)
        bsz, m, d = x.shape
        n, p, _ = phi_n.shape
        logits = jnp.einsum('bmd,npd->bmnp', x, phi_n)
        D = jax.nn.softmax(logits, axis=1)
        C = jax.nn.softmax(logits.reshape(bsz, m, n * p), axis=-1)
        Xs = jnp.einsum('bmd,bmnp->bnpd', x, D)
        hdn = _layernorm(Xs, ln_g[:, None, :], ln_b[:, None, :])
        hdn = jnp.einsum('bnpd,ndh->bnph', hdn, w1) + b1[:, None, :]
        hdn = jax.nn.gelu(hdn, approximate=False)
        Ys = jnp.einsum('bnph,nhd->bnpd', hdn, w2) + b2[:, None, :]
        Ys = Ys.reshape(bsz, n * p, d)
        Y = jnp.einsum('bsd,bms->bmd', Ys, C)
        return Y
    h = _L0_tok_ref(x, L0_tok_link_ids, L0_tok_wte, L0_tok_gamma, L0_tok_beta, L0_tok_W_proj, L0_tok_W_val, L0_tok_W_out, L0_tok_value_traces)
    h = h + _L0_attn_ref(_layernorm(h, axis=-1), L0_attn_W_qkv, L0_attn_b_qkv, L0_attn_W_proj, L0_attn_b_proj, L0_attn_W_gp, L0_attn_alpha)
    h = h + _L0_ffn_ref(_layernorm(h, axis=-1), L0_ffn_phi, L0_ffn_ln_g, L0_ffn_ln_b, L0_ffn_w1, L0_ffn_b1, L0_ffn_w2, L0_ffn_b2)
    return h

_drawn_inputs = setup_inputs


def setup_inputs(seed=0):
    import zlib

    import numpy as np

    out = dict(_drawn_inputs(seed))
    spreads = {'L0_tok_gamma': (1.0, 0.2),
     'L0_tok_beta': (0.0, 0.1),
     'L0_attn_b_qkv': (0.0, 0.1),
     'L0_attn_b_proj': (0.0, 0.1),
     'L0_ffn_ln_g': (1.0, 0.6),
     'L0_ffn_ln_b': (0.0, 0.626)}
    factors = {'L0_tok_W_val': 6.303, 'L0_ffn_b1': 50.187, 'L0_ffn_b2': 34.382}
    for name, (base, spread) in spreads.items():
        noise = np.random.default_rng([zlib.crc32(name.encode()), seed]).standard_normal(out[name].shape)
        drawn = base * np.exp(spread * noise) if base else spread * noise
        out[name] = jnp.asarray(drawn.astype(out[name].dtype))
    for name, factor in factors.items():
        out[name] = (out[name] * factor).astype(out[name].dtype)
    return out
```

```python
from contextlib import ExitStack

import concourse.bass as bass
from concourse import mybir

F32 = mybir.dt.float32
F32R = mybir.dt.float32r
I32 = mybir.dt.int32
ALU = mybir.AluOpType
ACT = mybir.ActivationFunctionType
AX = mybir.AxisListType.X

P = 128


def build(nc, a, out):
    NB, S = a["x"].shape
    D = a["L0_tok_wte"].shape[1]
    HD = a["L0_tok_W_proj"].shape[0]
    HEADS, DT, _ = a["L0_tok_value_traces"].shape
    G = a["L0_attn_W_gp"].shape[1]
    NE, NP, _ = a["L0_ffn_phi"].shape
    HID = a["L0_ffn_w1"].shape[2]
    NL = a["L0_tok_link_ids"].shape[0]
    DB = D - P
    Q = 64
    KT = S // P
    NT = NB * KT
    C = S // Q
    SLOTS = C + 1
    HP = HD // P
    PC = P + 3 * DB + 2
    CB1, CB2 = P, P + 2 * DB
    W2N = D + G + 1
    NS = NE * NP
    ST = NS // P
    EPT = P // NP
    GE = 4
    NG = NE // GE
    DH = D // 2
    HC = HID // P
    SCALE = float(D) ** -0.5
    TRACE_LR, TRACE_DECAY, ERASE_LR = 0.1, 0.99, 1.0

    ctx = ExitStack()
    early = ExitStack()
    front = ExitStack()
    late = ExitStack()
    moe_in = ExitStack()

    def sb(name, shape, dt=F32, where=None):
        return (where or ctx).enter_context(nc.sbuf_tensor(name, shape, dt))

    def sem(name):
        return ctx.enter_context(nc.semaphore(name))

    with ctx:
        ident = sb("ident", [P, P])
        res = sb("res", [P, NT, D])
        phAh = sb("phAh", [P, NS], F32R)
        phAl = sb("phAl", [P, NS], F32R)
        phB = sb("phB", [P, NS], F32R)
        lnT = sb("lnT", [DH, 4, NE])
        st6 = sb("st6", [P, NT, 6])
        mv = sb("mv", [P, NT, 2])
        ve = sb("ve", [P, NT])
        rstd = sb("rstd", [P, NT])
        nmr = sb("nmr", [P, NT])
        mhalf = sb("mhalf", [P, 32])
        aw = sb("aw", [P, 4])
        X1H = sb("X1H", [P, 2, NT * P], F32R, early)
        X1L = sb("X1L", [P, 2, NT * P], F32R, early)
        pr = sb("pr", [P, NT, W2N], where=early)
        x1t = sb("x1t", [P, 3, P + 2 * DB], where=early)
        wqkA = sb("wqkA", [P, 3 * D], where=early)
        wqkB = sb("wqkB", [DB, 3 * D], where=early)
        bcol = sb("bcol", [P, 2, 3], where=early)
        wpg = sb("wpg", [P, 2, D + G], where=early)
        bproj = sb("bproj", [P, D], where=early)
        wTq = sb("wTq", [P, 2, PC], where=early)
        wTk = sb("wTk", [P, 2, P + 2 * DB], where=early)
        wTv = sb("wTv", [P, 2, PC], where=early)
        kAh = sb("kAh", [P, P + 2 * DB], F32R, early)
        kAl = sb("kAl", [P, P + 2 * DB], F32R, early)
        kB1 = sb("kB1", [P, P + 2 * DB], F32R, early)
        kB2 = sb("kB2", [DB + 2, P + 2 * DB], F32R, early)
        vAh = sb("vAh", [P, W2N], F32R, early)
        vAl = sb("vAl", [P, W2N], F32R, early)
        vB1 = sb("vB1", [P, W2N], F32R, early)
        vB2 = sb("vB2", [DB + 2, W2N], F32R, early)
        ids = sb("ids", [P, C + 2], I32, front)
        idsf = sb("idsf", [P, C + 2], where=front)
        idx = sb("idx", [P, NB * (KT + 1)], I32, front)
        links = sb("links", [P, NL], I32, front)
        linkf = sb("linkf", [P, NL], where=front)
        valid = sb("valid", [P, C], where=front)
        eq = sb("eq", [P, C, NL], where=front)
        maskP = sb("maskP", [P, C], where=front)
        mask = sb("mask", [P, NT], where=front)
        msum = sb("msum", [P, 1], where=front)
        ones = sb("ones", [P, P], where=front)
        cnt = sb("cnt", [P, 4], where=front)
        rm = sb("rm", [P, NT], where=front)
        tok = sb("tok", [P, NB * (KT + 1), D], where=front)
        xh = sb("xh", [P, 3, P + 2 * DB], where=front)
        xm = sb("xm", [P, 3, D + 1], where=front)
        XH = sb("XH", [P, 2, NB * SLOTS * Q], F32R, front)
        XL = sb("XL", [P, 2, NB * SLOTS * Q], F32R, front)
        sq = sb("sq", [P, 2, HD], where=front)
        ss = sb("ss", [P, NT, HEADS], where=front)
        fac = sb("fac", [P, NT, HEADS], where=front)
        qe = sb("qe", [P, 2, HD], where=front)
        gam = sb("gam", [P, D], where=front)
        bet = sb("bet", [P, D], where=front)
        wp = sb("wp", [P, HP, D], where=front)
        wpt = sb("wpt", [P, HP, PC], where=front)
        wv = sb("wv", [P, HP, D], where=front)
        woA = sb("woA", [P, HD], where=front)
        woB = sb("woB", [DB, HD], where=front)
        vt = sb("vt", [P, HP, DT], where=front)
        wpAh = sb("wpAh", [P, HD], F32R, front)
        wpAl = sb("wpAl", [P, HD], F32R, front)
        wpB1 = sb("wpB1", [P, HD], F32R, front)
        wpB2 = sb("wpB2", [DB + 2, HD], F32R, front)
        wpT = sb("wpT", [P, 2, HD], where=front)
        wvT = sb("wvT", [P, 2, HD], where=front)
        woT = sb("woT", [P, HP, D], where=front)
        eyeP = sb("eyeP", [P, DT], where=front)
        cc = sb("cc", [P, 2, D], where=front)
        r1 = sb("r1", [P, HP, DT], where=front)
        bs = sq
        tt = sb("tt", [P, HP, DT], where=front)
        mm_ = qe[:].rearrange("p a b -> p (a b)")[:, 0:HP * D].rearrange("p (t c) -> p t c", t=HP)
        nAh = sb("nAh", [P, D], F32R, front)
        nAl = sb("nAl", [P, D], F32R, front)
        nB1 = sb("nB1", [P, D], F32R, front)
        nB2 = sb("nB2", [DB + 2, D], F32R, front)
        front.close()
        qAh = sb("qAh", [P, NT * P], F32R, late)
        qAl = sb("qAl", [P, NT * P], F32R, late)
        qB = sb("qB", [P, NT * P], F32R, late)
        gw = sb("gw", [P, NT, P], where=late)
        gm = sb("gm", [P, NT], where=late)
        gs = sb("gs", [P, NT], where=late)
        gD = sb("gD", [P, NT * P], F32R, late)
        gL = sb("gL", [P, NT * P], F32R, late)
        gP = sb("gP", [P, NT * P], F32R, late)
        uP = sb("uP", [P, NB, D], F32R, late)
        zz = sb("zz", [P, 2, S], where=late)
        gws = sb("gws", [P, S], where=late)
        et = sb("et", [P, KT, P], where=late)
        nmx = sb("nmx", [P, NT], where=late)
        rsum = sb("rsum", [P, NT], where=late)
        rinv = sb("rinv", [P, NT], where=late)
        cn = sb("cn", [P, NT], where=late)
        o1 = sb("o1", [P, D], where=late)
        phn = sb("phn", [NE, NP, P + 2 * DB], where=late)
        phT = sb("phT", [P, 2, NS], where=late)
        pss = sb("pss", [P, 2, NP], where=late)
        prs = sb("prs", [P, 2, NP], where=late)
        lnn = sb("lnn", [NE, 2, D], where=late)
        late.close()
        early.close()
        ec = sb("ec", [P, NT, NS])
        rsC = sb("rsC", [P, NT])
        riC = sb("riC", [P, NT])
        nmC = sb("nmC", [P, NT])
        nmD = sb("nmD", [P, NB * ST])
        csD = sb("csD", [P, NB * ST])
        ciD = sb("ciD", [P, NB * ST])
        xsT = sb("xsT", [DH + 1, 2, NE, NB, NP])
        xs = sb("xs", [P, 2, D])
        w1r = [sb("w1r0", [DH + 1, GE, 2, HID])]
        w2r = [sb("w2r0", [P, GE, HC, D])]
        b2r = [sb("b2r0", [P, D])]
        ls = sb("ls", [P, KT, NS], where=moe_in)
        dt_ = sb("dt_", [P, S], where=moe_in)
        ds = sb("ds", [P, KT, P], where=moe_in)
        x2 = sb("x2", [P, NT, D], where=moe_in)
        x2t = sb("x2t", [P, 2, P + 2 * DB], where=moe_in)
        X2H = sb("X2H", [P, 2, 2, P], F32R, moe_in)
        X2L = sb("X2L", [P, 2, 2, P], F32R, moe_in)
        moe_in.close()
        RING = 3
        for r in range(1, RING):
            w1r.append(sb(f"w1r{r}", [DH + 1, GE, 2, HID]))
            w2r.append(sb(f"w2r{r}", [P, GE, HC, D]))
            b2r.append(sb(f"b2r{r}", [P, D]))
        hs = sb("hs", [P, 2, HID])
        hT = sb("hT", [P, 2, HC, P])
        ysb = sb("ysb", [P, 2, D])
        ys = sb("ys", [P, 2, NB, D])
        ct = sb("ct", [P, 2, KT, P])
        ys_dram = nc.dram_tensor("ys_dram", [NG, P, D], F32, kind="Internal").ap()

        ps = ctx.enter_context(nc.psum_tensor("ps", [P, 8, 512], F32))

        def bank(k, n=1):
            return ps[:, k:k + n, :].rearrange("p k c -> p (k c)")

        names = """in_ids in_tok in_mix in_attn in_phi barrier
            v_chain a_chain p_chain
            idsf_ready ids_permuted idx_ready maskp_ready mask_permuted mask_ready msum_ready count_ready
            cnt_ready wpt_ready setup_filled setup_taken ones_ready half_ready
            front_stats front_rstd xh_ready xT_filled xh_copied xl_ready q_filled q_squared q_normed q_fac
            qe_ready gram_done cprime_done cc_ready   traces_part tt_ready mix_done
            mm_ready xl_ones wn_ready
            h_filled h_stats h_rstd h_taken x1_ready x1T_filled x1h_ready x1l_ready pr_filled pr_taken
            g_gelu g_shifted g_exp gw_ready gwT_filled gwT_hi gwT_taken
            u_filled u_taken qp_filled qph_taken qpl_taken  alpha_exp 
            s_filled gw_filled gw_copied z_ready e_ready et_filled et_copied_a et_copied_v o_filled o_taken
            norm_ready  ph_filled ph_copied ph_squared ph_summed ph_rsqrt ph_scaled ph_hi  ln_filled ln_taken
            f_stats f_rstd  x2t_ready x2T_filled x2h_ready x2l_ready l_filled  lmax_ready c_exp
            dT_filled dmax_ready d_exp d_filled d_copied_a d_copied_v xs_filled xs_sum xs_scaled xs_stats xs_rstd xs_norm xsT_filled
            xsT_ready xsT_ones
            hid_filled hid_gelu hT_filled hT_ready y_filled y_ready cT_filled cT_copied
            yp_filled yp_taken   stored""".split()
        m = {n: sem(n) for n in names}
        gathered = [sem(f"gathered{i}") for i in range(NB * (KT + 1))]
        ys_stored = [sem(f"ys_stored{i}") for i in range(2)]
        ys_loaded = [sem(f"ys_loaded{i}") for i in range(2)]
        w_loaded = [sem(f"w_loaded{r}") for r in range(RING)]

        ENGINES = 5

        def meet(eng, n):
            eng.drain().then_inc(m["barrier"], 1)
            eng.wait_ge(m["barrier"], ENGINES * n)

        block = ctx.enter_context(nc.Block())

        SETUP = ["wpA", "wpB1", "wpB2", "wqT", "wkT", "wvT3", "kA", "kB1", "kB2", "vA", "vB1", "vB2",
                 "wvA", "wvB", "woA", "woB", "bpA", "bpB", "nA", "nB1", "nB2"]
        at = {n: k for k, n in enumerate(SETUP)}

        def setup_bank(name):
            return bank(6 + at[name] % 2)

        @block.sync
        def _(sp):
            x_rows = a["x"].rearrange("b (q c) -> (b q) c", c=C)
            sp.dma_start(ids[:, 0:C], x_rows).then_inc(m["in_ids"], 16)
            sp.dma_start(ids[0:P - 1, C:C + 2], x_rows[1:P, 0:2]).then_inc(m["in_ids"], 16)
            sp.dma_start(ids[P - 1:P, C:C + 2], x_rows[P - 1:P, 0:2]).then_inc(m["in_ids"], 16)
            sp.dma_start(ident[:], a["c_ident"]).then_inc(m["in_ids"], 16)
            sp.dma_start(links[:], a["L0_tok_link_ids"].unsqueeze(0).broadcast_to([P, NL])).then_inc(m["in_tok"], 16)
            sp.dma_start(valid[:], a["c_valid"]).then_inc(m["in_tok"], 16)
            sp.dma_start(gam[:], a["L0_tok_gamma"].unsqueeze(0).broadcast_to([P, D])).then_inc(m["in_tok"], 16)
            sp.dma_start(bet[:], a["L0_tok_beta"].unsqueeze(0).broadcast_to([P, D])).then_inc(m["in_tok"], 16)
            sp.dma_start(wp[:], a["L0_tok_W_proj"].rearrange("(t p) d -> p t d", p=P)).then_inc(m["in_tok"], 16)
            sp.dma_start(wqkA[:], a["L0_attn_W_qkv"][0:P, :]).then_inc(m["in_attn"], 16)
            sp.dma_start(wqkB[:], a["L0_attn_W_qkv"][P:D, :]).then_inc(m["in_attn"], 16)
            bq = a["L0_attn_b_qkv"].rearrange("(y d) -> d y", y=3)
            sp.dma_start(bcol[:, 0, :], bq[0:P, :], allow_slow_non_contiguous=True).then_inc(m["in_attn"], 16)
            sp.dma_start(bcol[0:DB, 1, :], bq[P:D, :], allow_slow_non_contiguous=True).then_inc(m["in_attn"], 16)
            for c, (lo, n) in enumerate(((0, P), (P, DB))):
                sp.dma_start(wpg[0:n, c, 0:D], a["L0_attn_W_proj"][lo:lo + n, :]).then_inc(m["in_attn"], 16)
                sp.dma_start(wpg[0:n, c, D:D + G], a["L0_attn_W_gp"][lo:lo + n, :]).then_inc(m["in_attn"], 16)
            sp.dma_start(bproj[:], a["L0_attn_b_proj"].unsqueeze(0).broadcast_to([P, D])).then_inc(m["in_attn"], 16)
            sp.dma_start(aw[:, 0:1], a["L0_attn_alpha"].broadcast_to([P, 1])).then_inc(m["in_attn"], 16)
            sp.dma_start(wv[:], a["L0_tok_W_val"].rearrange("(t p) d -> p t d", p=P)).then_inc(m["in_mix"], 16)
            sp.dma_start(woA[:], a["L0_tok_W_out"][0:P, :]).then_inc(m["in_mix"], 16)
            sp.dma_start(woB[:], a["L0_tok_W_out"][P:D, :]).then_inc(m["in_mix"], 16)
            v4 = a["L0_tok_value_traces"].rearrange("(t r) p q -> r p t q", r=2)
            for r in range(2):
                sp.dma_start(vt[r * DT:(r + 1) * DT, :, :], v4[r]).then_inc(m["in_mix"], 16)
            meet(sp, 1)
            sp.dma_start(phn[:, :, 0:D], a["L0_ffn_phi"]).then_inc(m["in_phi"], 16)
            sp.dma_start(phn[:, :, D:D + DB], a["L0_ffn_phi"][:, :, P:D]).then_inc(m["in_phi"], 16)
            sp.dma_start(lnn[:, 0, :], a["L0_ffn_ln_g"]).then_inc(m["in_phi"], 16)
            sp.dma_start(lnn[:, 1, :], a["L0_ffn_ln_b"]).then_inc(m["in_phi"], 16)
            meet(sp, 2)

            def load_group(g):
                r = g % RING
                e = slice(GE * g, GE * g + GE)
                sp.dma_start(w1r[r][0:DH, :, :, :],
                             a["L0_ffn_w1"][e].rearrange("e (c r) h -> r e c h", c=2)).then_inc(w_loaded[r], 16)
                sp.dma_start(w1r[r][DH:DH + 1, :, 1, :], a["L0_ffn_b1"][e].unsqueeze(0)).then_inc(w_loaded[r], 16)
                sp.dma_start(w2r[r][:], a["L0_ffn_w2"][e].rearrange("e (c r) d -> r e c d", c=HC)).then_inc(w_loaded[r], 16)
                for j in range(GE):
                    sp.dma_start(b2r[r][32 * j:32 * j + 32, :],
                                 a["L0_ffn_b2"][GE * g + j:GE * g + j + 1, :].broadcast_to([32, D])).then_inc(w_loaded[r], 16)

            load_group(0)
            meet(sp, 3)
            load_group(1)
            load_group(2)
            for g in range(NG):
                sp.wait_ge(m["y_ready"], g + 1)
                sp.dma_start(ys_dram[g], ysb[:, g % 2, :]).then_inc(ys_stored[g % 2], 16)
                if g + RING < NG:
                    load_group(g + RING)
                t = g // 2
                sp.wait_ge(ys_stored[g % 2], 16 * (t + 1))
                if t >= 2 and g % 2 == 0:
                    sp.wait_ge(m["yp_filled"], NT * (t - 1))
                rows = slice((g % 2) * GE * NP, (g % 2 + 1) * GE * NP)
                y4 = ys_dram[g].rearrange("(j b s) d -> b j s d", b=NB, s=NP)
                for b in range(NB):
                    sp.dma_start(ys[rows, t % 2, b, :], y4[b]).then_inc(ys_loaded[t % 2], 16)
            o4 = out.rearrange("b (q c) d -> b q c d", c=C)
            for i in range(NT):
                b, k = divmod(i, KT)
                sp.wait_ge(m["yp_taken"], NT * (ST - 1) + i + 1)
                for jj in range(2):
                    sp.dma_start(o4[b, :, 2 * k + jj, :], res[jj * Q:(jj + 1) * Q, i, :]).then_inc(m["stored"], 16)
            sp.wait_ge(m["stored"], 16 * 2 * NT)

        @block.gpsimd
        def _(pool):
            pc = [0]

            def link(ins):
                pc[0] += 1
                ins.then_inc(m["p_chain"], 1)
                pool.wait_ge(m["p_chain"], pc[0])

            nc.gpsimd.memset(ones[:], 1.0).then_inc(m["ones_ready"], 1)
            link(nc.gpsimd.memset(mhalf[:], -0.5))
            pool.wait_ge(m["idx_ready"], 1)
            for i in range(NB * (KT + 1)):
                nc.gpsimd.indirect_dma_start(
                    tok[:, i, :], None, a["L0_tok_wte"], bass.IndirectOffsetOnAxis(ap=idx[:, i:i + 1], axis=0)
                ).then_inc(gathered[i], 16)
            nc.gpsimd.memset(XL[DB:P, 1, :].bitcast(F32), 1.0).then_inc(m["xl_ones"], 1)
            pool.wait_ge(m["xl_ones"], 1)
            nc.gpsimd.memset(X1L[DB:P, 1, :].bitcast(F32), 1.0).then_inc(m["xl_ones"], 1)
            pool.wait_ge(m["xl_ones"], 2)

            def rsqrt(i, eps):
                link(nc.gpsimd.tensor_scalar(ve[:, i:i + 1], mv[:, i, 1:2], eps, None, ALU.add))
                return nc.gpsimd.tensor_tensor(rstd[:, i:i + 1], ve[:, i:i + 1], mhalf[:, 0:1], ALU.pow)

            def head_factors(i):
                pool.wait_ge(m["q_normed"], i + 1)
                link(nc.gpsimd.tensor_scalar(fac[:, i, :], ss[:, i, :], 1e-16, None, ALU.max))
                link(nc.gpsimd.tensor_tensor(fac[:, i, :], fac[:, i, :], mhalf[:, 0:HEADS], ALU.pow))
                nc.gpsimd.tensor_scalar(fac[:, i, :], fac[:, i, :], mask[:, i:i + 1], None, ALU.mult).then_inc(m["q_fac"], 1)

            pool.wait_ge(m["mask_ready"], 1)
            for s in range(NT + 4):
                if s < NT:
                    pool.wait_ge(m["front_stats"], s + 1)
                    link(rsqrt(s, 1e-5))
                    nc.gpsimd.tensor_scalar(rm[:, s:s + 1], rstd[:, s:s + 1], mask[:, s:s + 1], None,
                                            ALU.mult).then_inc(m["front_rstd"], 1)
                if 3 <= s < NT + 3:
                    head_factors(s - 3)

            def ln_factors(i, eps, done):
                link(rsqrt(i, eps))
                nc.gpsimd.tensor_scalar(nmr[:, i:i + 1], mv[:, i, 0:1], rstd[:, i:i + 1], -1.0,
                                        ALU.mult, ALU.mult).then_inc(done, 1)

            for i in range(NT):
                pool.wait_ge(m["h_stats"], i + 1)
                ln_factors(i, 1e-5, m["h_rstd"])
            meet(pool, 1)
            nc.gpsimd.memset(gw[:], 0.0).then_inc(m["half_ready"], 1)
            pool.wait_ge(m["ph_summed"], 1)
            link(nc.gpsimd.tensor_scalar(prs[:], pss[:], 1e-6, None, ALU.add))
            nc.gpsimd.tensor_tensor(prs[:].rearrange("p c k -> p (c k)"), prs[:].rearrange("p c k -> p (c k)"),
                                    mhalf[:, 0:2 * NP], ALU.pow).then_inc(m["ph_rsqrt"], 1)
            meet(pool, 2)
            nc.gpsimd.memset(xsT[DH:DH + 1, 1, :, :, :], 1.0).then_inc(m["xsT_ones"], 1)
            pool.wait_ge(m["xsT_ones"], 1)
            for b in range(NB):
                for k in range(KT):
                    i = b * KT + k
                    pool.wait_ge(m["f_stats"], i + 1)
                    ln_factors(i, 1e-5, m["f_rstd"])
                for t in range(ST):
                    pool.wait_ge(m["xs_stats"], b * ST + t + 1)
                    ln_factors(b * ST + t, 1e-5, m["xs_rstd"])
            meet(pool, 3)

        @block.tensor
        def _(pe):
            mm = nc.tensor.matmul

            def fill(name):
                k = at[name]
                if k >= 2:
                    pe.wait_ge(m["setup_taken"], k - 1)
                return setup_bank(name)

            def filled(ins):
                ins.then_inc(m["setup_filled"], 1)

            def permute(dst, src, n):
                for b in range(NB):
                    for jj in range(2):
                        last = mm(dst[jj * Q:(jj + 1) * Q, b * n:(b + 1) * n], ident[:, b * Q:(b + 1) * Q],
                                  src[:, jj:2 * n:2], start=True, stop=True)
                return last

            def product(dst, xH, xL, wAh, wAl, wB1, wB2):
                mm(dst, xH(0, P), wAh, start=True, stop=False)
                mm(dst, xH(0, P), wAl, start=False, stop=False)
                mm(dst, xL(0, P), wAh, start=False, stop=False)
                mm(dst, xH(1, P), wB1, start=False, stop=False)
                return mm(dst, xL(1, DB + 2), wB2, start=False, stop=True)

            pe.wait_ge(m["in_ids"], 64)
            pe.wait_ge(m["idsf_ready"], 1)
            permute(bank(5), idsf, KT + 1).then_inc(m["ids_permuted"], 1)
            pe.wait_ge(m["maskp_ready"], 1)
            permute(bank(4), maskP, KT).then_inc(m["mask_permuted"], 1)
            pe.wait_ge(m["msum_ready"], 1)
            pe.wait_ge(m["ones_ready"], 1)
            mm(bank(3)[:, 0:1], ones[:], msum[:], start=True, stop=True).then_inc(m["count_ready"], 1)

            pe.wait_ge(m["wpt_ready"], 1)
            for name, lo, n in (("wpA", 0, P), ("wpB1", CB1, P), ("wpB2", CB2, DB + 2)):
                d = fill(name)
                for t in range(HP):
                    last = nc.tensor.transpose(d[0:n, t * P:(t + 1) * P], wpt[:, t, lo:lo + n], ident[:])
                filled(last)
            pe.wait_ge(m["in_attn"], 16 * 10)
            for y, name in enumerate(("wqT", "wkT", "wvT3")):
                d = fill(name)
                for c, (lo, n) in enumerate(((0, P), (P, DB))):
                    cols = slice(y * D + lo, y * D + lo + n)
                    nc.tensor.transpose(d[0:n, c * D:c * D + P], wqkA[:, cols], ident[:])
                    last = nc.tensor.transpose(d[0:n, c * D + P:(c + 1) * D], wqkB[:, cols], ident[0:DB, 0:DB])
                filled(last)
            pe.wait_ge(m["setup_taken"], at["wvT3"] + 1)
            for name, lo, n in (("kA", 0, P), ("kB1", CB1, P), ("kB2", CB2, DB + 2)):
                d = fill(name)
                mm(d[0:n, 0:P + 2 * DB], wTq[:, 0, lo:lo + n], wTk[:, 0, :], start=True, stop=False)
                filled(mm(d[0:n, 0:P + 2 * DB], wTq[0:DB, 1, lo:lo + n], wTk[0:DB, 1, :], start=False, stop=True))
            for name, lo, n in (("vA", 0, P), ("vB1", CB1, P), ("vB2", CB2, DB + 2)):
                d = fill(name)
                mm(d[0:n, 0:D + G], wTv[:, 0, lo:lo + n], wpg[:, 0, :], start=True, stop=False)
                mm(d[0:n, 0:D + G], wTv[0:DB, 1, lo:lo + n], wpg[0:DB, 1, :], start=False, stop=True)
                mm(d[0:n, D + G:W2N], wTq[:, 0, lo:lo + n], bcol[:, 0, 1:2], start=True, stop=False)
                filled(mm(d[0:n, D + G:W2N], wTq[0:DB, 1, lo:lo + n], bcol[0:DB, 1, 1:2], start=False, stop=True))
            pe.wait_ge(m["in_mix"], 16 * 5)
            for name, lo, n in (("wvA", 0, P), ("wvB", P, DB)):
                d = fill(name)
                for t in range(HP):
                    last = nc.tensor.transpose(d[0:n, t * P:(t + 1) * P], wv[:, t, lo:lo + n], ident[:])
                filled(last)
            d = fill("woA")
            for t in range(HP):
                last = nc.tensor.transpose(d[:, t * P:(t + 1) * P], woA[:, t * P:(t + 1) * P], ident[:])
            filled(last)
            d = fill("woB")
            for t in range(HP):
                last = nc.tensor.transpose(d[:, t * DB:(t + 1) * DB], woB[:, t * P:(t + 1) * P], ident[0:DB, 0:DB])
            filled(last)

            def slots(b, s):
                lo = (b * SLOTS + s) * Q
                return slice(lo, lo + P)

            gram = bank(4)[:, 0:HP * DT].rearrange("p (t c) -> p t c", t=HP)
            cpr = bank(5)

            def tok_T(i):
                pe.wait_ge(m["xh_ready"], i + 1)
                if i >= 2:
                    pe.wait_ge(m["xl_ready"], i - 1)
                d = bank(i % 2)
                nc.tensor.transpose(d[:, 0:P], xh[:, i % 3, 0:P], ident[:])
                nc.tensor.transpose(d[:, P:2 * P], xh[:, i % 3, P:P + 2 * DB], ident[:]).then_inc(m["xT_filled"], 1)

            def cprime(i):
                b, k = divmod(i, KT)
                nxt = b * (KT + 1) + k + 1
                pe.wait_ge(gathered[nxt], 16)
                mm(cpr[:, 0:D], xm[:, i % 3, 0:P], tok[:, nxt, :], start=(i == 0), stop=False, skip_group_check=True)
                mm(cpr[0:DB + 1, 256:256 + D], xm[:, i % 3, P:D + 1], tok[:, nxt, :], start=False, stop=False,
                   skip_group_check=True).then_inc(m["cprime_done"], 1)

            def q_proj(i):
                b, k = divmod(i, KT)
                pe.wait_ge(m["xl_ready"], i + 1)
                if i >= 2:
                    pe.wait_ge(m["qe_ready"], i - 1)
                c = slots(b, 2 * k + 1)
                product(bank(2 + i % 2), lambda h, n: XH[0:n, h, c], lambda h, n: XL[0:n, h, c],
                        wpAh[:], wpAl[:], wpB1[:], wpB2[:]).then_inc(m["q_filled"], 1)

            def grams(i):
                pe.wait_ge(m["qe_ready"], i + 1)
                for h in range(HEADS):
                    t, r = divmod(h, 2)
                    q = qe[:, i % 2, h * DT:(h + 1) * DT]
                    last = mm(gram[r * DT:(r + 1) * DT, t, :], q, q, start=(i == 0 and t == 0), stop=False,
                              skip_group_check=True)
                last.then_inc(m["gram_done"], 1)

            pe.wait_ge(m["cnt_ready"], 1)
            pe.wait_ge(m["xl_ones"], 1)
            for s in range(NT + 5):
                if 2 <= s < NT + 2:
                    q_proj(s - 2)
                if 4 <= s < NT + 4:
                    grams(s - 4)
                if 1 <= s < NT + 1:
                    tok_T(s - 1)
                    cprime(s - 1)

            pe.wait_ge(m["cc_ready"], 1)
            for name, lo, n in (("bpA", 0, P), ("bpB", P, DB)):
                d = fill(name)
                mm(d[0:n, :], cc[:, 0, lo:lo + n], wpT[:, 0, :], start=True, stop=False)
                filled(mm(d[0:n, :], cc[0:DB + 1, 1, lo:lo + n], wpT[0:DB + 1, 1, :], start=False, stop=True))
            pe.wait_ge(m["setup_taken"], at["bpB"] + 1)
            tr = bank(2)[:, 0:HP * DT].rearrange("p (t c) -> p t c", t=HP)
            for h in range(HEADS):
                t, r = divmod(h, 2)
                rows, cols = slice(r * DT, (r + 1) * DT), slice(h * DT, (h + 1) * DT)
                mm(tr[rows, t, :], vt[rows, t, :], r1[rows, t, :], start=True, stop=False).then_inc(m["traces_part"], 1)
                pe.wait_ge(m["traces_part"], 2 * h + 1)
                mm(tr[rows, t, :], wvT[:, 0, cols], bs[:, 0, cols], start=False, stop=False)
                mm(tr[rows, t, :], wvT[0:DB, 1, cols], bs[0:DB, 1, cols], start=False, stop=True
                   ).then_inc(m["traces_part"], 1)
                pe.wait_ge(m["traces_part"], 2 * h + 2)
            pe.wait_ge(m["tt_ready"], 1)
            for t in range(HP):
                d = bank(t // 2)[:, (t % 2) * 256:(t % 2) * 256 + D]
                for r in range(2):
                    rows = slice(r * DT, (r + 1) * DT)
                    last = mm(d[rows, :], tt[rows, t, :], woT[rows, t, :], start=True, stop=True)
            last.then_inc(m["mix_done"], 1)
            pe.wait_ge(m["mm_ready"], 1)
            for name, lo, n in (("nA", 0, P), ("nB1", CB1, P), ("nB2", CB2, DB + 2)):
                d = fill(name)
                for t in range(HP):
                    last = mm(d[0:n, 0:D], wpt[:, t, lo:lo + n], mm_[:, t, :], start=(t == 0), stop=(t == HP - 1))
                filled(last)
            pe.wait_ge(m["setup_taken"], len(SETUP))
            pe.wait_ge(m["wn_ready"], NB)

            def mixed(i):
                b, k = divmod(i, KT)
                if i >= 3:
                    pe.wait_ge(m["x1_ready"], i - 2)
                    pe.wait_ge(m["h_taken"], i - 2)
                c = slots(b, 2 * k)
                product(bank(i % 3)[:, 0:D], lambda h, n: XH[0:n, h, c], lambda h, n: XL[0:n, h, c],
                        nAh[:], nAl[:], nB1[:], nB2[:]).then_inc(m["h_filled"], 1)

            def x1_T(i):
                pe.wait_ge(m["x1_ready"], i + 1)
                if i >= 2:
                    pe.wait_ge(m["x1l_ready"], i - 1)
                d = bank(3 + i % 2)
                nc.tensor.transpose(d[:, 0:P], x1t[:, i % 3, 0:P], ident[:])
                nc.tensor.transpose(d[:, P:2 * P], x1t[:, i % 3, P:P + 2 * DB], ident[:]).then_inc(m["x1T_filled"], 1)

            def value_proj(i):
                pe.wait_ge(m["x1l_ready"], i + 1)
                if i >= 2:
                    pe.wait_ge(m["pr_taken"], i - 1)
                c = slice(i * P, (i + 1) * P)
                product(bank(5 + i % 2)[:, 0:W2N], lambda h, n: X1H[0:n, h, c], lambda h, n: X1L[0:n, h, c],
                        vAh[:], vAl[:], vB1[:], vB2[:]).then_inc(m["pr_filled"], 1)

            pe.wait_ge(m["xl_ones"], 2)
            for s in range(NT + 4):
                if s < NT:
                    mixed(s)
                if 2 <= s < NT + 2:
                    x1_T(s - 2)
                if 3 <= s < NT + 3:
                    value_proj(s - 3)
            meet(pe, 1)

            j = 0
            for blk in range(NT * P // 512):
                for c0, w in ((0, slice(0, P)), (1, slice(P, P + 2 * DB))):
                    if j >= 3:
                        pe.wait_ge(m["qpl_taken"], j - 2)
                    d = bank(j % 3)
                    n = slice(blk * 512, (blk + 1) * 512)
                    mm(d, kAh[:, w], X1H[:, 0, n], start=True, stop=False)
                    mm(d, kAl[:, w], X1H[:, 0, n], start=False, stop=False)
                    mm(d, kAh[:, w], X1L[:, 0, n], start=False, stop=False)
                    mm(d, kB1[:, w], X1H[:, 1, n], start=False, stop=False)
                    mm(d, kB2[:, w], X1L[0:DB + 2, 1, n], start=False, stop=True).then_inc(m["qp_filled"], 1)
                    j += 1
            pe.wait_ge(m["in_phi"], 64)
            for j in range(4):
                half, p8 = divmod(j, 2)
                if j >= 2:
                    pe.wait_ge(m["ph_copied"], j - 1)
                d = bank(3 + j % 2)
                for q in range(8):
                    last = nc.tensor.transpose(d[:, q * NE:(q + 1) * NE], phn[:, 8 * p8 + q, half * P:(half + 1) * P],
                                               ident[0:NE, 0:NE])
                last.then_inc(m["ph_filled"], 1)
            d = bank(5)
            for w in range(4):
                last = nc.tensor.transpose(d[0:DH, w * NE:(w + 1) * NE], lnn[:, w // 2, (w % 2) * DH:(w % 2 + 1) * DH],
                                           ident[0:NE, 0:NE])
            last.then_inc(m["ln_filled"], 1)
            pe.wait_ge(m["gw_ready"], 1)
            for j in range(NT // 4):
                d = bank(6 + j % 2)
                if j >= 2:
                    pe.wait_ge(m["gwT_taken"], j - 1)
                for q in range(4):
                    last = nc.tensor.transpose(d[:, q * P:(q + 1) * P], gw[:, 4 * j + q, :], ident[:])
                last.then_inc(m["gwT_filled"], 1)
            pe.wait_ge(m["qpl_taken"], 8)
            for b in range(NB):
                d = bank(b)[:, 0:D]
                for k in range(KT):
                    i = b * KT + k
                    last = mm(d, gw[:, i, :], pr[:, i, 0:D], start=(k == 0), stop=(k == KT - 1))
                last.then_inc(m["u_filled"], 1)
            pe.wait_ge(m["gwT_taken"], NT // 4)
            pe.wait_ge(m["u_taken"], NB)
            pe.wait_ge(m["ph_copied"], 4)
            pe.wait_ge(m["ln_taken"], 1)

            def scores(i):
                b = i // KT
                n = slice(i * P, (i + 1) * P)
                if i >= 1:
                    pe.wait_ge(m["z_ready"], i)
                for hf in range(2):
                    d = bank(hf)
                    c = slice(b * S + hf * 512, b * S + (hf + 1) * 512)
                    mm(d, qAh[:, n], X1H[:, 0, c], start=True, stop=False)
                    mm(d, qAl[:, n], X1H[:, 0, c], start=False, stop=False)
                    mm(d, qAh[:, n], X1L[:, 0, c], start=False, stop=False)
                    mm(d, qB[:, n], X1H[:, 1, c], start=False, stop=False)
                    last = mm(d, qB[0:DB, n], X1L[0:DB, 1, c], start=False, stop=True)
                last.then_inc(m["s_filled"], 1)
                if i >= 1:
                    pe.wait_ge(m["gw_copied"], i)
                for hf in range(2):
                    d = bank(2 + hf)
                    c = slice(b * S + hf * 512, b * S + (hf + 1) * 512)
                    mm(d, gP[0:DB + G, n], gD[0:DB + G, c], start=True, stop=False)
                    last = mm(d, gP[0:G, n], gL[0:G, c], start=False, stop=True)
                last.then_inc(m["gw_filled"], 1)

            def attend(i):
                b = i // KT
                n = slice(i * P, (i + 1) * P)
                pe.wait_ge(m["e_ready"], i + 1)
                if i >= 1:
                    pe.wait_ge(m["et_copied_a"], i)
                    pe.wait_ge(m["et_copied_v"], i)
                for k in range(KT):
                    last = nc.tensor.transpose(bank(4 + k // 4)[:, (k % 4) * P:(k % 4 + 1) * P],
                                               zz[:, i % 2, k * P:(k + 1) * P], ident[:])
                    if k % 4 == 3:
                        last.then_inc(m["et_filled"], 1)
                if i >= 2:
                    pe.wait_ge(m["o_taken"], i - 1)
                d = bank(6 + i % 2)
                mm(d[:, 256:256 + D], gD[0:DB + G, n], uP[0:DB + G, b, :], start=True, stop=False)
                mm(d[:, 256:256 + D], gL[0:G, n], uP[0:G, b, :], start=False, stop=True)
                for k in range(KT):
                    if k == 0:
                        pe.wait_ge(m["et_copied_a"], i + 1)
                    if k == KT // 2:
                        pe.wait_ge(m["et_copied_v"], i + 1)
                    last = mm(d[:, 0:D], et[:, k, :], pr[:, b * KT + k, 0:D], start=(k == 0), stop=(k == KT - 1))
                last.then_inc(m["o_filled"], 1)

            for s in range(NT + 1):
                if s < NT:
                    scores(s)
                if s >= 1:
                    attend(s - 1)
            meet(pe, 2)

            def x2_T(i):
                pe.wait_ge(m["x2t_ready"], i + 1)
                if i >= 2:
                    pe.wait_ge(m["x2l_ready"], i - 1)
                d = bank(6 + i % 2)
                nc.tensor.transpose(d[:, 0:P], x2t[:, i % 2, 0:P], ident[:])
                nc.tensor.transpose(d[:, P:2 * P], x2t[:, i % 2, P:P + 2 * DB], ident[:]).then_inc(m["x2T_filled"], 1)

            def logits(i):
                pe.wait_ge(m["x2l_ready"], i + 1)
                if i >= 2:
                    pe.wait_ge(m["c_exp"], i - 1)
                for hf in range(2):
                    d = bank(2 * (i % 2) + hf)
                    c = slice(hf * 512, (hf + 1) * 512)
                    xHt, xLt = X2H[:, i % 2], X2L[:, i % 2]
                    mm(d, xHt[:, 0, :], phAh[:, c], start=True, stop=False)
                    mm(d, xHt[:, 0, :], phAl[:, c], start=False, stop=False)
                    mm(d, xLt[:, 0, :], phAh[:, c], start=False, stop=False)
                    mm(d, xHt[:, 1, :], phB[:, c], start=False, stop=False)
                    last = mm(d, xLt[0:DB, 1, :], phB[0:DB, c], start=False, stop=True)
                last.then_inc(m["l_filled"], 1)

            def logits_T(j):
                b, t = divmod(j, ST)
                if t >= 2:
                    pe.wait_ge(m["d_exp"], j - 1)
                for k in range(KT):
                    last = nc.tensor.transpose(bank(2 * (t % 2) + k // 4)[:, (k % 4) * P:(k % 4 + 1) * P],
                                               ls[:, k, t * P:(t + 1) * P], ident[:])
                last.then_inc(m["dT_filled"], 1)

            def dispatch_T(j):
                b, t = divmod(j, ST)
                pe.wait_ge(m["d_exp"], j + 1)
                if j >= 1:
                    pe.wait_ge(m["d_copied_a"], j)
                    pe.wait_ge(m["d_copied_v"], j)
                for k in range(KT):
                    last = nc.tensor.transpose(bank(4 + k // 4)[:, (k % 4) * P:(k % 4 + 1) * P],
                                               dt_[:, k * P:(k + 1) * P], ident[:])
                    if k % 4 == 3:
                        last.then_inc(m["d_filled"], 1)

            def dispatch(j):
                b, t = divmod(j, ST)
                if j >= 1:
                    pe.wait_ge(m["xs_scaled"], j)
                for k in range(KT):
                    if k == 0:
                        pe.wait_ge(m["d_copied_a"], j + 1)
                    if k == KT // 2:
                        pe.wait_ge(m["d_copied_v"], j + 1)
                    last = mm(bank(6)[:, 0:D], ds[:, k, :], x2[:, b * KT + k, :], start=(k == 0), stop=(k == KT - 1))
                last.then_inc(m["xs_filled"], 1)

            def xs_T(j):
                pe.wait_ge(m["xs_norm"], j + 1)
                if j >= 1:
                    pe.wait_ge(m["xsT_ready"], j)
                d = bank(7)
                nc.tensor.transpose(d[0:DH, 0:P], xs[:, j % 2, 0:DH], ident[:])
                nc.tensor.transpose(d[0:DH, P:2 * P], xs[:, j % 2, DH:D], ident[:]).then_inc(m["xsT_filled"], 1)

            for b in range(NB):
                if b:
                    pe.wait_ge(m["xsT_ready"], b * ST)
                    pe.wait_ge(m["xs_scaled"], b * ST)
                for s in range(KT + 1):
                    if s < KT:
                        x2_T(b * KT + s)
                    if s >= 1:
                        logits(b * KT + s - 1)
                pe.wait_ge(m["c_exp"], (b + 1) * KT)
                pe.wait_ge(m["lmax_ready"], (b + 1) * KT)
                for s in range(ST + 2):
                    j = b * ST + s
                    if 1 <= s < ST + 1:
                        dispatch_T(j - 1)
                    if s < ST:
                        logits_T(j)
                    if 1 <= s < ST + 1:
                        dispatch(j - 1)
                    if s >= 2:
                        xs_T(j - 2)
            meet(pe, 3)

            def hidden(g):
                r = g % RING
                pe.wait_ge(w_loaded[r], 16 * (3 + GE) * (g // RING + 1))
                if g >= 1:
                    pe.wait_ge(m["hid_gelu"], g)
                for half in range(2):
                    n = DH + half
                    for j in range(GE):
                        last = mm(bank(0)[32 * j:32 * j + 32, 0:HID],
                                  xsT[0:n, half, GE * g + j, :, :].rearrange("d b s -> d (b s)"),
                                  w1r[r][0:n, j, half, :], start=(half == 0), stop=(half == 1),
                                  tile_position=(0, 32 * j))
                last.then_inc(m["hid_filled"], 1)

            def hidden_T(g):
                pe.wait_ge(m["hid_gelu"], g + 1)
                if g >= 1:
                    pe.wait_ge(m["hT_ready"], g)
                for c in range(HC):
                    last = nc.tensor.transpose(bank(1)[:, c * P:(c + 1) * P], hs[:, g % 2, c * P:(c + 1) * P], ident[:])
                last.then_inc(m["hT_filled"], 1)

            def expert_out(g):
                r = g % RING
                pe.wait_ge(m["hT_ready"], g + 1)
                if g >= 1:
                    pe.wait_ge(m["y_ready"], g)
                for c in range(HC):
                    for j in range(GE):
                        last = mm(bank(2)[32 * j:32 * j + 32, 0:D], hT[:, g % 2, c, 32 * j:32 * j + 32],
                                  w2r[r][:, j, c, :], start=(c == 0), stop=(c == HC - 1), tile_position=(0, 32 * j))
                last.then_inc(m["y_filled"], 1)

            def combine_T(u):
                t, b = divmod(u, NB)
                if u >= 1:
                    pe.wait_ge(m["cT_copied"], u)
                for k in range(KT):
                    last = nc.tensor.transpose(bank(3 + k // 4)[:, (k % 4) * P:(k % 4 + 1) * P],
                                               ec[:, b * KT + k, t * P:(t + 1) * P], ident[:])
                last.then_inc(m["cT_filled"], 1)

            def combine(u):
                t, b = divmod(u, NB)
                pe.wait_ge(m["cT_copied"], u + 1)
                pe.wait_ge(ys_loaded[t % 2], 16 * 2 * NB * (t // 2 + 1))
                for k in range(KT):
                    q = u * KT + k
                    if q >= 3:
                        pe.wait_ge(m["yp_taken"], q - 2)
                    mm(bank(5 + q % 3)[:, 0:D], ct[:, u % 2, k, :], ys[:, t % 2, b, :], start=True,
                       stop=True).then_inc(m["yp_filled"], 1)

            LAG = 4
            for s in range(NG + LAG + 1):
                if s < NG:
                    hidden(s)
                if LAG <= s < NG + LAG:
                    combine(s - LAG)
                if s < NG:
                    hidden_T(s)
                if LAG - 1 <= s < NG + LAG - 1:
                    combine_T(s - LAG + 1)
                if s < NG:
                    expert_out(s)

        @block.scalar
        def _(act):
            sc = nc.scalar
            ac = [0]

            def link(ins):
                ac[0] += 1
                ins.then_inc(m["a_chain"], 1)
                act.wait_ge(m["a_chain"], ac[0])

            for s in range(NT + 4):
                if 2 <= s < NT + 2:
                    i = s - 2
                    b, k = divmod(i, KT)
                    lo = (b * SLOTS + 2 * k + 1) * Q
                    act.wait_ge(m["xT_filled"], i + 1)
                    sc.copy(XH[:, :, lo:lo + P], bank(i % 2)[:, 0:2 * P].rearrange("p (h c) -> p h c", h=2)
                            ).then_inc(m["xh_copied"], 1)
                if 3 <= s < NT + 3:
                    i = s - 3
                    act.wait_ge(m["q_filled"], i + 1)
                    if i >= 2:
                        act.wait_ge(m["q_normed"], i - 1)
                    sc.activation(sq[:, i % 2, :], bank(2 + i % 2), ACT.Square).then_inc(m["q_squared"], 1)
            for s in range(NT + 3):
                if 1 <= s < NT + 1:
                    i = s - 1
                    act.wait_ge(m["h_rstd"], i + 1)
                    if i >= 3:
                        act.wait_ge(m["x1T_filled"], i - 2)
                    d = bank(i % 3)
                    sc.activation(x1t[:, i % 3, 0:D], d[:, 0:D], ACT.Identity, bias=nmr[:, i:i + 1], scale=rstd[:, i:i + 1])
                    sc.activation(x1t[:, i % 3, D:D + DB], d[:, P:D], ACT.Identity, bias=nmr[:, i:i + 1],
                                  scale=rstd[:, i:i + 1]).then_inc(m["x1_ready"], 1)
                if 2 <= s < NT + 2:
                    i = s - 2
                    act.wait_ge(m["x1T_filled"], i + 1)
                    sc.copy(X1H[:, :, i * P:(i + 1) * P], bank(3 + i % 2)[:, 0:2 * P].rearrange("p (h c) -> p h c", h=2)
                            ).then_inc(m["x1h_ready"], 1)
                if s >= 3:
                    i = s - 3
                    act.wait_ge(m["pr_filled"], i + 1)
                    sc.copy(pr[:, i, :], bank(5 + i % 2)[:, 0:W2N]).then_inc(m["pr_taken"], 1)
            meet(act, 1)
            logit = pr[:, :, D:D + G]
            sc.activation(logit, logit, ACT.Gelu).then_inc(m["g_gelu"], 1)
            for j in range(2 * (NT * P // 512)):
                blk, c0 = divmod(j, 2)
                act.wait_ge(m["qp_filled"], j + 1)
                sc.copy((qB if c0 else qAh)[:, blk * 512:(blk + 1) * 512], bank(j % 3)).then_inc(m["qph_taken"], 1)
                if j == 1:
                    act.wait_ge(m["g_shifted"], 1)
                    sc.activation(logit, logit, ACT.Exp).then_inc(m["g_exp"], 1)
                    sc.activation(aw[:, 1:2], aw[:, 0:1], ACT.Exp, scale=-1.0).then_inc(m["alpha_exp"], 1)
            for j in range(4):
                half, p8 = divmod(j, 2)
                act.wait_ge(m["ph_filled"], j + 1)
                sc.copy(phT[:, half, :].rearrange("d (n p) -> d p n", p=NP)[:, 8 * p8:8 * p8 + 8, :],
                        bank(3 + j % 2).rearrange("d (p n) -> d p n", n=NE)).then_inc(m["ph_copied"], 1)
            act.wait_ge(m["ph_copied"], 4)
            sc.activation(zz[:], phT[:], ACT.Square).then_inc(m["ph_squared"], 1)
            for j in range(NT // 4):
                act.wait_ge(m["gwT_filled"], j + 1)
                c = slice(j * 512, (j + 1) * 512)
                sc.copy(gP[0:DB, c], bank(6 + j % 2)[0:DB, :])
                sc.copy(gD[:, c], bank(6 + j % 2)).then_inc(m["gwT_hi"], 1)
            act.wait_ge(m["ph_scaled"], 1)
            sc.copy(phAh[:], phT[:, 0, :])
            sc.copy(phB[:], phT[:, 1, :]).then_inc(m["ph_hi"], 1)

            def group_weights(i):
                act.wait_ge(m["gw_filled"], i + 1)
                if i >= 1:
                    act.wait_ge(m["z_ready"], i)
                sc.copy(gws[:], bank(2, 2)).then_inc(m["gw_copied"], 1)

            def exps(i):
                act.wait_ge(m["norm_ready"], i + 1)
                sc.activation(zz[:, i % 2, :], zz[:, i % 2, :], ACT.Exp, bias=nmx[:, i:i + 1],
                              accum_out=rsum[:, i:i + 1]).then_inc(m["e_ready"], 1)

            def turn(i):
                act.wait_ge(m["et_filled"], 2 * i + 1)
                if i >= 1:
                    act.wait_ge(m["o_filled"], i)
                sc.copy(et[:, 0:KT // 2, :].rearrange("p k c -> p (k c)"), bank(4)).then_inc(m["et_copied_a"], 1)

            for s in range(NT + 1):
                if s >= 1:
                    exps(s - 1)
                    turn(s - 1)
                if s < NT:
                    group_weights(s)
            meet(act, 2)

            def x2_tile(i):
                act.wait_ge(m["f_rstd"], i + 1)
                if i >= 2:
                    act.wait_ge(m["x2T_filled"], i - 1)
                sc.activation(x2[:, i, :], res[:, i, :], ACT.Identity, bias=nmr[:, i:i + 1], scale=rstd[:, i:i + 1])
                sc.activation(x2t[:, i % 2, 0:D], res[:, i, :], ACT.Identity, bias=nmr[:, i:i + 1], scale=rstd[:, i:i + 1])
                sc.activation(x2t[:, i % 2, D:D + DB], res[:, i, P:D], ACT.Identity, bias=nmr[:, i:i + 1],
                              scale=rstd[:, i:i + 1]).then_inc(m["x2t_ready"], 1)

            def x2_hi(i):
                act.wait_ge(m["x2T_filled"], i + 1)
                if i >= 2:
                    act.wait_ge(m["l_filled"], i - 1)
                sc.copy(X2H[:, i % 2, :, :], bank(6 + i % 2)[:, 0:2 * P].rearrange("p (h c) -> p h c", h=2)
                        ).then_inc(m["x2h_ready"], 1)

            def c_exps(i):
                act.wait_ge(m["lmax_ready"], i + 1)
                sc.activation(ec[:, i, :], bank(2 * (i % 2), 2), ACT.Exp, bias=nmC[:, i:i + 1],
                              accum_out=rsC[:, i:i + 1]).then_inc(m["c_exp"], 1)

            for b in range(NB):
                for s in range(KT + 2):
                    if s < KT:
                        x2_tile(b * KT + s)
                    if 1 <= s < KT + 1:
                        x2_hi(b * KT + s - 1)
                    if s >= 2:
                        c_exps(b * KT + s - 2)
                for s in range(ST + 2):
                    j = b * ST + s
                    if s < ST:
                        act.wait_ge(m["dmax_ready"], j + 1)
                        if s >= 1:
                            act.wait_ge(m["d_filled"], 2 * j)
                        sc.activation(dt_[:], bank(2 * (s % 2), 2), ACT.Exp, bias=nmD[:, j:j + 1],
                                      accum_out=csD[:, j:j + 1]).then_inc(m["d_exp"], 1)
                        act.wait_ge(m["d_filled"], 2 * j + 1)
                        if j >= 1:
                            act.wait_ge(m["xs_filled"], j)
                        sc.copy(ds[:, 0:KT // 2, :].rearrange("p k c -> p (k c)"), bank(4)).then_inc(m["d_copied_a"], 1)
                    if 1 <= s < ST + 1:
                        q = j - 1
                        act.wait_ge(m["xs_filled"], q + 1)
                        act.wait_ge(m["xs_sum"], q + 1)
                        if q >= 2:
                            act.wait_ge(m["xsT_filled"], q - 1)
                        sc.activation(xs[:, q % 2, :], bank(6)[:, 0:D], ACT.Copy, scale=ciD[:, q:q + 1]
                                      ).then_inc(m["xs_scaled"], 1)
            meet(act, 3)

            def gelus(g):
                act.wait_ge(m["hid_filled"], g + 1)
                if g >= 2:
                    act.wait_ge(m["hT_filled"], g - 1)
                sc.activation(hs[:, g % 2, :], bank(0)[:, 0:HID], ACT.Gelu).then_inc(m["hid_gelu"], 1)

            def c_turn(u):
                act.wait_ge(m["cT_filled"], u + 1)
                if u >= 2:
                    act.wait_ge(m["yp_filled"], KT * (u - 1))
                sc.copy(ct[:, u % 2].rearrange("p k c -> p (k c)"), bank(3, 2)).then_inc(m["cT_copied"], 1)

            LAG = 4
            for s in range(NG + LAG):
                if s < NG:
                    gelus(s)
                if LAG - 1 <= s < NG + LAG - 1:
                    c_turn(s - LAG + 1)

        @block.vector
        def _(dve):
            v = nc.vector
            vc = [0]

            def link(ins):
                vc[0] += 1
                ins.then_inc(m["v_chain"], 1)
                dve.wait_ge(m["v_chain"], vc[0])

            def bc(ap, shape):
                return ap.broadcast_to(shape)

            dve.wait_ge(m["in_ids"], 64)
            v.tensor_copy(idsf[:], ids[:]).then_inc(m["idsf_ready"], 1)
            dve.wait_ge(m["ids_permuted"], 1)
            v.tensor_copy(idx[:], bank(5)[:, 0:NB * (KT + 1)]).then_inc(m["idx_ready"], 1)
            dve.wait_ge(m["in_tok"], 16 * 5)
            link(v.tensor_copy(linkf[:], links[:]))
            link(v.tensor_tensor(eq[:], bc(idsf[:, 1:C + 1].unsqueeze(2), [P, C, NL]),
                                 bc(linkf[:].unsqueeze(1), [P, C, NL]), ALU.is_equal))
            link(v.tensor_reduce(maskP[:], eq[:], AX, ALU.max))
            v.tensor_tensor(maskP[:], maskP[:], valid[:], ALU.mult).then_inc(m["maskp_ready"], 1)
            dve.wait_ge(m["mask_permuted"], 1)
            v.tensor_copy(mask[:], bank(4)[:, 0:NT]).then_inc(m["mask_ready"], 1)
            dve.wait_ge(m["mask_ready"], 1)
            v.tensor_reduce(msum[:], mask[:], AX, ALU.add).then_inc(m["msum_ready"], 1)
            dve.wait_ge(m["count_ready"], 1)
            link(v.tensor_scalar(cnt[:, 0:1], bank(3)[:, 0:1], float(HEADS), 1.0, ALU.mult, ALU.max))
            link(v.reciprocal(cnt[:, 1:2], cnt[:, 0:1]))
            v.tensor_scalar(cnt[:, 2:3], cnt[:, 1:2], -TRACE_DECAY * ERASE_LR, None, ALU.mult)
            v.tensor_scalar(cnt[:, 3:4], cnt[:, 1:2], TRACE_LR, None, ALU.mult).then_inc(m["cnt_ready"], 1)

            v.tensor_tensor(wpt[:, :, 0:D], wp[:], bc(gam[:].unsqueeze(1), [P, HP, D]), ALU.mult)
            v.tensor_tensor(wpt[:, :, D:D + DB], wp[:, :, P:D], bc(gam[:, P:D].unsqueeze(1), [P, HP, DB]), ALU.mult)
            link(v.tensor_tensor(wpt[:, :, CB2:CB2 + DB], wp[:, :, P:D], bc(gam[:, P:D].unsqueeze(1), [P, HP, DB]), ALU.mult))
            link(v.tensor_tensor(wp[:], wp[:], bc(bet[:].unsqueeze(1), [P, HP, D]), ALU.mult))
            v.tensor_reduce(wpt[:, :, CB2 + DB:CB2 + DB + 1], wp[:].unsqueeze(2), AX, ALU.add)
            v.tensor_reduce(wpt[:, :, CB2 + DB + 1:PC], wp[:].unsqueeze(2), AX, ALU.add).then_inc(m["wpt_ready"], 1)

            def take(name):
                dve.wait_ge(m["setup_filled"], at[name] + 1)
                return setup_bank(name)

            def taken(ins):
                ins.then_inc(m["setup_taken"], 1)

            def f(ap):
                return ap.bitcast(F32)

            def form_p(pre, Ah, Al, B1, B2, n, copies=(None, None)):
                d = take(pre + "A")
                link(v.tensor_copy(Ah[:], d[:, 0:n]))
                if copies[0] is not None:
                    v.tensor_copy(copies[0], d[:, 0:n])
                taken(v.tensor_tensor(Al[:], d[:, 0:n], f(Ah[:]), ALU.subtract))
                d = take(pre + "B1")
                link(v.tensor_copy(B1[:], d[:, 0:n]))
                taken(v.tensor_tensor(B1[DB:P, :], d[DB:P, 0:n], f(B1[DB:P, :]), ALU.subtract))
                d = take(pre + "B2")
                link(v.tensor_copy(B2[:], d[0:DB + 2, 0:n]))
                if copies[1] is not None:
                    v.tensor_copy(copies[1], d[0:DB + 1, 0:n])
                link(v.tensor_tensor(B2[DB:DB + 2, :], d[DB:DB + 2, 0:n], f(B2[DB:DB + 2, :]), ALU.subtract))
                taken(v.tensor_copy(B2[DB:DB + 1, :], d[DB:DB + 1, 0:n]))

            form_p("wp", wpAh, wpAl, wpB1, wpB2, HD, (wpT[:, 0, :], wpT[0:DB + 1, 1, :]))
            dve.wait_ge(m["in_attn"], 16 * 10)
            for y, (name, w) in enumerate((("wqT", wTq), ("wkT", wTk), ("wvT3", wTv))):
                d = take(name)
                scale = SCALE if y == 0 else 1.0
                for c, n in enumerate((P, DB)):
                    v.tensor_scalar(w[0:n, c, 0:D], d[0:n, c * D:(c + 1) * D], scale, None, ALU.mult)
                    last = v.tensor_scalar(w[0:n, c, D:D + DB], d[0:n, c * D + P:(c + 1) * D], scale, None, ALU.mult)
                    if y != 1:
                        v.tensor_scalar(w[0:n, c, CB2:CB2 + DB], d[0:n, c * D + P:(c + 1) * D], scale, None, ALU.mult)
                        last = v.tensor_scalar(w[0:n, c, CB2 + DB:PC], bc(bcol[0:n, c, y:y + 1], [n, 2]), scale, None, ALU.mult)
                taken(last)
            form_p("k", kAh, kAl, kB1, kB2, P + 2 * DB)
            form_p("v", vAh, vAl, vB1, vB2, W2N)
            taken(v.tensor_copy(wvT[:, 0, :], take("wvA")))
            taken(v.tensor_copy(wvT[0:DB, 1, :], take("wvB")[0:DB, :]))
            taken(v.tensor_copy(woT[:, :, 0:P], take("woA").rearrange("p (t c) -> p t c", t=HP)))
            taken(v.tensor_copy(woT[:, :, P:D], take("woB")[:, 0:HP * DB].rearrange("p (t c) -> p t c", t=HP)))
            for r in range(2):
                rows = slice(r * DT, (r + 1) * DT)
                v.tensor_scalar(eyeP[rows, :], ident[rows, rows], TRACE_DECAY, None, ALU.mult)

            def stats(i):
                t = (i // KT) * (KT + 1) + i % KT
                dve.wait_ge(gathered[t], 16)
                link(v.bn_stats(st6[:, i, :], tok[:, t, :]))
                v.bn_aggr(mv[:, i, :], st6[:, i, :]).then_inc(m["front_stats"], 1)

            def normalise(i):
                t = (i // KT) * (KT + 1) + i % KT
                dve.wait_ge(m["front_rstd"], i + 1)
                if i >= 3:
                    dve.wait_ge(m["cprime_done"], i - 2)
                mean = mv[:, i, 0:1]
                v.tensor_scalar(xh[:, i % 3, 0:D], tok[:, t, :], mean, rstd[:, i:i + 1], ALU.subtract, ALU.mult)
                v.tensor_scalar(xh[:, i % 3, D:D + DB], tok[:, t, P:D], mean, rstd[:, i:i + 1], ALU.subtract, ALU.mult)
                v.tensor_scalar(xm[:, i % 3, 0:D], tok[:, t, :], mean, rm[:, i:i + 1], ALU.subtract, ALU.mult)
                v.tensor_copy(xm[:, i % 3, D:D + 1], mask[:, i:i + 1]).then_inc(m["xh_ready"], 1)

            def lo_parts(i):
                b, k = divmod(i, KT)
                lo = (b * SLOTS + 2 * k + 1) * Q
                dve.wait_ge(m["xh_copied"], i + 1)
                d = bank(i % 2)
                v.tensor_tensor(XL[:, 0, lo:lo + P], d[:, 0:P], f(XH[:, 0, lo:lo + P]), ALU.subtract)
                ins = v.tensor_tensor(XL[0:DB, 1, lo:lo + P], d[0:DB, P:2 * P], f(XH[0:DB, 1, lo:lo + P]), ALU.subtract)
                ins.then_inc(m["xl_ready"], 1)
                if k == KT - 1:
                    dve.wait_ge(m["xl_ready"], i + 1)
                    z, e = b * SLOTS * Q, (b * SLOTS + SLOTS - 1) * Q
                    v.tensor_copy(XH[:, :, z + 1:z + Q], f(XH[:, :, e:e + Q - 1]))
                    v.tensor_copy(XL[:, :, z + 1:z + Q], f(XL[:, :, e:e + Q - 1]))
                    v.memset(f(XH[:, :, z:z + 1]), 0.0)
                    v.memset(f(XL[:, :, z:z + 1]), 0.0).then_inc(m["wn_ready"], 1)

            def norms(i):
                dve.wait_ge(m["q_squared"], i + 1)
                v.tensor_reduce(ss[:, i, :], sq[:, i % 2, :].rearrange("p (h c) -> p h c", h=HEADS), AX,
                                ALU.add).then_inc(m["q_normed"], 1)

            def erase_q(i):
                dve.wait_ge(m["q_fac"], i + 1)
                if i >= 2:
                    dve.wait_ge(m["gram_done"], i - 1)
                v.tensor_tensor(qe[:, i % 2, :].rearrange("p (h c) -> p h c", h=HEADS),
                                bank(2 + i % 2).rearrange("p (h c) -> p h c", h=HEADS),
                                bc(fac[:, i, :].unsqueeze(2), [P, HEADS, DT]), ALU.mult).then_inc(m["qe_ready"], 1)

            dve.wait_ge(m["mask_ready"], 1)
            dve.wait_ge(m["xl_ones"], 1)
            for s in range(NT + 5):
                if 2 <= s < NT + 2:
                    lo_parts(s - 2)
                if 3 <= s < NT + 3:
                    norms(s - 3)
                if 4 <= s < NT + 4:
                    erase_q(s - 4)
                if s < NT:
                    stats(s)
                if 1 <= s < NT + 1:
                    normalise(s - 1)

            dve.wait_ge(m["cprime_done"], NT)
            v.tensor_copy(cc[:, 0, :], bank(5)[:, 0:D])
            v.tensor_copy(cc[0:DB + 1, 1, :], bank(5)[0:DB + 1, 256:256 + D]).then_inc(m["cc_ready"], 1)
            dve.wait_ge(m["gram_done"], NT)
            dve.wait_ge(m["cnt_ready"], 1)
            v.scalar_tensor_tensor(r1[:], bank(4)[:, 0:HP * DT].rearrange("p (t c) -> p t c", t=HP), cnt[:, 2:3],
                                   bc(eyeP[:].unsqueeze(1), [P, HP, DT]), ALU.mult, ALU.add)
            taken(v.tensor_scalar(bs[:, 0, :], take("bpA"), cnt[:, 3:4], None, ALU.mult))
            taken(v.tensor_scalar(bs[0:DB, 1, :], take("bpB")[0:DB, :], cnt[0:DB, 3:4], None, ALU.mult))
            dve.wait_ge(m["traces_part"], 2 * HEADS)
            v.tensor_copy(tt[:], bank(2)[:, 0:HP * DT].rearrange("p (t c) -> p t c", t=HP)).then_inc(m["tt_ready"], 1)
            dve.wait_ge(m["mix_done"], 1)
            for t in range(HP):
                last = v.tensor_copy(mm_[:, t, :], bank(t // 2)[:, (t % 2) * 256:(t % 2) * 256 + D])
            last.then_inc(m["mm_ready"], 1)
            form_p("n", nAh, nAl, nB1, nB2, D)

            dve.wait_ge(m["xl_ones"], 2)
            for s in range(NT + 2):
                if s >= 2:
                    i = s - 2
                    c = slice(i * P, (i + 1) * P)
                    dve.wait_ge(m["x1h_ready"], i + 1)
                    d = bank(3 + i % 2)
                    v.tensor_tensor(X1L[:, 0, c], d[:, 0:P], f(X1H[:, 0, c]), ALU.subtract)
                    v.tensor_tensor(X1L[0:DB, 1, c], d[0:DB, P:2 * P], f(X1H[0:DB, 1, c]), ALU.subtract
                                    ).then_inc(m["x1l_ready"], 1)
                if s < NT:
                    i = s
                    dve.wait_ge(m["h_filled"], i + 1)
                    link(v.bn_stats(st6[:, i, :], bank(i % 3)[:, 0:D]))
                    v.tensor_tensor(res[:, i, :], bank(i % 3)[:, 0:D], bproj[:], ALU.add).then_inc(m["h_taken"], 1)
                    v.bn_aggr(mv[:, i, :], st6[:, i, :]).then_inc(m["h_stats"], 1)
            meet(dve, 1)
            logit = pr[:, :, D:D + G]
            dve.wait_ge(m["g_gelu"], 1)
            link(v.tensor_reduce(gm[:], logit, AX, ALU.max))
            v.tensor_tensor(logit, logit, bc(gm[:].unsqueeze(2), [P, NT, G]), ALU.subtract).then_inc(m["g_shifted"], 1)
            def q_lo(j):
                blk, c0 = divmod(j, 2)
                n = slice(blk * 512, (blk + 1) * 512)
                dve.wait_ge(m["qph_taken"], j + 1)
                if c0:
                    v.tensor_tensor(qB[DB:P, n], bank(j % 3)[DB:P, :], f(qB[DB:P, n]), ALU.subtract).then_inc(m["qpl_taken"], 1)
                else:
                    v.tensor_tensor(qAl[:, n], bank(j % 3), f(qAh[:, n]), ALU.subtract).then_inc(m["qpl_taken"], 1)

            for j in range(2):
                q_lo(j)
            dve.wait_ge(m["g_exp"], 1)
            link(v.tensor_reduce(gs[:], logit, AX, ALU.add))
            link(v.reciprocal(gs[:], gs[:]))
            dve.wait_ge(m["half_ready"], 1)
            v.tensor_tensor(gw[:, :, 0:G], logit, bc(gs[:].unsqueeze(2), [P, NT, G]), ALU.mult)
            v.tensor_tensor(gw[:, :, DB:DB + G], logit, bc(gs[:].unsqueeze(2), [P, NT, G]), ALU.mult).then_inc(m["gw_ready"], 1)
            dve.wait_ge(m["alpha_exp"], 1)
            link(v.tensor_scalar(aw[:, 2:3], aw[:, 1:2], 1.0, None, ALU.add))
            link(v.reciprocal(aw[:, 2:3], aw[:, 2:3]))
            link(v.tensor_tensor(aw[:, 3:4], aw[:, 1:2], aw[:, 2:3], ALU.mult))
            for j in range(2, 2 * (NT * P // 512)):
                q_lo(j)
            dve.wait_ge(m["ln_filled"], 1)
            v.tensor_copy(lnT[:], bank(5)[0:DH, 0:4 * NE].rearrange("d (w e) -> d w e", w=4)).then_inc(m["ln_taken"], 1)
            dve.wait_ge(m["ph_squared"], 1)
            v.tensor_reduce(pss[:], zz[:].rearrange("d c (n p) -> d c p n", p=NP), AX, ALU.add).then_inc(m["ph_summed"], 1)
            for j in range(NT // 4):
                c = slice(j * 512, (j + 1) * 512)
                d = bank(6 + j % 2)
                dve.wait_ge(m["gwT_hi"], j + 1)
                v.tensor_tensor(gL[:, c], d, f(gD[:, c]), ALU.subtract)
                v.tensor_tensor(gP[DB:P, c], d[DB:P, :], f(gD[DB:P, c]), ALU.subtract).then_inc(m["gwT_taken"], 1)
            for b in range(NB):
                d = bank(b)[:, 0:D]
                dve.wait_ge(m["u_filled"], b + 1)
                link(v.tensor_scalar(uP[:, b, :], d, aw[:, 2:3], None, ALU.mult))
                v.scalar_tensor_tensor(uP[DB:P, b, :], d[DB:P, :], aw[DB:P, 2:3], f(uP[DB:P, b, :]), ALU.mult,
                                       ALU.subtract).then_inc(m["u_taken"], 1)
            dve.wait_ge(m["ph_rsqrt"], 1)
            for half in range(2):
                w = phT[:, half, :].rearrange("d (n p) -> d n p", p=NP)
                last = v.tensor_tensor(w, w, bc(prs[:, half, :].unsqueeze(1), [P, NE, NP]), ALU.mult)
            last.then_inc(m["ph_scaled"], 1)
            dve.wait_ge(m["ph_hi"], 1)
            v.tensor_tensor(phAl[:], phT[:, 0, :], f(phAh[:]), ALU.subtract)
            v.tensor_tensor(phB[DB:P, :], phT[DB:P, 1, :], f(phB[DB:P, :]), ALU.subtract)

            def z_tile(i):
                dve.wait_ge(m["gw_copied"], i + 1)
                dve.wait_ge(m["s_filled"], i + 1)
                if i >= 2:
                    dve.wait_ge(m["et_filled"], 2 * (i - 1))
                v.scalar_tensor_tensor(zz[:, i % 2, :], bank(0, 2), pr[:, i, W2N - 1:W2N], gws[:], ALU.add,
                                       ALU.mult).then_inc(m["z_ready"], 1)
                dve.wait_ge(m["z_ready"], i + 1)
                v.tensor_reduce(nmx[:, i:i + 1], zz[:, i % 2, :], AX, ALU.max, negate=True).then_inc(m["norm_ready"], 1)

            def turn(i):
                dve.wait_ge(m["et_filled"], 2 * i + 2)
                if i >= 1:
                    dve.wait_ge(m["o_filled"], i)
                v.tensor_copy(et[:, KT // 2:KT, :].rearrange("p k c -> p (k c)"), bank(5)).then_inc(m["et_copied_v"], 1)

            def weight(i):
                dve.wait_ge(m["e_ready"], i + 1)
                link(v.reciprocal(rinv[:, i:i + 1], rsum[:, i:i + 1]))
                link(v.tensor_scalar(cn[:, i:i + 1], rinv[:, i:i + 1], aw[:, 3:4], None, ALU.mult))

            def finish(i):
                d = bank(6 + i % 2)
                dve.wait_ge(m["o_filled"], i + 1)
                link(v.tensor_tensor(res[:, i, :], d[:, 256:256 + D], res[:, i, :], ALU.add))
                v.scalar_tensor_tensor(res[:, i, :], d[:, 0:D], cn[:, i:i + 1], res[:, i, :], ALU.mult,
                                       ALU.add).then_inc(m["o_taken"], 1)

            for s in range(NT + 1):
                if s >= 1:
                    weight(s - 1)
                    turn(s - 1)
                if s < NT:
                    z_tile(s)
                if s >= 1:
                    finish(s - 1)
            meet(dve, 2)

            v.memset(f(X2L[DB:P, :, 1, :]), 1.0)

            def f_stats(i):
                link(v.bn_stats(st6[:, i, :], res[:, i, :]))
                v.bn_aggr(mv[:, i, :], st6[:, i, :]).then_inc(m["f_stats"], 1)

            def x2_lo(i):
                dve.wait_ge(m["x2h_ready"], i + 1)
                d = bank(6 + i % 2)
                if i >= 2:
                    dve.wait_ge(m["l_filled"], i - 1)
                v.tensor_tensor(X2L[:, i % 2, 0, :], d[:, 0:P], f(X2H[:, i % 2, 0, :]), ALU.subtract)
                v.tensor_tensor(X2L[0:DB, i % 2, 1, :], d[0:DB, P:2 * P], f(X2H[0:DB, i % 2, 1, :]), ALU.subtract
                                ).then_inc(m["x2l_ready"], 1)

            def l_tile(i):
                b, k = divmod(i, KT)
                dve.wait_ge(m["l_filled"], i + 1)
                if b and k == 0:
                    dve.wait_ge(m["dT_filled"], ST * b)
                d = bank(2 * (i % 2), 2)
                link(v.tensor_reduce(nmC[:, i:i + 1], d, AX, ALU.max, negate=True))
                v.tensor_copy(ls[:, k, :], d).then_inc(m["lmax_ready"], 1)

            for b in range(NB):
                for s in range(KT + 2):
                    if s < KT:
                        if b:
                            dve.wait_ge(m["xs_norm"], ST)
                        f_stats(b * KT + s)
                    if 1 <= s < KT + 1:
                        x2_lo(b * KT + s - 1)
                    if s >= 2:
                        l_tile(b * KT + s - 2)
                for s in range(ST + 2):
                    j = b * ST + s
                    if s < ST:
                        dve.wait_ge(m["dT_filled"], j + 1)
                        v.tensor_reduce(nmD[:, j:j + 1], bank(2 * (s % 2), 2), AX, ALU.max, negate=True
                                        ).then_inc(m["dmax_ready"], 1)
                        dve.wait_ge(m["d_filled"], 2 * j + 2)
                        if j >= 1:
                            dve.wait_ge(m["xs_filled"], j)
                        v.tensor_copy(ds[:, KT // 2:KT, :].rearrange("p k c -> p (k c)"), bank(5)).then_inc(m["d_copied_v"], 1)
                    if 1 <= s < ST + 1:
                        q = j - 1
                        dve.wait_ge(m["d_exp"], q + 1)
                        v.reciprocal(ciD[:, q:q + 1], csD[:, q:q + 1]).then_inc(m["xs_sum"], 1)
                        dve.wait_ge(m["xs_scaled"], q + 1)
                        link(v.bn_stats(st6[:, q, :], xs[:, q % 2, :]))
                        v.bn_aggr(mv[:, q, :], st6[:, q, :]).then_inc(m["xs_stats"], 1)
                        dve.wait_ge(m["xs_rstd"], q + 1)
                        v.tensor_scalar(xs[:, q % 2, :], xs[:, q % 2, :], rstd[:, q:q + 1], nmr[:, q:q + 1], ALU.mult,
                                        ALU.add).then_inc(m["xs_norm"], 1)
                    if s >= 2:
                        q = j - 2
                        bq_, t = divmod(q, ST)
                        dve.wait_ge(m["xsT_filled"], q + 1)
                        for half in range(2):
                            e = slice(EPT * t, EPT * (t + 1))
                            dst = xsT[0:DH, half, e, bq_, :]
                            src = bank(7)[0:DH, half * P:(half + 1) * P].rearrange("d (e s) -> d e s", s=NP)
                            link(v.tensor_tensor(dst, src, bc(lnT[:, half, e].unsqueeze(2), [DH, EPT, NP]), ALU.mult))
                            last = v.tensor_tensor(dst, dst, bc(lnT[:, 2 + half, e].unsqueeze(2), [DH, EPT, NP]), ALU.add)
                        last.then_inc(m["xsT_ready"], 1)
            v.reciprocal(riC[:], rsC[:])
            meet(dve, 3)

            def h_turn(g):
                dve.wait_ge(m["hT_filled"], g + 1)
                if g >= 2:
                    dve.wait_ge(m["y_filled"], g - 1)
                v.tensor_copy(hT[:, g % 2].rearrange("p c r -> p (c r)"), bank(1)[:, 0:HC * P]).then_inc(m["hT_ready"], 1)

            def y_bias(g):
                dve.wait_ge(m["y_filled"], g + 1)
                if g >= 2:
                    dve.wait_ge(ys_stored[g % 2], 16 * (g // 2))
                v.tensor_tensor(ysb[:, g % 2, :], bank(2)[:, 0:D], b2r[g % RING][:], ALU.add).then_inc(m["y_ready"], 1)

            def add_up(u):
                t, b = divmod(u, NB)
                for k in range(KT):
                    q, i = u * KT + k, b * KT + k
                    dve.wait_ge(m["yp_filled"], q + 1)
                    if t:
                        dve.wait_ge(m["yp_taken"], NT * (t - 1) + i + 1)
                    v.scalar_tensor_tensor(res[:, i, :], bank(5 + q % 3)[:, 0:D], riC[:, i:i + 1], res[:, i, :],
                                           ALU.mult, ALU.add).then_inc(m["yp_taken"], 1)

            LAG = 4
            for s in range(NG + LAG + 1):
                if LAG <= s < NG + LAG:
                    add_up(s - LAG)
                if s < NG:
                    h_turn(s)
                    dve.wait_ge(w_loaded[s % RING], 16 * (3 + GE) * (s // RING + 1))
                    y_bias(s)


INPUTS = ["x", "L0_tok_link_ids", "L0_tok_wte", "L0_tok_gamma", "L0_tok_beta", "L0_tok_W_proj", "L0_tok_W_val",
          "L0_tok_W_out", "L0_tok_value_traces", "L0_attn_W_qkv", "L0_attn_b_qkv", "L0_attn_W_proj",
          "L0_attn_b_proj", "L0_attn_W_gp", "L0_attn_alpha", "L0_ffn_phi", "L0_ffn_ln_g", "L0_ffn_ln_b",
          "L0_ffn_w1", "L0_ffn_b1", "L0_ffn_w2", "L0_ffn_b2"]


def kernel(**inputs):
    import numpy as np
    import concourse.bacc as bacc
    from concourse.bass_utils import run_bass_kernel_spmd as run

    nc = bacc.Bacc("TRN2", target_bir_lowering=False, num_devices=1)
    arrays, args = {}, {}
    data = {n: np.ascontiguousarray(inputs[n]) for n in INPUTS}
    data["L0_attn_alpha"] = data["L0_attn_alpha"].reshape(1, 1)
    nb, s = data["x"].shape
    d = data["L0_tok_wte"].shape[1]
    data["c_ident"] = np.eye(P, dtype=np.float32)
    per = nb * s // P
    data["c_valid"] = ((np.arange(nb * s) % s) < s - 2).astype(np.float32).reshape(P, per)
    for n, v in data.items():
        arrays[f"in_{n}"] = v
        args[n] = nc.dram_tensor(f"in_{n}", v.shape, mybir.dt.from_np(v.dtype), kind="ExternalInput").ap()
    out = nc.dram_tensor("out", [nb, s, d], F32, kind="ExternalOutput").ap()
    build(nc, args, out)
    r = run(nc, [arrays], core_ids=[0])
    return r.results[0]["out"]
```

```python
from contextlib import ExitStack

import concourse.bass as bass
from concourse import mybir

F32 = mybir.dt.float32
F32R = mybir.dt.float32r
I32 = mybir.dt.int32
ALU = mybir.AluOpType
ACT = mybir.ActivationFunctionType
AX = mybir.AxisListType.X

P = 128


def build(nc, a, out):
    NB, S = a["x"].shape
    D = a["L0_tok_wte"].shape[1]
    HD = a["L0_tok_W_proj"].shape[0]
    HEADS, DT, _ = a["L0_tok_value_traces"].shape
    G = a["L0_attn_W_gp"].shape[1]
    NE, NP, _ = a["L0_ffn_phi"].shape
    HID = a["L0_ffn_w1"].shape[2]
    NL = a["L0_tok_link_ids"].shape[0]
    DB = D - P
    Q = 64
    KT = S // P
    NT = NB * KT
    C = S // Q
    SLOTS = C + 1
    HP = HD // P
    PC = P + 3 * DB + 2
    CB1, CB2 = P, P + 2 * DB
    W2N = D + G + 1
    NS = NE * NP
    ST = NS // P
    EPT = P // NP
    GE = 4
    NG = NE // GE
    DH = D // 2
    HC = HID // P
    SCALE = float(D) ** -0.5
    TRACE_LR, TRACE_DECAY, ERASE_LR = 0.1, 0.99, 1.0

    ctx = ExitStack()
    early = ExitStack()
    front = ExitStack()
    late = ExitStack()
    moe_in = ExitStack()

    def sb(name, shape, dt=F32, where=None):
        return (where or ctx).enter_context(nc.sbuf_tensor(name, shape, dt))

    def sem(name):
        return ctx.enter_context(nc.semaphore(name))

    with ctx:
        ident = sb("ident", [P, P])
        res = sb("res", [P, NT, D])
        phAh = sb("phAh", [P, NS], F32R)
        phAl = sb("phAl", [P, NS], F32R)
        phB = sb("phB", [P, NS], F32R)
        lnT = sb("lnT", [DH, 4, NE])
        st6 = sb("st6", [P, NT, 6])
        mv = sb("mv", [P, NT, 2])
        ve = sb("ve", [P, NT])
        rstd = sb("rstd", [P, NT])
        nmr = sb("nmr", [P, NT])
        mhalf = sb("mhalf", [P, 32])
        aw = sb("aw", [P, 4])
        X1H = sb("X1H", [P, 2, NT * P], F32R, early)
        X1L = sb("X1L", [P, 2, NT * P], F32R, early)
        pr = sb("pr", [P, NT, W2N], where=early)
        x1t = sb("x1t", [P, 3, P + 2 * DB], where=early)
        wqkA = sb("wqkA", [P, 3 * D], where=early)
        wqkB = sb("wqkB", [DB, 3 * D], where=early)
        bcol = sb("bcol", [P, 2, 3], where=early)
        wpg = sb("wpg", [P, 2, D + G], where=early)
        bproj = sb("bproj", [P, D], where=early)
        wTq = sb("wTq", [P, 2, PC], where=early)
        wTk = sb("wTk", [P, 2, P + 2 * DB], where=early)
        wTv = sb("wTv", [P, 2, PC], where=early)
        kAh = sb("kAh", [P, P + 2 * DB], F32R, early)
        kAl = sb("kAl", [P, P + 2 * DB], F32R, early)
        kB1 = sb("kB1", [P, P + 2 * DB], F32R, early)
        kB2 = sb("kB2", [DB + 2, P + 2 * DB], F32R, early)
        vAh = sb("vAh", [P, W2N], F32R, early)
        vAl = sb("vAl", [P, W2N], F32R, early)
        vB1 = sb("vB1", [P, W2N], F32R, early)
        vB2 = sb("vB2", [DB + 2, W2N], F32R, early)
        ids = sb("ids", [P, C + 2], I32, front)
        idsf = sb("idsf", [P, C + 2], where=front)
        idx = sb("idx", [P, NB * (KT + 1)], I32, front)
        links = sb("links", [P, NL], I32, front)
        linkf = sb("linkf", [P, NL], where=front)
        valid = sb("valid", [P, C], where=front)
        eq = sb("eq", [P, C, NL], where=front)
        maskP = sb("maskP", [P, C], where=front)
        mask = sb("mask", [P, NT], where=front)
        msum = sb("msum", [P, 1], where=front)
        ones = sb("ones", [P, P], where=front)
        cnt = sb("cnt", [P, 4], where=front)
        tok = sb("tok", [P, NB * (KT + 1), D], where=front)
        xh = sb("xh", [P, 3, P + 2 * DB], where=front)
        xm = sb("xm", [P, 3, D + 1], where=front)
        XH = sb("XH", [P, 2, NB * SLOTS * Q], F32R, front)
        XL = sb("XL", [P, 2, NB * SLOTS * Q], F32R, front)
        sq = sb("sq", [P, 2, HD], where=front)
        ss = sb("ss", [P, NT, HEADS], where=front)
        fac = sb("fac", [P, NT, HEADS], where=front)
        qe = sb("qe", [P, 2, HD], where=front)
        gam = sb("gam", [P, D], where=front)
        bet = sb("bet", [P, D], where=front)
        wp = sb("wp", [P, HP, D], where=front)
        wpt = sb("wpt", [P, HP, PC], where=front)
        wv = sb("wv", [P, HP, D], where=front)
        woA = sb("woA", [P, HD], where=front)
        woB = sb("woB", [DB, HD], where=front)
        vt = sb("vt", [P, HP, DT], where=front)
        wpAh = sb("wpAh", [P, HD], F32R, front)
        wpAl = sb("wpAl", [P, HD], F32R, front)
        wpB1 = sb("wpB1", [P, HD], F32R, front)
        wpB2 = sb("wpB2", [DB + 2, HD], F32R, front)
        wpT = sb("wpT", [P, 2, HD], where=front)
        wvT = sb("wvT", [P, 2, HD], where=front)
        woT = sb("woT", [P, HP, D], where=front)
        eyeP = sb("eyeP", [P, DT], where=front)
        cc = sb("cc", [P, 2, D], where=front)
        r1 = sb("r1", [P, HP, DT], where=front)
        bs = sq
        tt = sb("tt", [P, HP, DT], where=front)
        mm_ = qe[:].rearrange("p a b -> p (a b)")[:, 0:HP * D].rearrange("p (t c) -> p t c", t=HP)
        nAh = sb("nAh", [P, D], F32R, front)
        nAl = sb("nAl", [P, D], F32R, front)
        nB1 = sb("nB1", [P, D], F32R, front)
        nB2 = sb("nB2", [DB + 2, D], F32R, front)
        front.close()
        qAh = sb("qAh", [P, NT * P], F32R, late)
        qAl = sb("qAl", [P, NT * P], F32R, late)
        qB = sb("qB", [P, NT * P], F32R, late)
        gw = sb("gw", [P, NT, P], where=late)
        gm = sb("gm", [P, NT], where=late)
        gs = sb("gs", [P, NT], where=late)
        gD = sb("gD", [P, NT * P], F32R, late)
        gL = sb("gL", [P, NT * P], F32R, late)
        gP = sb("gP", [P, NT * P], F32R, late)
        uP = sb("uP", [P, NB, D], F32R, late)
        zz = sb("zz", [P, 2, S], where=late)
        gws = sb("gws", [P, S], where=late)
        et = sb("et", [P, KT, P], where=late)
        nmx = sb("nmx", [P, NT], where=late)
        rsum = sb("rsum", [P, NT], where=late)
        rinv = sb("rinv", [P, NT], where=late)
        cn = sb("cn", [P, NT], where=late)
        o1 = sb("o1", [P, D], where=late)
        phn = sb("phn", [NE, NP, P + 2 * DB], where=late)
        phT = sb("phT", [P, 2, NS], where=late)
        pss = sb("pss", [P, 2, NP], where=late)
        prs = sb("prs", [P, 2, NP], where=late)
        lnn = sb("lnn", [NE, 2, D], where=late)
        late.close()
        early.close()
        ec = sb("ec", [P, NT, NS])
        rsC = sb("rsC", [P, NT])
        riC = sb("riC", [P, NT])
        nmC = sb("nmC", [P, NT])
        xsT = sb("xsT", [DH + 1, 2, NE, NB, NP])
        w1r = [sb("w1r0", [DH + 1, GE, 2, HID])]
        w2r = [sb("w2r0", [P, GE, HC, D])]
        b2r = [sb("b2r0", [P, D])]
        ls = sb("ls", [P, KT, NS], where=moe_in)
        top = sb("top", [P, NS], where=moe_in)
        ctop = sb("ctop", [P, NS], where=moe_in)
        x2 = sb("x2", [P, NT, 1 + P + 2 * DB], where=moe_in)
        X2H = sb("X2H", [P, 2, 2, P], F32R, moe_in)
        X2L = sb("X2L", [P, 2, 2, P], F32R, moe_in)
        xs = sb("xs", [P, ST, D], where=moe_in)
        ci = sb("ci", [P, NB, ST], where=moe_in)
        xst6 = sb("xst6", [P, ST, 6], where=moe_in)
        xmv = sb("xmv", [P, ST, 2], where=moe_in)
        xve = sb("xve", [P, ST], where=moe_in)
        moe_in.close()
        RING = 3
        for r in range(1, RING):
            w1r.append(sb(f"w1r{r}", [DH + 1, GE, 2, HID]))
            w2r.append(sb(f"w2r{r}", [P, GE, HC, D]))
            b2r.append(sb(f"b2r{r}", [P, D]))
        hs = sb("hs", [P, 2, HID])
        hT = sb("hT", [P, 2, HC, P])
        ysb = sb("ysb", [P, 2, D])
        ys = sb("ys", [P, 2, NB, D])
        ct = sb("ct", [P, 2, KT, P])
        ys_dram = nc.dram_tensor("ys_dram", [NG, P, D], F32, kind="Internal").ap()

        ps = ctx.enter_context(nc.psum_tensor("ps", [P, 8, 512], F32))

        def bank(k, n=1):
            return ps[:, k:k + n, :].rearrange("p k c -> p (k c)")

        names = """in_ids in_tok in_mix in_attn in_phi barrier
            v_chain a_chain p_chain
            idsf_ready ids_permuted idx_ready maskp_ready mask_permuted mask_ready msum_ready count_ready
            cnt_ready wpt_ready setup_filled setup_taken ones_ready half_ready
            front_stats front_rstd xh_ready xT_filled xh_copied xl_ready q_filled q_squared q_normed q_fac
            qe_ready gram_done cprime_done cc_ready   xm_ready update_done r1_ready traces_done tt_ready mix_done
            mm_ready xl_ones wn_ready
            h_filled h_stats h_rstd h_taken x1_ready x1T_filled x1h_ready x1l_ready pr_filled pr_taken
            g_gelu g_shifted g_exp gw_ready gwT_filled gwT_hi gwT_taken
            u_filled u_taken qp_filled qph_taken qpl_taken  alpha_exp 
            s_filled gw_filled gw_copied z_ready e_ready et_filled et_copied_a et_copied_v o_filled o_taken
            norm_ready  ph_filled ph_copied ph_squared ph_summed ph_rsqrt ph_scaled ph_hi  ln_filled ln_taken
            f_stats f_rstd x2_ready x2t_ready x2T_filled x2h_ready x2l_ready l_filled l_copied lmax_ready c_exp
            top_ready ctop_ready d_shifted d_exp dispatched xs_taken xs_ready xs_stats xs_rstd xs_norm xsT_filled
            xsT_ready xsT_ones x2l_ones
            hid_filled hid_gelu hT_filled hT_ready y_filled y_ready cT_filled cT_copied
            yp_filled yp_taken   stored""".split()
        m = {n: sem(n) for n in names}
        gathered = [sem(f"gathered{i}") for i in range(NB * (KT + 1))]
        ys_stored = [sem(f"ys_stored{i}") for i in range(2)]
        ys_loaded = [sem(f"ys_loaded{i}") for i in range(2)]
        w_loaded = [sem(f"w_loaded{r}") for r in range(RING)]

        ENGINES = 5

        def meet(eng, n):
            eng.drain().then_inc(m["barrier"], 1)
            eng.wait_ge(m["barrier"], ENGINES * n)

        block = ctx.enter_context(nc.Block())

        def logit_bank(i):
            return 4 if i < KT and i % 2 else 0

        SETUP = ["wpA", "wpB1", "wpB2", "wqT", "wkT", "wvT3", "kA", "kB1", "kB2", "vA", "vB1", "vB2",
                 "tvA", "tvB", "toA", "toB", "bpA", "bpB", "nA", "nB1", "nB2"]
        at = {n: k for k, n in enumerate(SETUP)}

        BESIDE = [None] + SETUP[3:16] + [None] * (NT + 3 - 14) + ["bpA", "bpB", None]
        FIRST, LAST = at["wqT"], at["bpB"]

        def setup_bank(name):
            return bank(7) if FIRST <= at[name] <= LAST else bank(6 + at[name] % 2)

        def q_bank(i):
            return bank((2, 3, 6)[i % 3])

        def h_bank(i):
            return bank((0, 1, 2, 7)[i % 4])

        @block.sync
        def _(sp):
            x_rows = a["x"].rearrange("b (q c) -> (b q) c", c=C)
            sp.dma_start(ids[:, 0:C], x_rows).then_inc(m["in_ids"], 16)
            sp.dma_start(ids[0:P - 1, C:C + 2], x_rows[1:P, 0:2]).then_inc(m["in_ids"], 16)
            sp.dma_start(ids[P - 1:P, C:C + 2], x_rows[P - 1:P, 0:2]).then_inc(m["in_ids"], 16)
            sp.dma_start(ident[:], a["c_ident"]).then_inc(m["in_ids"], 16)
            sp.dma_start(links[:], a["L0_tok_link_ids"].unsqueeze(0).broadcast_to([P, NL])).then_inc(m["in_tok"], 16)
            sp.dma_start(valid[:], a["c_valid"]).then_inc(m["in_tok"], 16)
            sp.dma_start(gam[:], a["L0_tok_gamma"].unsqueeze(0).broadcast_to([P, D])).then_inc(m["in_tok"], 16)
            sp.dma_start(bet[:], a["L0_tok_beta"].unsqueeze(0).broadcast_to([P, D])).then_inc(m["in_tok"], 16)
            sp.dma_start(wp[:], a["L0_tok_W_proj"].rearrange("(t p) d -> p t d", p=P)).then_inc(m["in_tok"], 16)
            sp.dma_start(wqkA[:], a["L0_attn_W_qkv"][0:P, :]).then_inc(m["in_attn"], 16)
            sp.dma_start(wqkB[:], a["L0_attn_W_qkv"][P:D, :]).then_inc(m["in_attn"], 16)
            bq = a["L0_attn_b_qkv"].rearrange("(y d) -> d y", y=3)
            sp.dma_start(bcol[:, 0, :], bq[0:P, :], allow_slow_non_contiguous=True).then_inc(m["in_attn"], 16)
            sp.dma_start(bcol[0:DB, 1, :], bq[P:D, :], allow_slow_non_contiguous=True).then_inc(m["in_attn"], 16)
            for c, (lo, n) in enumerate(((0, P), (P, DB))):
                sp.dma_start(wpg[0:n, c, 0:D], a["L0_attn_W_proj"][lo:lo + n, :]).then_inc(m["in_attn"], 16)
                sp.dma_start(wpg[0:n, c, D:D + G], a["L0_attn_W_gp"][lo:lo + n, :]).then_inc(m["in_attn"], 16)
            sp.dma_start(bproj[:], a["L0_attn_b_proj"].unsqueeze(0).broadcast_to([P, D])).then_inc(m["in_attn"], 16)
            sp.dma_start(aw[:, 0:1], a["L0_attn_alpha"].broadcast_to([P, 1])).then_inc(m["in_attn"], 16)
            sp.dma_start(wv[:], a["L0_tok_W_val"].rearrange("(t p) d -> p t d", p=P)).then_inc(m["in_mix"], 16)
            sp.dma_start(woA[:], a["L0_tok_W_out"][0:P, :]).then_inc(m["in_mix"], 16)
            sp.dma_start(woB[:], a["L0_tok_W_out"][P:D, :]).then_inc(m["in_mix"], 16)
            v4 = a["L0_tok_value_traces"].rearrange("(t r) p q -> r p t q", r=2)
            for r in range(2):
                sp.dma_start(vt[r * DT:(r + 1) * DT, :, :], v4[r]).then_inc(m["in_mix"], 16)
            meet(sp, 1)
            sp.dma_start(phn[:, :, 0:D], a["L0_ffn_phi"]).then_inc(m["in_phi"], 16)
            sp.dma_start(phn[:, :, D:D + DB], a["L0_ffn_phi"][:, :, P:D]).then_inc(m["in_phi"], 16)
            sp.dma_start(lnn[:, 0, :], a["L0_ffn_ln_g"]).then_inc(m["in_phi"], 16)
            sp.dma_start(lnn[:, 1, :], a["L0_ffn_ln_b"]).then_inc(m["in_phi"], 16)
            meet(sp, 2)

            def load_group(g):
                r = g % RING
                e = slice(GE * g, GE * g + GE)
                sp.dma_start(w1r[r][0:DH, :, :, :],
                             a["L0_ffn_w1"][e].rearrange("e (c r) h -> r e c h", c=2)).then_inc(w_loaded[r], 16)
                sp.dma_start(w1r[r][DH:DH + 1, :, 1, :], a["L0_ffn_b1"][e].unsqueeze(0)).then_inc(w_loaded[r], 16)
                sp.dma_start(w2r[r][:], a["L0_ffn_w2"][e].rearrange("e (c r) d -> r e c d", c=HC)).then_inc(w_loaded[r], 16)
                for j in range(GE):
                    sp.dma_start(b2r[r][32 * j:32 * j + 32, :],
                                 a["L0_ffn_b2"][GE * g + j:GE * g + j + 1, :].broadcast_to([32, D])).then_inc(w_loaded[r], 16)

            load_group(0)
            meet(sp, 3)
            load_group(1)
            load_group(2)
            for g in range(NG):
                sp.wait_ge(m["y_ready"], g + 1)
                sp.dma_start(ys_dram[g], ysb[:, g % 2, :]).then_inc(ys_stored[g % 2], 16)
                if g + RING < NG:
                    load_group(g + RING)
                t = g // 2
                sp.wait_ge(ys_stored[g % 2], 16 * (t + 1))
                if t >= 2 and g % 2 == 0:
                    sp.wait_ge(m["yp_filled"], NT * (t - 1))
                rows = slice((g % 2) * GE * NP, (g % 2 + 1) * GE * NP)
                y4 = ys_dram[g].rearrange("(j b s) d -> b j s d", b=NB, s=NP)
                for b in range(NB):
                    sp.dma_start(ys[rows, t % 2, b, :], y4[b]).then_inc(ys_loaded[t % 2], 16)
            o4 = out.rearrange("b (q c) d -> b q c d", c=C)
            for i in range(NT):
                b, k = divmod(i, KT)
                sp.wait_ge(m["yp_taken"], NT * (ST - 1) + i + 1)
                for jj in range(2):
                    sp.dma_start(o4[b, :, 2 * k + jj, :], res[jj * Q:(jj + 1) * Q, i, :]).then_inc(m["stored"], 16)
            sp.wait_ge(m["stored"], 16 * 2 * NT)

        @block.gpsimd
        def _(pool):
            pc = [0]

            def link(ins):
                pc[0] += 1
                ins.then_inc(m["p_chain"], 1)
                pool.wait_ge(m["p_chain"], pc[0])

            nc.gpsimd.memset(ones[:], 1.0).then_inc(m["ones_ready"], 1)
            link(nc.gpsimd.memset(mhalf[:], -0.5))
            nc.gpsimd.memset(XL[DB:P, 1, :].bitcast(F32), 1.0).then_inc(m["xl_ones"], 1)
            pool.wait_ge(m["idx_ready"], 1)
            for i in range(NB * (KT + 1)):
                nc.gpsimd.indirect_dma_start(
                    tok[:, i, :], None, a["L0_tok_wte"], bass.IndirectOffsetOnAxis(ap=idx[:, i:i + 1], axis=0)
                ).then_inc(gathered[i], 16)
            pool.wait_ge(m["xl_ones"], 1)
            nc.gpsimd.memset(X1L[DB:P, 1, :].bitcast(F32), 1.0).then_inc(m["xl_ones"], 1)
            pool.wait_ge(m["xl_ones"], 2)

            def rsqrt(i, eps):
                link(nc.gpsimd.tensor_scalar(ve[:, i:i + 1], mv[:, i, 1:2], eps, None, ALU.add))
                return nc.gpsimd.tensor_tensor(rstd[:, i:i + 1], ve[:, i:i + 1], mhalf[:, 0:1], ALU.pow)

            for b in range(NB):
                t = slice(b * KT, (b + 1) * KT)
                pool.wait_ge(m["front_stats"], (b + 1) * KT)
                link(nc.gpsimd.tensor_scalar(ve[:, t], mv[:, t, 1], 1e-5, None, ALU.add))
                link(nc.gpsimd.tensor_tensor(rstd[:, t], ve[:, t], mhalf[:, 0:KT], ALU.pow))
                link(nc.gpsimd.tensor_tensor(nmr[:, t], mv[:, t, 0], rstd[:, t], ALU.mult))
                nc.gpsimd.tensor_scalar(nmr[:, t], nmr[:, t], -1.0, None, ALU.mult).then_inc(m["front_rstd"], 1)

            def masked(i):
                pool.wait_ge(m["xh_ready"], i + 1)
                if i >= 3:
                    pool.wait_ge(m["cprime_done"], i - 2)
                nc.gpsimd.tensor_scalar(xm[:, i % 3, 0:D], xh[:, i % 3, 0:D], mask[:, i:i + 1], None, ALU.mult)
                nc.gpsimd.tensor_copy(xm[:, i % 3, D:D + 1], mask[:, i:i + 1]).then_inc(m["xm_ready"], 1)

            def head_factors(i):
                pool.wait_ge(m["q_normed"], i + 1)
                link(nc.gpsimd.tensor_scalar(fac[:, i, :], ss[:, i, :], 1e-16, None, ALU.max))
                link(nc.gpsimd.tensor_tensor(fac[:, i, :], fac[:, i, :], mhalf[:, 0:HEADS], ALU.pow))
                nc.gpsimd.tensor_scalar(fac[:, i, :], fac[:, i, :], mask[:, i:i + 1], None, ALU.mult).then_inc(m["q_fac"], 1)

            pool.wait_ge(m["mask_ready"], 1)
            for s in range(NT + 4):
                if s < NT:
                    masked(s)
                if 4 <= s:
                    head_factors(s - 4)

            def ln_factors(i, eps, done):
                link(rsqrt(i, eps))
                nc.gpsimd.tensor_scalar(nmr[:, i:i + 1], mv[:, i, 0:1], rstd[:, i:i + 1], -1.0,
                                        ALU.mult, ALU.mult).then_inc(done, 1)

            for i in range(NT):
                pool.wait_ge(m["h_stats"], i + 1)
                ln_factors(i, 1e-5, m["h_rstd"])
            meet(pool, 1)
            nc.gpsimd.memset(gw[:], 0.0).then_inc(m["half_ready"], 1)
            pool.wait_ge(m["ph_summed"], 1)
            link(nc.gpsimd.tensor_scalar(prs[:], pss[:], 1e-6, None, ALU.add))
            nc.gpsimd.tensor_tensor(prs[:].rearrange("p c k -> p (c k)"), prs[:].rearrange("p c k -> p (c k)"),
                                    mhalf[:, 0:2 * NP], ALU.pow).then_inc(m["ph_rsqrt"], 1)
            for i in range(NT):
                pool.wait_ge(m["f_stats"], i + 1)
                ln_factors(i, 1e-5, m["f_rstd"])
            meet(pool, 2)
            nc.gpsimd.memset(xsT[DH:DH + 1, 1, :, :, :], 1.0).then_inc(m["xsT_ones"], 1)
            pool.wait_ge(m["xsT_ones"], 1)
            for i in range(NT):
                pool.wait_ge(m["x2_ready"], i + 1)
                nc.gpsimd.tensor_copy(x2[:, i, 1 + D:1 + D + DB], x2[:, i, 1 + P:1 + D]).then_inc(m["x2t_ready"], 1)

            def all_tokens_top(b):
                pool.wait_ge(m["x2t_ready"], NT)
                pool.wait_ge(m["top_ready"], KT * (b + 1))
                if b:
                    pool.wait_ge(m["d_shifted"], KT * b)
                nc.gpsimd.partition_all_reduce(ctop[:], top[:], P, bass.bass_isa.ReduceOp.max).then_inc(m["ctop_ready"], 1)
                pool.wait_ge(m["ctop_ready"], b + 1)

            def xs_factors(b):
                pool.wait_ge(m["xs_stats"], b + 1)
                link(nc.gpsimd.tensor_scalar(xve[:], xmv[:, :, 1], 1e-5, None, ALU.add))
                nc.gpsimd.tensor_tensor(xve[:], xve[:], mhalf[:, 0:ST], ALU.pow).then_inc(m["xs_rstd"], 1)

            all_tokens_top(0)
            for k in range(KT):
                pool.wait_ge(m["c_exp"], k + 1)
                nc.gpsimd.tensor_tensor(ls[:, k, :], ls[:, k, :], ctop[:], ALU.subtract).then_inc(m["d_shifted"], 1)
            all_tokens_top(1)
            for b in range(NB):
                xs_factors(b)
            meet(pool, 3)

        @block.tensor
        def _(pe):
            mm = nc.tensor.matmul

            def fill(name):
                k = at[name]
                if FIRST <= k <= LAST + 1:
                    pe.wait_ge(m["setup_taken"], k)
                elif k >= 2:
                    pe.wait_ge(m["setup_taken"], k - 1)
                return setup_bank(name)

            def filled(ins):
                ins.then_inc(m["setup_filled"], 1)

            def permute(dst, src, n):
                for b in range(NB):
                    for jj in range(2):
                        last = mm(dst[jj * Q:(jj + 1) * Q, b * n:(b + 1) * n], ident[:, b * Q:(b + 1) * Q],
                                  src[:, jj:2 * n:2], start=True, stop=True)
                return last

            def product(dst, xH, xL, wAh, wAl, wB1, wB2):
                mm(dst, xH(0, P), wAh, start=True, stop=False)
                mm(dst, xH(0, P), wAl, start=False, stop=False)
                mm(dst, xL(0, P), wAh, start=False, stop=False)
                mm(dst, xH(1, P), wB1, start=False, stop=False)
                return mm(dst, xL(1, DB + 2), wB2, start=False, stop=True)

            pe.wait_ge(m["in_ids"], 64)
            pe.wait_ge(m["idsf_ready"], 1)
            permute(bank(5), idsf, KT + 1).then_inc(m["ids_permuted"], 1)
            pe.wait_ge(m["maskp_ready"], 1)
            permute(bank(4), maskP, KT).then_inc(m["mask_permuted"], 1)
            pe.wait_ge(m["msum_ready"], 1)
            pe.wait_ge(m["ones_ready"], 1)
            mm(bank(3)[:, 0:1], ones[:], msum[:], start=True, stop=True).then_inc(m["count_ready"], 1)

            pe.wait_ge(m["wpt_ready"], 1)
            for name, lo, n in (("wpA", 0, P), ("wpB1", CB1, P), ("wpB2", CB2, DB + 2)):
                d = fill(name)
                for t in range(HP):
                    last = nc.tensor.transpose(d[0:n, t * P:(t + 1) * P], wpt[:, t, lo:lo + n], ident[:])
                filled(last)
            def prepare(name):
                if name in ("wqT", "wkT", "wvT3"):
                    y = ("wqT", "wkT", "wvT3").index(name)
                    pe.wait_ge(m["in_attn"], 16 * 10)
                    d = fill(name)
                    for c, (lo, n) in enumerate(((0, P), (P, DB))):
                        cols = slice(y * D + lo, y * D + lo + n)
                        nc.tensor.transpose(d[0:n, c * D:c * D + P], wqkA[:, cols], ident[:])
                        last = nc.tensor.transpose(d[0:n, c * D + P:(c + 1) * D], wqkB[:, cols], ident[0:DB, 0:DB])
                elif name[0] in "kv":
                    lo, n = {"A": (0, P), "B1": (CB1, P), "B2": (CB2, DB + 2)}[name[1:]]
                    d = fill(name)
                    if name[0] == "k":
                        mm(d[0:n, 0:P + 2 * DB], wTq[:, 0, lo:lo + n], wTk[:, 0, :], start=True, stop=False)
                        last = mm(d[0:n, 0:P + 2 * DB], wTq[0:DB, 1, lo:lo + n], wTk[0:DB, 1, :], start=False, stop=True)
                    else:
                        mm(d[0:n, 0:D + G], wTv[:, 0, lo:lo + n], wpg[:, 0, :], start=True, stop=False)
                        mm(d[0:n, 0:D + G], wTv[0:DB, 1, lo:lo + n], wpg[0:DB, 1, :], start=False, stop=True)
                        mm(d[0:n, D + G:W2N], wTq[:, 0, lo:lo + n], bcol[:, 0, 1:2], start=True, stop=False)
                        last = mm(d[0:n, D + G:W2N], wTq[0:DB, 1, lo:lo + n], bcol[0:DB, 1, 1:2], start=False, stop=True)
                elif name in ("tvA", "tvB"):
                    lo, n = {"tvA": (0, P), "tvB": (P, DB)}[name]
                    pe.wait_ge(m["in_mix"], 16 * 5)
                    d = fill(name)
                    for t in range(HP):
                        last = nc.tensor.transpose(d[0:n, t * P:(t + 1) * P], wv[:, t, lo:lo + n], ident[:])
                elif name in ("toA", "toB"):
                    n, rows = {"toA": (P, woA), "toB": (DB, woB)}[name]
                    d = fill(name)
                    for t in range(HP):
                        last = nc.tensor.transpose(d[:, t * n:(t + 1) * n], rows[:, t * P:(t + 1) * P], ident[0:n, 0:n])
                else:
                    lo, n = {"bpA": (0, P), "bpB": (P, DB)}[name]
                    pe.wait_ge(m["cc_ready"], 1)
                    d = fill(name)
                    mm(d[0:n, :], cc[:, 0, lo:lo + n], wpT[:, 0, :], start=True, stop=False)
                    last = mm(d[0:n, :], cc[0:DB + 1, 1, lo:lo + n], wpT[0:DB + 1, 1, :], start=False, stop=True)
                filled(last)

            def slots(b, s):
                lo = (b * SLOTS + s) * Q
                return slice(lo, lo + P)

            gram = bank(4)[:, 0:HP * DT].rearrange("p (t c) -> p t c", t=HP)
            cpr = bank(5)

            def tok_T(i):
                pe.wait_ge(m["xh_ready"], i + 1)
                if i >= 2:
                    pe.wait_ge(m["xl_ready"], i - 1)
                d = bank(i % 2)
                nc.tensor.transpose(d[:, 0:P], xh[:, i % 3, 0:P], ident[:])
                nc.tensor.transpose(d[:, P:2 * P], xh[:, i % 3, P:P + 2 * DB], ident[:]).then_inc(m["xT_filled"], 1)

            def cprime(i):
                b, k = divmod(i, KT)
                nxt = b * (KT + 1) + k + 1
                pe.wait_ge(m["xm_ready"], i + 1)
                pe.wait_ge(gathered[nxt], 16)
                mm(cpr[:, 0:D], xm[:, i % 3, 0:P], tok[:, nxt, :], start=(i == 0), stop=False, skip_group_check=True)
                mm(cpr[0:DB + 1, 256:256 + D], xm[:, i % 3, P:D + 1], tok[:, nxt, :], start=False, stop=False,
                   skip_group_check=True).then_inc(m["cprime_done"], 1)

            def q_proj(i):
                b, k = divmod(i, KT)
                pe.wait_ge(m["xl_ready"], i + 1)
                if i >= 3:
                    pe.wait_ge(m["qe_ready"], i - 2)
                elif i == 2:
                    pe.wait_ge(m["setup_taken"], FIRST)
                c = slots(b, 2 * k + 1)
                product(q_bank(i), lambda h, n: XH[0:n, h, c], lambda h, n: XL[0:n, h, c],
                        wpAh[:], wpAl[:], wpB1[:], wpB2[:]).then_inc(m["q_filled"], 1)

            def grams(i):
                pe.wait_ge(m["qe_ready"], i + 1)
                for h in range(HEADS):
                    t, r = divmod(h, 2)
                    q = qe[:, i % 2, h * DT:(h + 1) * DT]
                    last = mm(gram[r * DT:(r + 1) * DT, t, :], q, q, start=(i == 0 and t == 0), stop=False,
                              skip_group_check=True)
                last.then_inc(m["gram_done"], 1)

            pe.wait_ge(m["cnt_ready"], 1)
            pe.wait_ge(m["xl_ones"], 1)
            for s in range(NT + 6):
                if 3 <= s < NT + 3:
                    q_proj(s - 3)
                if 6 <= s:
                    grams(s - 6)
                if 1 <= s < NT + 1:
                    tok_T(s - 1)
                if 2 <= s < NT + 2:
                    cprime(s - 2)
                if BESIDE[s]:
                    prepare(BESIDE[s])

            pe.wait_ge(m["setup_taken"], at["bpB"] + 1)
            for h in range(HEADS):
                t, r = divmod(h, 2)
                rows, cols = slice(r * DT, (r + 1) * DT), slice(h * DT, (h + 1) * DT)
                d = bank(0)[rows, t * DT:(t + 1) * DT]
                mm(d, wvT[:, 0, cols], bs[:, 0, cols], start=True, stop=False)
                last = mm(d, wvT[0:DB, 1, cols], bs[0:DB, 1, cols], start=False, stop=True)
            last.then_inc(m["update_done"], 1)
            pe.wait_ge(m["r1_ready"], 1)
            for r in range(2):
                rows = slice(r * DT, (r + 1) * DT)
                for t in range(HP):
                    last = mm(bank(1 + 2 * r)[rows, t * DT:(t + 1) * DT], vt[rows, t, :], r1[rows, t, :], start=True, stop=True)
            last.then_inc(m["traces_done"], 1)
            pe.wait_ge(m["tt_ready"], 1)
            for odd in range(2):
                for t in range(odd, HP, 2):
                    d = bank(2 * odd + t // 2)[:, 0:D]
                    for r in range(2):
                        rows = slice(r * DT, (r + 1) * DT)
                        last = mm(d[rows, :], tt[rows, t, :], woT[rows, t, :], start=True, stop=True)
                last.then_inc(m["mix_done"], 1)
            pe.wait_ge(m["mm_ready"], 2)
            for name, lo, n in (("nA", 0, P), ("nB1", CB1, P), ("nB2", CB2, DB + 2)):
                d = fill(name)
                for t in range(HP):
                    last = mm(d[0:n, 0:D], wpt[:, t, lo:lo + n], mm_[:, t, :], start=(t == 0), stop=(t == HP - 1))
                filled(last)
            pe.wait_ge(m["setup_taken"], len(SETUP))
            pe.wait_ge(m["wn_ready"], NB)

            def mixed(i):
                b, k = divmod(i, KT)
                if i >= 4:
                    pe.wait_ge(m["x1_ready"], i - 3)
                    pe.wait_ge(m["h_taken"], i - 3)
                c = slots(b, 2 * k)
                product(h_bank(i)[:, 0:D], lambda h, n: XH[0:n, h, c], lambda h, n: XL[0:n, h, c],
                        nAh[:], nAl[:], nB1[:], nB2[:]).then_inc(m["h_filled"], 1)

            def x1_T(i):
                pe.wait_ge(m["x1_ready"], i + 1)
                if i >= 2:
                    pe.wait_ge(m["x1l_ready"], i - 1)
                d = bank(3 + i % 2)
                nc.tensor.transpose(d[:, 0:P], x1t[:, i % 3, 0:P], ident[:])
                nc.tensor.transpose(d[:, P:2 * P], x1t[:, i % 3, P:P + 2 * DB], ident[:]).then_inc(m["x1T_filled"], 1)

            def value_proj(i):
                pe.wait_ge(m["x1l_ready"], i + 1)
                if i >= 2:
                    pe.wait_ge(m["pr_taken"], i - 1)
                c = slice(i * P, (i + 1) * P)
                product(bank(5 + i % 2)[:, 0:W2N], lambda h, n: X1H[0:n, h, c], lambda h, n: X1L[0:n, h, c],
                        vAh[:], vAl[:], vB1[:], vB2[:]).then_inc(m["pr_filled"], 1)

            pe.wait_ge(m["xl_ones"], 2)
            for s in range(NT + 5):
                if s < NT:
                    mixed(s)
                if 3 <= s < NT + 3:
                    x1_T(s - 3)
                if 5 <= s:
                    value_proj(s - 5)
            meet(pe, 1)

            j = 0
            for blk in range(NT * P // 512):
                for c0, w in ((0, slice(0, P)), (1, slice(P, P + 2 * DB))):
                    if j >= 3:
                        pe.wait_ge(m["qpl_taken"], j - 2)
                    d = bank(j % 3)
                    n = slice(blk * 512, (blk + 1) * 512)
                    mm(d, kAh[:, w], X1H[:, 0, n], start=True, stop=False)
                    mm(d, kAl[:, w], X1H[:, 0, n], start=False, stop=False)
                    mm(d, kAh[:, w], X1L[:, 0, n], start=False, stop=False)
                    mm(d, kB1[:, w], X1H[:, 1, n], start=False, stop=False)
                    mm(d, kB2[:, w], X1L[0:DB + 2, 1, n], start=False, stop=True).then_inc(m["qp_filled"], 1)
                    j += 1
            pe.wait_ge(m["in_phi"], 64)
            for j in range(4):
                half, p8 = divmod(j, 2)
                if j >= 2:
                    pe.wait_ge(m["ph_copied"], j - 1)
                d = bank(3 + j % 2)
                for q in range(8):
                    last = nc.tensor.transpose(d[:, q * NE:(q + 1) * NE], phn[:, 8 * p8 + q, half * P:(half + 1) * P],
                                               ident[0:NE, 0:NE])
                last.then_inc(m["ph_filled"], 1)
            d = bank(5)
            for w in range(4):
                last = nc.tensor.transpose(d[0:DH, w * NE:(w + 1) * NE], lnn[:, w // 2, (w % 2) * DH:(w % 2 + 1) * DH],
                                           ident[0:NE, 0:NE])
            last.then_inc(m["ln_filled"], 1)
            pe.wait_ge(m["gw_ready"], 1)
            for j in range(NT // 4):
                d = bank(6 + j % 2)
                if j >= 2:
                    pe.wait_ge(m["gwT_taken"], j - 1)
                for q in range(4):
                    last = nc.tensor.transpose(d[:, q * P:(q + 1) * P], gw[:, 4 * j + q, :], ident[:])
                last.then_inc(m["gwT_filled"], 1)
            pe.wait_ge(m["qpl_taken"], 8)
            for b in range(NB):
                d = bank(b)[:, 0:D]
                for k in range(KT):
                    i = b * KT + k
                    last = mm(d, gw[:, i, :], pr[:, i, 0:D], start=(k == 0), stop=(k == KT - 1))
                last.then_inc(m["u_filled"], 1)
            pe.wait_ge(m["gwT_taken"], NT // 4)
            pe.wait_ge(m["u_taken"], NB)
            pe.wait_ge(m["ph_copied"], 4)
            pe.wait_ge(m["ln_taken"], 1)

            def scores(i):
                b = i // KT
                n = slice(i * P, (i + 1) * P)
                if i >= 1:
                    pe.wait_ge(m["z_ready"], i)
                for hf in range(2):
                    d = bank(hf)
                    c = slice(b * S + hf * 512, b * S + (hf + 1) * 512)
                    mm(d, qAh[:, n], X1H[:, 0, c], start=True, stop=False)
                    mm(d, qAl[:, n], X1H[:, 0, c], start=False, stop=False)
                    mm(d, qAh[:, n], X1L[:, 0, c], start=False, stop=False)
                    mm(d, qB[:, n], X1H[:, 1, c], start=False, stop=False)
                    last = mm(d, qB[0:DB, n], X1L[0:DB, 1, c], start=False, stop=True)
                last.then_inc(m["s_filled"], 1)
                if i >= 1:
                    pe.wait_ge(m["gw_copied"], i)
                for hf in range(2):
                    d = bank(2 + hf)
                    c = slice(b * S + hf * 512, b * S + (hf + 1) * 512)
                    mm(d, gP[0:DB + G, n], gD[0:DB + G, c], start=True, stop=False)
                    last = mm(d, gP[0:G, n], gL[0:G, c], start=False, stop=True)
                last.then_inc(m["gw_filled"], 1)

            def attend(i):
                b = i // KT
                n = slice(i * P, (i + 1) * P)
                pe.wait_ge(m["e_ready"], i + 1)
                if i >= 1:
                    pe.wait_ge(m["et_copied_a"], i)
                    pe.wait_ge(m["et_copied_v"], i)
                for k in range(KT):
                    last = nc.tensor.transpose(bank(4 + k // 4)[:, (k % 4) * P:(k % 4 + 1) * P],
                                               zz[:, i % 2, k * P:(k + 1) * P], ident[:])
                    if k % 4 == 3:
                        last.then_inc(m["et_filled"], 1)
                if i >= 2:
                    pe.wait_ge(m["o_taken"], i - 1)
                d = bank(6 + i % 2)
                mm(d[:, 256:256 + D], gD[0:DB + G, n], uP[0:DB + G, b, :], start=True, stop=False)
                mm(d[:, 256:256 + D], gL[0:G, n], uP[0:G, b, :], start=False, stop=True)
                for k in range(KT):
                    if k == 0:
                        pe.wait_ge(m["et_copied_a"], i + 1)
                    if k == KT // 2:
                        pe.wait_ge(m["et_copied_v"], i + 1)
                    last = mm(d[:, 0:D], et[:, k, :], pr[:, b * KT + k, 0:D], start=(k == 0), stop=(k == KT - 1))
                last.then_inc(m["o_filled"], 1)

            for s in range(NT + 1):
                if s < NT:
                    scores(s)
                if s >= 1:
                    attend(s - 1)
            meet(pe, 2)

            def x2_T(i):
                pe.wait_ge(m["x2t_ready"], i + 1)
                if i >= 2:
                    pe.wait_ge(m["x2l_ready"], i - 1)
                d = bank(2 + i % 2)
                nc.tensor.transpose(d[:, 0:P], x2[:, i, 1:1 + P], ident[:])
                nc.tensor.transpose(d[:, P:2 * P], x2[:, i, 1 + P:1 + P + 2 * DB], ident[:]).then_inc(m["x2T_filled"], 1)

            def logits(i):
                pe.wait_ge(m["x2l_ready"], i + 1)
                if i >= 1:
                    n = i if i > KT else i - 1
                    if n:
                        pe.wait_ge(m["l_copied"], n)
                for hf in range(2):
                    d = bank(logit_bank(i) + hf)
                    c = slice(hf * 512, (hf + 1) * 512)
                    xHt, xLt = X2H[:, i % 2], X2L[:, i % 2]
                    mm(d, xHt[:, 0, :], phAh[:, c], start=True, stop=False)
                    mm(d, xHt[:, 0, :], phAl[:, c], start=False, stop=False)
                    mm(d, xLt[:, 0, :], phAh[:, c], start=False, stop=False)
                    mm(d, xHt[:, 1, :], phB[:, c], start=False, stop=False)
                    last = mm(d, xLt[0:DB, 1, :], phB[0:DB, c], start=False, stop=True)
                last.then_inc(m["l_filled"], 1)

            def dispatch(b, k):
                i = b * KT + k
                pe.wait_ge(m["d_exp"], i + 1)
                if k == 0:
                    if b:
                        pe.wait_ge(m["xs_taken"], b)
                    else:
                        pe.wait_ge(m["l_copied"], KT)
                for t in range(ST):
                    d = bank(4 + t // 2)[:, (t % 2) * 256:(t % 2) * 256 + 1 + D]
                    last = mm(d, ls[:, k, t * P:(t + 1) * P], x2[:, i, 0:1 + D], start=(k == 0 and t % 2 == 0),
                              stop=(k == KT - 1), skip_group_check=True)
                last.then_inc(m["dispatched"], 1)

            def xs_T(b):
                pe.wait_ge(m["xs_norm"], b + 1)
                if b:
                    pe.wait_ge(m["xsT_ready"], b)
                for half in range(2):
                    for t in range(ST):
                        last = nc.tensor.transpose(bank(2 * half + t // 4)[0:DH, (t % 4) * P:(t % 4 + 1) * P],
                                                   xs[:, t, half * DH:(half + 1) * DH], ident[:])
                last.then_inc(m["xsT_filled"], 1)

            pe.wait_ge(m["x2l_ones"], 1)
            for s in range(KT + 1):
                x2_T(s)
                if s >= 1:
                    logits(s - 1)
            logits(KT)
            dispatch(0, 0)
            for s in range(1, KT):
                x2_T(KT + s)
                dispatch(0, s)
                logits(KT + s)
            pe.wait_ge(m["l_copied"], NT)
            xs_T(0)
            for k in range(KT):
                dispatch(1, k)
            xs_T(1)
            meet(pe, 3)

            def hidden(g):
                r = g % RING
                pe.wait_ge(w_loaded[r], 16 * (3 + GE) * (g // RING + 1))
                if g >= 1:
                    pe.wait_ge(m["hid_gelu"], g)
                for half in range(2):
                    n = DH + half
                    for j in range(GE):
                        last = mm(bank(0)[32 * j:32 * j + 32, 0:HID],
                                  xsT[0:n, half, GE * g + j, :, :].rearrange("d b s -> d (b s)"),
                                  w1r[r][0:n, j, half, :], start=(half == 0), stop=(half == 1),
                                  tile_position=(0, 32 * j))
                last.then_inc(m["hid_filled"], 1)

            def hidden_T(g):
                pe.wait_ge(m["hid_gelu"], g + 1)
                if g >= 1:
                    pe.wait_ge(m["hT_ready"], g)
                for c in range(HC):
                    last = nc.tensor.transpose(bank(1)[:, c * P:(c + 1) * P], hs[:, g % 2, c * P:(c + 1) * P], ident[:])
                last.then_inc(m["hT_filled"], 1)

            def expert_out(g):
                r = g % RING
                pe.wait_ge(m["hT_ready"], g + 1)
                if g >= 1:
                    pe.wait_ge(m["y_ready"], g)
                for c in range(HC):
                    for j in range(GE):
                        last = mm(bank(2)[32 * j:32 * j + 32, 0:D], hT[:, g % 2, c, 32 * j:32 * j + 32],
                                  w2r[r][:, j, c, :], start=(c == 0), stop=(c == HC - 1), tile_position=(0, 32 * j))
                last.then_inc(m["y_filled"], 1)

            def combine_T(u):
                t, b = divmod(u, NB)
                if u >= 1:
                    pe.wait_ge(m["cT_copied"], u)
                for k in range(KT):
                    last = nc.tensor.transpose(bank(3 + k // 4)[:, (k % 4) * P:(k % 4 + 1) * P],
                                               ec[:, b * KT + k, t * P:(t + 1) * P], ident[:])
                last.then_inc(m["cT_filled"], 1)

            def combine(u):
                t, b = divmod(u, NB)
                pe.wait_ge(m["cT_copied"], u + 1)
                pe.wait_ge(ys_loaded[t % 2], 16 * 2 * NB * (t // 2 + 1))
                for k in range(KT):
                    q = u * KT + k
                    if q >= 3:
                        pe.wait_ge(m["yp_taken"], q - 2)
                    mm(bank(5 + q % 3)[:, 0:D], ct[:, u % 2, k, :], ys[:, t % 2, b, :], start=True,
                       stop=True).then_inc(m["yp_filled"], 1)

            LAG = 4
            for s in range(NG + LAG + 1):
                if s < NG:
                    hidden(s)
                if LAG <= s < NG + LAG:
                    combine(s - LAG)
                if s < NG:
                    hidden_T(s)
                if LAG - 1 <= s < NG + LAG - 1:
                    combine_T(s - LAG + 1)
                if s < NG:
                    expert_out(s)

        @block.scalar
        def _(act):
            sc = nc.scalar
            ac = [0]

            def link(ins):
                ac[0] += 1
                ins.then_inc(m["a_chain"], 1)
                act.wait_ge(m["a_chain"], ac[0])

            def normalise(i):
                b, k = divmod(i, KT)
                t = b * (KT + 1) + k
                act.wait_ge(m["front_rstd"], b + 1)
                act.wait_ge(gathered[t], 16)
                if i >= 3:
                    act.wait_ge(m["xT_filled"], i - 2)
                    act.wait_ge(m["xm_ready"], i - 2)
                sc.activation(xh[:, i % 3, 0:D], tok[:, t, :], ACT.Identity, bias=nmr[:, i:i + 1], scale=rstd[:, i:i + 1])
                sc.activation(xh[:, i % 3, D:D + DB], tok[:, t, P:D], ACT.Identity, bias=nmr[:, i:i + 1],
                              scale=rstd[:, i:i + 1]).then_inc(m["xh_ready"], 1)

            def hi_parts(i):
                b, k = divmod(i, KT)
                lo = (b * SLOTS + 2 * k + 1) * Q
                act.wait_ge(m["xT_filled"], i + 1)
                sc.copy(XH[:, :, lo:lo + P], bank(i % 2)[:, 0:2 * P].rearrange("p (h c) -> p h c", h=2)
                        ).then_inc(m["xh_copied"], 1)

            def squares(i):
                act.wait_ge(m["q_filled"], i + 1)
                if i >= 2:
                    act.wait_ge(m["q_normed"], i - 1)
                sc.activation(sq[:, i % 2, :], q_bank(i), ACT.Square).then_inc(m["q_squared"], 1)

            for s in range(NT + 3):
                if 2 <= s < NT + 2:
                    hi_parts(s - 2)
                if s < NT:
                    normalise(s)
                if 3 <= s:
                    squares(s - 3)

            act.wait_ge(m["mix_done"], 1)
            for t in range(0, HP, 2):
                last = sc.copy(mm_[:, t, :], bank(t // 2)[:, 0:D])
            last.then_inc(m["mm_ready"], 1)
            for s in range(NT + 6):
                if 4 <= s < NT + 4:
                    i = s - 4
                    act.wait_ge(m["x1T_filled"], i + 1)
                    sc.copy(X1H[:, :, i * P:(i + 1) * P], bank(3 + i % 2)[:, 0:2 * P].rearrange("p (h c) -> p h c", h=2)
                            ).then_inc(m["x1h_ready"], 1)
                if 2 <= s < NT + 2:
                    i = s - 2
                    act.wait_ge(m["h_rstd"], i + 1)
                    if i >= 3:
                        act.wait_ge(m["x1T_filled"], i - 2)
                    d = h_bank(i)
                    sc.activation(x1t[:, i % 3, 0:D], d[:, 0:D], ACT.Identity, bias=nmr[:, i:i + 1], scale=rstd[:, i:i + 1])
                    sc.activation(x1t[:, i % 3, D:D + DB], d[:, P:D], ACT.Identity, bias=nmr[:, i:i + 1],
                                  scale=rstd[:, i:i + 1]).then_inc(m["x1_ready"], 1)
                if s >= 6:
                    i = s - 6
                    act.wait_ge(m["pr_filled"], i + 1)
                    sc.copy(pr[:, i, :], bank(5 + i % 2)[:, 0:W2N]).then_inc(m["pr_taken"], 1)
            meet(act, 1)
            logit = pr[:, :, D:D + G]
            sc.activation(logit, logit, ACT.Gelu).then_inc(m["g_gelu"], 1)
            for j in range(2 * (NT * P // 512)):
                blk, c0 = divmod(j, 2)
                act.wait_ge(m["qp_filled"], j + 1)
                sc.copy((qB if c0 else qAh)[:, blk * 512:(blk + 1) * 512], bank(j % 3)).then_inc(m["qph_taken"], 1)
                if j == 1:
                    act.wait_ge(m["g_shifted"], 1)
                    sc.activation(logit, logit, ACT.Exp).then_inc(m["g_exp"], 1)
                    sc.activation(aw[:, 1:2], aw[:, 0:1], ACT.Exp, scale=-1.0).then_inc(m["alpha_exp"], 1)
            for j in range(4):
                half, p8 = divmod(j, 2)
                act.wait_ge(m["ph_filled"], j + 1)
                sc.copy(phT[:, half, :].rearrange("d (n p) -> d p n", p=NP)[:, 8 * p8:8 * p8 + 8, :],
                        bank(3 + j % 2).rearrange("d (p n) -> d p n", n=NE)).then_inc(m["ph_copied"], 1)
            act.wait_ge(m["ph_copied"], 4)
            sc.activation(zz[:], phT[:], ACT.Square).then_inc(m["ph_squared"], 1)
            for j in range(NT // 4):
                act.wait_ge(m["gwT_filled"], j + 1)
                c = slice(j * 512, (j + 1) * 512)
                sc.copy(gP[0:DB, c], bank(6 + j % 2)[0:DB, :])
                sc.copy(gD[:, c], bank(6 + j % 2)).then_inc(m["gwT_hi"], 1)
            act.wait_ge(m["ph_scaled"], 1)
            sc.copy(phAh[:], phT[:, 0, :])
            sc.copy(phB[:], phT[:, 1, :]).then_inc(m["ph_hi"], 1)

            def group_weights(i):
                act.wait_ge(m["gw_filled"], i + 1)
                if i >= 1:
                    act.wait_ge(m["z_ready"], i)
                sc.copy(gws[:], bank(2, 2)).then_inc(m["gw_copied"], 1)

            def exps(i):
                act.wait_ge(m["norm_ready"], i + 1)
                sc.activation(zz[:, i % 2, :], zz[:, i % 2, :], ACT.Exp, bias=nmx[:, i:i + 1],
                              accum_out=rsum[:, i:i + 1]).then_inc(m["e_ready"], 1)

            def turn(i):
                act.wait_ge(m["et_filled"], 2 * i + 1)
                if i >= 1:
                    act.wait_ge(m["o_filled"], i)
                sc.copy(et[:, 0:KT // 2, :].rearrange("p k c -> p (k c)"), bank(4)).then_inc(m["et_copied_a"], 1)

            for s in range(NT + 1):
                if s >= 1:
                    exps(s - 1)
                    turn(s - 1)
                if s < NT:
                    group_weights(s)
            meet(act, 2)

            def x2_tile(i):
                act.wait_ge(m["f_rstd"], i + 1)
                sc.activation(x2[:, i, 1:1 + D], res[:, i, :], ACT.Identity, bias=nmr[:, i:i + 1], scale=rstd[:, i:i + 1]
                              ).then_inc(m["x2_ready"], 1)

            def x2_hi(i):
                act.wait_ge(m["x2T_filled"], i + 1)
                if i >= 2:
                    act.wait_ge(m["l_filled"], i - 1)
                sc.copy(X2H[:, i % 2, :, :], bank(2 + i % 2)[:, 0:2 * P].rearrange("p (h c) -> p h c", h=2)
                        ).then_inc(m["x2h_ready"], 1)

            def c_exps(i):
                act.wait_ge(m["lmax_ready"], i + 1)
                sc.activation(ec[:, i, :], ls[:, i % KT, :], ACT.Exp, bias=nmC[:, i:i + 1],
                              accum_out=rsC[:, i:i + 1]).then_inc(m["c_exp"], 1)

            def l_copy(i):
                b, k = divmod(i, KT)
                act.wait_ge(m["l_filled"], i + 1)
                if b:
                    act.wait_ge(m["dispatched"], i - KT + 1)
                sc.copy(ls[:, k, :], bank(logit_bank(i), 2)).then_inc(m["l_copied"], 1)

            def d_exps(b, k):
                i = b * KT + k
                act.wait_ge(m["d_shifted"], i + 1)
                sc.activation(ls[:, k, :], ls[:, k, :], ACT.Exp).then_inc(m["d_exp"], 1)

            for s in range(KT + 2):
                if s < KT:
                    x2_tile(2 * s)
                if 1 <= s < KT + 1:
                    x2_hi(s - 1)
                if 2 <= s:
                    l_copy(s - 2)
                if s >= 3:
                    c_exps(s - 3)
                if s < KT:
                    x2_tile(2 * s + 1)
            x2_hi(KT)
            c_exps(KT - 1)
            d_exps(0, 0)
            for s in range(KT):
                if s + 1 < KT:
                    x2_hi(KT + s + 1)
                    d_exps(0, s + 1)
                l_copy(KT + s)
                c_exps(KT + s)
            for k in range(KT):
                d_exps(1, k)
            meet(act, 3)

            def gelus(g):
                act.wait_ge(m["hid_filled"], g + 1)
                if g >= 2:
                    act.wait_ge(m["hT_filled"], g - 1)
                sc.activation(hs[:, g % 2, :], bank(0)[:, 0:HID], ACT.Gelu).then_inc(m["hid_gelu"], 1)

            def c_turn(u):
                act.wait_ge(m["cT_filled"], u + 1)
                if u >= 2:
                    act.wait_ge(m["yp_filled"], KT * (u - 1))
                sc.copy(ct[:, u % 2].rearrange("p k c -> p (k c)"), bank(3, 2)).then_inc(m["cT_copied"], 1)

            LAG = 4
            for s in range(NG + LAG):
                if s < NG:
                    gelus(s)
                if LAG - 1 <= s < NG + LAG - 1:
                    c_turn(s - LAG + 1)

        @block.vector
        def _(dve):
            v = nc.vector
            vc = [0]

            def link(ins):
                vc[0] += 1
                ins.then_inc(m["v_chain"], 1)
                dve.wait_ge(m["v_chain"], vc[0])

            def bc(ap, shape):
                return ap.broadcast_to(shape)

            dve.wait_ge(m["in_ids"], 64)
            v.tensor_copy(idsf[:], ids[:]).then_inc(m["idsf_ready"], 1)
            dve.wait_ge(m["ids_permuted"], 1)
            v.tensor_copy(idx[:], bank(5)[:, 0:NB * (KT + 1)]).then_inc(m["idx_ready"], 1)
            dve.wait_ge(m["in_tok"], 16 * 5)
            link(v.tensor_copy(linkf[:], links[:]))
            link(v.tensor_tensor(eq[:], bc(idsf[:, 1:C + 1].unsqueeze(2), [P, C, NL]),
                                 bc(linkf[:].unsqueeze(1), [P, C, NL]), ALU.is_equal))
            link(v.tensor_reduce(maskP[:], eq[:], AX, ALU.max))
            v.tensor_tensor(maskP[:], maskP[:], valid[:], ALU.mult).then_inc(m["maskp_ready"], 1)
            dve.wait_ge(m["mask_permuted"], 1)
            v.tensor_copy(mask[:], bank(4)[:, 0:NT]).then_inc(m["mask_ready"], 1)
            dve.wait_ge(m["mask_ready"], 1)
            v.tensor_reduce(msum[:], mask[:], AX, ALU.add).then_inc(m["msum_ready"], 1)
            dve.wait_ge(m["count_ready"], 1)
            link(v.tensor_scalar(cnt[:, 0:1], bank(3)[:, 0:1], float(HEADS), 1.0, ALU.mult, ALU.max))
            link(v.reciprocal(cnt[:, 1:2], cnt[:, 0:1]))
            v.tensor_scalar(cnt[:, 2:3], cnt[:, 1:2], -TRACE_DECAY * ERASE_LR, None, ALU.mult)
            v.tensor_scalar(cnt[:, 3:4], cnt[:, 1:2], TRACE_LR, None, ALU.mult).then_inc(m["cnt_ready"], 1)

            v.tensor_tensor(wpt[:, :, 0:D], wp[:], bc(gam[:].unsqueeze(1), [P, HP, D]), ALU.mult)
            v.tensor_tensor(wpt[:, :, D:D + DB], wp[:, :, P:D], bc(gam[:, P:D].unsqueeze(1), [P, HP, DB]), ALU.mult)
            link(v.tensor_tensor(wpt[:, :, CB2:CB2 + DB], wp[:, :, P:D], bc(gam[:, P:D].unsqueeze(1), [P, HP, DB]), ALU.mult))
            link(v.tensor_tensor(wp[:], wp[:], bc(bet[:].unsqueeze(1), [P, HP, D]), ALU.mult))
            v.tensor_reduce(wpt[:, :, CB2 + DB:CB2 + DB + 1], wp[:].unsqueeze(2), AX, ALU.add)
            v.tensor_reduce(wpt[:, :, CB2 + DB + 1:PC], wp[:].unsqueeze(2), AX, ALU.add).then_inc(m["wpt_ready"], 1)

            def take(name):
                dve.wait_ge(m["setup_filled"], at[name] + 1)
                return setup_bank(name)

            def taken(ins):
                ins.then_inc(m["setup_taken"], 1)

            def f(ap):
                return ap.bitcast(F32)

            def form_p(name, Ah, Al, B1, B2, n, copies=(None, None)):
                d = take(name)
                part = name[-2:]
                if part == "B1":
                    link(v.tensor_copy(B1[:], d[:, 0:n]))
                    taken(v.tensor_tensor(B1[DB:P, :], d[DB:P, 0:n], f(B1[DB:P, :]), ALU.subtract))
                elif part == "B2":
                    link(v.tensor_copy(B2[:], d[0:DB + 2, 0:n]))
                    if copies[1] is not None:
                        v.tensor_copy(copies[1], d[0:DB + 1, 0:n])
                    link(v.tensor_tensor(B2[DB:DB + 2, :], d[DB:DB + 2, 0:n], f(B2[DB:DB + 2, :]), ALU.subtract))
                    taken(v.tensor_copy(B2[DB:DB + 1, :], d[DB:DB + 1, 0:n]))
                else:
                    link(v.tensor_copy(Ah[:], d[:, 0:n]))
                    if copies[0] is not None:
                        v.tensor_copy(copies[0], d[:, 0:n])
                    taken(v.tensor_tensor(Al[:], d[:, 0:n], f(Ah[:]), ALU.subtract))

            def receive(name):
                if name in ("wqT", "wkT", "wvT3"):
                    y = ("wqT", "wkT", "wvT3").index(name)
                    w = (wTq, wTk, wTv)[y]
                    dve.wait_ge(m["in_attn"], 16 * 10)
                    d = take(name)
                    scale = SCALE if y == 0 else 1.0
                    for c, n in enumerate((P, DB)):
                        v.tensor_scalar(w[0:n, c, 0:D], d[0:n, c * D:(c + 1) * D], scale, None, ALU.mult)
                        last = v.tensor_scalar(w[0:n, c, D:D + DB], d[0:n, c * D + P:(c + 1) * D], scale, None, ALU.mult)
                        if y != 1:
                            v.tensor_scalar(w[0:n, c, CB2:CB2 + DB], d[0:n, c * D + P:(c + 1) * D], scale, None, ALU.mult)
                            last = v.tensor_scalar(w[0:n, c, CB2 + DB:PC], bc(bcol[0:n, c, y:y + 1], [n, 2]), scale, None,
                                                   ALU.mult)
                    taken(last)
                elif name[0] == "k":
                    form_p(name, kAh, kAl, kB1, kB2, P + 2 * DB)
                elif name[0] == "v":
                    form_p(name, vAh, vAl, vB1, vB2, W2N)
                elif name == "tvA":
                    taken(v.tensor_copy(wvT[:, 0, :], take(name)))
                elif name == "tvB":
                    taken(v.tensor_copy(wvT[0:DB, 1, :], take(name)[0:DB, :]))
                elif name == "toA":
                    taken(v.tensor_copy(woT[:, :, 0:P], take(name).rearrange("p (t c) -> p t c", t=HP)))
                elif name == "toB":
                    taken(v.tensor_copy(woT[:, :, P:D], take(name)[:, 0:HP * DB].rearrange("p (t c) -> p t c", t=HP)))
                elif name == "bpA":
                    taken(v.tensor_scalar(bs[:, 0, :], take(name), cnt[:, 3:4], None, ALU.mult))
                else:
                    taken(v.tensor_scalar(bs[0:DB, 1, :], take(name)[0:DB, :], cnt[0:DB, 3:4], None, ALU.mult))

            for name in SETUP[0:3]:
                form_p(name, wpAh, wpAl, wpB1, wpB2, HD, (wpT[:, 0, :], wpT[0:DB + 1, 1, :]))
            for r in range(2):
                rows = slice(r * DT, (r + 1) * DT)
                v.tensor_scalar(eyeP[rows, :], ident[rows, rows], TRACE_DECAY, None, ALU.mult)

            def stats(i):
                t = (i // KT) * (KT + 1) + i % KT
                dve.wait_ge(gathered[t], 16)
                link(v.bn_stats(st6[:, i, :], tok[:, t, :]))
                v.bn_aggr(mv[:, i, :], st6[:, i, :]).then_inc(m["front_stats"], 1)

            def lo_parts(i):
                b, k = divmod(i, KT)
                lo = (b * SLOTS + 2 * k + 1) * Q
                dve.wait_ge(m["xh_copied"], i + 1)
                d = bank(i % 2)
                v.tensor_tensor(XL[:, 0, lo:lo + P], d[:, 0:P], f(XH[:, 0, lo:lo + P]), ALU.subtract)
                ins = v.tensor_tensor(XL[0:DB, 1, lo:lo + P], d[0:DB, P:2 * P], f(XH[0:DB, 1, lo:lo + P]), ALU.subtract)
                ins.then_inc(m["xl_ready"], 1)
                if k == KT - 1:
                    dve.wait_ge(m["xl_ready"], i + 1)
                    z, e = b * SLOTS * Q, (b * SLOTS + SLOTS - 1) * Q
                    v.tensor_copy(XH[:, :, z + 1:z + Q], f(XH[:, :, e:e + Q - 1]))
                    v.tensor_copy(XL[:, :, z + 1:z + Q], f(XL[:, :, e:e + Q - 1]))
                    v.memset(f(XH[:, :, z:z + 1]), 0.0)
                    v.memset(f(XL[:, :, z:z + 1]), 0.0).then_inc(m["wn_ready"], 1)

            def norms(i):
                dve.wait_ge(m["q_squared"], i + 1)
                v.tensor_reduce(ss[:, i, :], sq[:, i % 2, :].rearrange("p (h c) -> p h c", h=HEADS), AX,
                                ALU.add).then_inc(m["q_normed"], 1)

            def erase_q(i):
                dve.wait_ge(m["q_fac"], i + 1)
                if i >= 2:
                    dve.wait_ge(m["gram_done"], i - 1)
                v.tensor_tensor(qe[:, i % 2, :].rearrange("p (h c) -> p h c", h=HEADS),
                                q_bank(i).rearrange("p (h c) -> p h c", h=HEADS),
                                bc(fac[:, i, :].unsqueeze(2), [P, HEADS, DT]), ALU.mult).then_inc(m["qe_ready"], 1)

            for i in range(NT):
                stats(i)
            dve.wait_ge(m["xl_ones"], 1)
            for s in range(NT + 6):
                if 2 <= s < NT + 2:
                    lo_parts(s - 2)
                if 4 <= s < NT + 4:
                    norms(s - 4)
                if 5 <= s < NT + 5:
                    erase_q(s - 5)
                if s == NT + 2:
                    dve.wait_ge(m["cprime_done"], NT)
                    v.tensor_copy(cc[:, 0, :], bank(5)[:, 0:D])
                    v.tensor_copy(cc[0:DB + 1, 1, :], bank(5)[0:DB + 1, 256:256 + D]).then_inc(m["cc_ready"], 1)
                if s == NT + 5:
                    dve.wait_ge(m["gram_done"], NT)
                    dve.wait_ge(m["cnt_ready"], 1)
                    v.scalar_tensor_tensor(r1[:], bank(4)[:, 0:HP * DT].rearrange("p (t c) -> p t c", t=HP), cnt[:, 2:3],
                                           bc(eyeP[:].unsqueeze(1), [P, HP, DT]), ALU.mult, ALU.add
                                           ).then_inc(m["r1_ready"], 1)
                if BESIDE[s]:
                    receive(BESIDE[s])

            def traces(k):
                return bank(k)[:, 0:HP * DT].rearrange("p (t c) -> p t c", t=HP)

            dve.wait_ge(m["update_done"], 1)
            link(v.tensor_copy(tt[:], traces(0)))
            dve.wait_ge(m["traces_done"], 1)
            v.tensor_tensor(tt[0:DT], traces(1)[0:DT], tt[0:DT], ALU.add)
            v.tensor_tensor(tt[DT:P], traces(3)[DT:P], tt[DT:P], ALU.add).then_inc(m["tt_ready"], 1)
            dve.wait_ge(m["mix_done"], 2)
            for t in range(1, HP, 2):
                last = v.tensor_copy(mm_[:, t, :], bank(2 + t // 2)[:, 0:D])
            last.then_inc(m["mm_ready"], 1)
            for name in SETUP[-3:]:
                form_p(name, nAh, nAl, nB1, nB2, D)

            dve.wait_ge(m["xl_ones"], 2)
            for s in range(NT + 4):
                if s >= 4:
                    i = s - 4
                    c = slice(i * P, (i + 1) * P)
                    dve.wait_ge(m["x1h_ready"], i + 1)
                    d = bank(3 + i % 2)
                    v.tensor_tensor(X1L[:, 0, c], d[:, 0:P], f(X1H[:, 0, c]), ALU.subtract)
                    v.tensor_tensor(X1L[0:DB, 1, c], d[0:DB, P:2 * P], f(X1H[0:DB, 1, c]), ALU.subtract
                                    ).then_inc(m["x1l_ready"], 1)
                if s < NT:
                    i = s
                    dve.wait_ge(m["h_filled"], i + 1)
                    link(v.bn_stats(st6[:, i, :], h_bank(i)[:, 0:D]))
                    v.tensor_tensor(res[:, i, :], h_bank(i)[:, 0:D], bproj[:], ALU.add).then_inc(m["h_taken"], 1)
                    v.bn_aggr(mv[:, i, :], st6[:, i, :]).then_inc(m["h_stats"], 1)
            meet(dve, 1)
            logit = pr[:, :, D:D + G]
            dve.wait_ge(m["g_gelu"], 1)
            link(v.tensor_reduce(gm[:], logit, AX, ALU.max))
            v.tensor_tensor(logit, logit, bc(gm[:].unsqueeze(2), [P, NT, G]), ALU.subtract).then_inc(m["g_shifted"], 1)
            def q_lo(j):
                blk, c0 = divmod(j, 2)
                n = slice(blk * 512, (blk + 1) * 512)
                dve.wait_ge(m["qph_taken"], j + 1)
                if c0:
                    v.tensor_tensor(qB[DB:P, n], bank(j % 3)[DB:P, :], f(qB[DB:P, n]), ALU.subtract).then_inc(m["qpl_taken"], 1)
                else:
                    v.tensor_tensor(qAl[:, n], bank(j % 3), f(qAh[:, n]), ALU.subtract).then_inc(m["qpl_taken"], 1)

            for j in range(2):
                q_lo(j)
            dve.wait_ge(m["g_exp"], 1)
            link(v.tensor_reduce(gs[:], logit, AX, ALU.add))
            link(v.reciprocal(gs[:], gs[:]))
            dve.wait_ge(m["half_ready"], 1)
            v.tensor_tensor(gw[:, :, 0:G], logit, bc(gs[:].unsqueeze(2), [P, NT, G]), ALU.mult)
            v.tensor_tensor(gw[:, :, DB:DB + G], logit, bc(gs[:].unsqueeze(2), [P, NT, G]), ALU.mult).then_inc(m["gw_ready"], 1)
            dve.wait_ge(m["alpha_exp"], 1)
            link(v.tensor_scalar(aw[:, 2:3], aw[:, 1:2], 1.0, None, ALU.add))
            link(v.reciprocal(aw[:, 2:3], aw[:, 2:3]))
            link(v.tensor_tensor(aw[:, 3:4], aw[:, 1:2], aw[:, 2:3], ALU.mult))
            for j in range(2, 2 * (NT * P // 512)):
                q_lo(j)
            dve.wait_ge(m["ln_filled"], 1)
            v.tensor_copy(lnT[:], bank(5)[0:DH, 0:4 * NE].rearrange("d (w e) -> d w e", w=4)).then_inc(m["ln_taken"], 1)
            dve.wait_ge(m["ph_squared"], 1)
            v.tensor_reduce(pss[:], zz[:].rearrange("d c (n p) -> d c p n", p=NP), AX, ALU.add).then_inc(m["ph_summed"], 1)
            for j in range(NT // 4):
                c = slice(j * 512, (j + 1) * 512)
                d = bank(6 + j % 2)
                dve.wait_ge(m["gwT_hi"], j + 1)
                v.tensor_tensor(gL[:, c], d, f(gD[:, c]), ALU.subtract)
                v.tensor_tensor(gP[DB:P, c], d[DB:P, :], f(gD[DB:P, c]), ALU.subtract).then_inc(m["gwT_taken"], 1)
            for b in range(NB):
                d = bank(b)[:, 0:D]
                dve.wait_ge(m["u_filled"], b + 1)
                link(v.tensor_scalar(uP[:, b, :], d, aw[:, 2:3], None, ALU.mult))
                v.scalar_tensor_tensor(uP[DB:P, b, :], d[DB:P, :], aw[DB:P, 2:3], f(uP[DB:P, b, :]), ALU.mult,
                                       ALU.subtract).then_inc(m["u_taken"], 1)
            dve.wait_ge(m["ph_rsqrt"], 1)
            for half in range(2):
                w = phT[:, half, :].rearrange("d (n p) -> d n p", p=NP)
                last = v.tensor_tensor(w, w, bc(prs[:, half, :].unsqueeze(1), [P, NE, NP]), ALU.mult)
            last.then_inc(m["ph_scaled"], 1)
            dve.wait_ge(m["ph_hi"], 1)
            v.tensor_tensor(phAl[:], phT[:, 0, :], f(phAh[:]), ALU.subtract)
            v.tensor_tensor(phB[DB:P, :], phT[DB:P, 1, :], f(phB[DB:P, :]), ALU.subtract)

            def z_tile(i):
                dve.wait_ge(m["gw_copied"], i + 1)
                dve.wait_ge(m["s_filled"], i + 1)
                if i >= 2:
                    dve.wait_ge(m["et_filled"], 2 * (i - 1))
                v.scalar_tensor_tensor(zz[:, i % 2, :], bank(0, 2), pr[:, i, W2N - 1:W2N], gws[:], ALU.add,
                                       ALU.mult).then_inc(m["z_ready"], 1)
                dve.wait_ge(m["z_ready"], i + 1)
                v.tensor_reduce(nmx[:, i:i + 1], zz[:, i % 2, :], AX, ALU.max, negate=True).then_inc(m["norm_ready"], 1)

            def turn(i):
                dve.wait_ge(m["et_filled"], 2 * i + 2)
                if i >= 1:
                    dve.wait_ge(m["o_filled"], i)
                v.tensor_copy(et[:, KT // 2:KT, :].rearrange("p k c -> p (k c)"), bank(5)).then_inc(m["et_copied_v"], 1)

            def weight(i):
                dve.wait_ge(m["e_ready"], i + 1)
                link(v.reciprocal(rinv[:, i:i + 1], rsum[:, i:i + 1]))
                link(v.tensor_scalar(cn[:, i:i + 1], rinv[:, i:i + 1], aw[:, 3:4], None, ALU.mult))

            def finish(i):
                d = bank(6 + i % 2)
                dve.wait_ge(m["o_filled"], i + 1)
                link(v.tensor_tensor(res[:, i, :], d[:, 256:256 + D], res[:, i, :], ALU.add))
                v.scalar_tensor_tensor(res[:, i, :], d[:, 0:D], cn[:, i:i + 1], res[:, i, :], ALU.mult,
                                       ALU.add).then_inc(m["o_taken"], 1)
                dve.wait_ge(m["o_taken"], i + 1)
                link(v.bn_stats(st6[:, i, :], res[:, i, :]))
                v.bn_aggr(mv[:, i, :], st6[:, i, :]).then_inc(m["f_stats"], 1)

            for s in range(NT + 1):
                if s >= 1:
                    weight(s - 1)
                    turn(s - 1)
                if s < NT:
                    z_tile(s)
                if s >= 1:
                    finish(s - 1)
            meet(dve, 2)

            v.memset(f(X2L[DB:P, :, 1, :]), 1.0)
            v.memset(x2[:, :, 0:1], 1.0).then_inc(m["x2l_ones"], 1)

            def x2_lo(i):
                dve.wait_ge(m["x2h_ready"], i + 1)
                d = bank(2 + i % 2)
                if i >= 2:
                    dve.wait_ge(m["l_filled"], i - 1)
                v.tensor_tensor(X2L[:, i % 2, 0, :], d[:, 0:P], f(X2H[:, i % 2, 0, :]), ALU.subtract)
                v.tensor_tensor(X2L[0:DB, i % 2, 1, :], d[0:DB, P:2 * P], f(X2H[0:DB, i % 2, 1, :]), ALU.subtract
                                ).then_inc(m["x2l_ready"], 1)

            def l_max(i):
                dve.wait_ge(m["l_copied"], i + 1)
                v.tensor_reduce(nmC[:, i:i + 1], ls[:, i % KT, :], AX, ALU.max, negate=True
                                ).then_inc(m["lmax_ready"], 1)

            def l_top(i):
                b, k = divmod(i, KT)
                if k == 0:
                    if b:
                        dve.wait_ge(m["ctop_ready"], b)
                    v.tensor_copy(top[:], ls[:, 0, :]).then_inc(m["top_ready"], 1)
                else:
                    dve.wait_ge(m["top_ready"], i)
                    v.tensor_tensor(top[:], top[:], ls[:, k, :], ALU.max).then_inc(m["top_ready"], 1)

            def xs_tiles(b):
                acc = bank(4, 4).rearrange("p (t c) -> p t c", c=256)
                dve.wait_ge(m["dispatched"], KT * (b + 1))
                if b:
                    dve.wait_ge(m["xsT_filled"], b)
                link(v.reciprocal(ci[:, b, :], acc[:, :, 0]))
                v.tensor_tensor(xs[:], acc[:, :, 1:1 + D], bc(ci[:, b, :].unsqueeze(2), [P, ST, D]), ALU.mult
                                ).then_inc(m["xs_taken"], 1)
                dve.wait_ge(m["xs_taken"], b + 1)
                for t in range(ST):
                    last = v.bn_stats(xst6[:, t, :], xs[:, t, :])
                link(last)
                for t in range(ST):
                    last = v.bn_aggr(xmv[:, t, :], xst6[:, t, :])
                last.then_inc(m["xs_stats"], 1)
                dve.wait_ge(m["xs_rstd"], b + 1)
                for t in range(ST):
                    last = v.tensor_scalar(xs[:, t, :], xs[:, t, :], xmv[:, t, 0:1], xve[:, t:t + 1], ALU.subtract, ALU.mult)
                last.then_inc(m["xs_norm"], 1)

            def xsT_tiles(b):
                dve.wait_ge(m["xsT_filled"], b + 1)
                for half in range(2):
                    dst = xsT[0:DH, half, :, b, :]
                    src = bank(2 * half, 2)[0:DH, :].rearrange("d (e s) -> d e s", s=NP)
                    link(v.tensor_tensor(dst, src, bc(lnT[:, half, :].unsqueeze(2), [DH, NE, NP]), ALU.mult))
                    last = v.tensor_tensor(dst, dst, bc(lnT[:, 2 + half, :].unsqueeze(2), [DH, NE, NP]), ALU.add)
                last.then_inc(m["xsT_ready"], 1)

            for s in range(KT + 2):
                if 1 <= s < KT + 1:
                    x2_lo(s - 1)
                if s >= 2:
                    l_max(s - 2)
                    l_top(s - 2)
            x2_lo(KT)
            for s in range(KT):
                l_max(KT + s)
                if s + 1 < KT:
                    x2_lo(KT + s + 1)
                l_top(KT + s)
            xs_tiles(0)
            dve.wait_ge(m["ctop_ready"], 2)
            for k in range(KT):
                dve.wait_ge(m["c_exp"], KT + k + 1)
                v.tensor_tensor(ls[:, k, :], ls[:, k, :], ctop[:], ALU.subtract).then_inc(m["d_shifted"], 1)
                if k == 0:
                    xsT_tiles(0)
            xs_tiles(1)
            xsT_tiles(1)
            v.reciprocal(riC[:], rsC[:])
            meet(dve, 3)

            def h_turn(g):
                dve.wait_ge(m["hT_filled"], g + 1)
                if g >= 2:
                    dve.wait_ge(m["y_filled"], g - 1)
                v.tensor_copy(hT[:, g % 2].rearrange("p c r -> p (c r)"), bank(1)[:, 0:HC * P]).then_inc(m["hT_ready"], 1)

            def y_bias(g):
                dve.wait_ge(m["y_filled"], g + 1)
                if g >= 2:
                    dve.wait_ge(ys_stored[g % 2], 16 * (g // 2))
                v.tensor_tensor(ysb[:, g % 2, :], bank(2)[:, 0:D], b2r[g % RING][:], ALU.add).then_inc(m["y_ready"], 1)

            def add_up(u):
                t, b = divmod(u, NB)
                for k in range(KT):
                    q, i = u * KT + k, b * KT + k
                    dve.wait_ge(m["yp_filled"], q + 1)
                    if t:
                        dve.wait_ge(m["yp_taken"], NT * (t - 1) + i + 1)
                    v.scalar_tensor_tensor(res[:, i, :], bank(5 + q % 3)[:, 0:D], riC[:, i:i + 1], res[:, i, :],
                                           ALU.mult, ALU.add).then_inc(m["yp_taken"], 1)

            LAG = 4
            for s in range(NG + LAG + 1):
                if LAG <= s < NG + LAG:
                    add_up(s - LAG)
                if s < NG:
                    h_turn(s)
                    dve.wait_ge(w_loaded[s % RING], 16 * (3 + GE) * (s // RING + 1))
                    y_bias(s)


INPUTS = ["x", "L0_tok_link_ids", "L0_tok_wte", "L0_tok_gamma", "L0_tok_beta", "L0_tok_W_proj", "L0_tok_W_val",
          "L0_tok_W_out", "L0_tok_value_traces", "L0_attn_W_qkv", "L0_attn_b_qkv", "L0_attn_W_proj",
          "L0_attn_b_proj", "L0_attn_W_gp", "L0_attn_alpha", "L0_ffn_phi", "L0_ffn_ln_g", "L0_ffn_ln_b",
          "L0_ffn_w1", "L0_ffn_b1", "L0_ffn_w2", "L0_ffn_b2"]


def kernel(**inputs):
    import numpy as np
    import concourse.bacc as bacc
    from concourse.bass_utils import run_bass_kernel_spmd as run

    nc = bacc.Bacc("TRN2", target_bir_lowering=False, num_devices=1)
    arrays, args = {}, {}
    data = {n: np.ascontiguousarray(inputs[n]) for n in INPUTS}
    data["L0_attn_alpha"] = data["L0_attn_alpha"].reshape(1, 1)
    nb, s = data["x"].shape
    d = data["L0_tok_wte"].shape[1]
    data["c_ident"] = np.eye(P, dtype=np.float32)
    per = nb * s // P
    data["c_valid"] = ((np.arange(nb * s) % s) < s - 2).astype(np.float32).reshape(P, per)
    for n, v in data.items():
        arrays[f"in_{n}"] = v
        args[n] = nc.dram_tensor(f"in_{n}", v.shape, mybir.dt.from_np(v.dtype), kind="ExternalInput").ap()
    out = nc.dram_tensor("out", [nb, s, d], F32, kind="ExternalOutput").ap()
    build(nc, args, out)
    r = run(nc, [arrays], core_ids=[0])
    return r.results[0]["out"]
```

```python
from contextlib import ExitStack

import concourse.bass as bass
from concourse import mybir

F32 = mybir.dt.float32
F32R = mybir.dt.float32r
I32 = mybir.dt.int32
ALU = mybir.AluOpType
ACT = mybir.ActivationFunctionType
AX = mybir.AxisListType.X

P = 128


def build(nc, a, out):
    NB, S = a["x"].shape
    D = a["L0_tok_wte"].shape[1]
    HD = a["L0_tok_W_proj"].shape[0]
    HEADS, DT, _ = a["L0_tok_value_traces"].shape
    G = a["L0_attn_W_gp"].shape[1]
    NE, NP, _ = a["L0_ffn_phi"].shape
    HID = a["L0_ffn_w1"].shape[2]
    NL = a["L0_tok_link_ids"].shape[0]
    DB = D - P
    Q = 64
    KT = S // P
    NT = NB * KT
    C = S // Q
    SLOTS = C + 1
    HP = HD // P
    PC = P + 3 * DB + 2
    CB1, CB2 = P, P + 2 * DB
    W2N = D + G + 1
    NS = NE * NP
    ST = NS // P
    PAIRS = ST // 2
    EPT = P // NP
    YR = 3
    YB = 3
    GE = 4
    NG = NE // GE
    DH = D // 2
    HC = HID // P
    SCALE = float(D) ** -0.5
    TRACE_LR, TRACE_DECAY, ERASE_LR = 0.1, 0.99, 1.0

    ctx = ExitStack()
    early = ExitStack()
    front = ExitStack()
    late = ExitStack()
    moe_in = ExitStack()
    last_read = ExitStack()

    def sb(name, shape, dt=F32, where=None, side="left"):
        return (where or ctx).enter_context(nc.sbuf_tensor(name, shape, dt, side=side))

    def sem(name):
        return ctx.enter_context(nc.semaphore(name))

    with ctx:
        ident = sb("ident", [P, P])
        res = sb("res", [P, NT, D])
        ph = sb("ph", [P, 3, NS], F32R, last_read, "right")
        phAh, phAl, phB = ph[:, 0, :], ph[:, 1, :], ph[:, 2, :]
        lnT = sb("lnT", [DH, 4, NE])
        st6 = sb("st6", [P, NT, 6])
        mv = sb("mv", [P, NT, 2])
        ve = sb("ve", [P, NT])
        rstd = sb("rstd", [P, NT])
        nmr = sb("nmr", [P, NT])
        mhalf = sb("mhalf", [P, 32])
        aw = sb("aw", [P, 4])
        X1H = sb("X1H", [P, 2, NT * P], F32R, early)
        X1L = sb("X1L", [P, 2, NT * P], F32R, early)
        pr = sb("pr", [P, NT, W2N], where=early)
        x1t = sb("x1t", [P, 3, P + 2 * DB], where=early)
        wqkA = sb("wqkA", [P, 3 * D], where=early)
        wqkB = sb("wqkB", [DB, 3 * D], where=early)
        bcol = sb("bcol", [P, 2, 3], where=early)
        wpg = sb("wpg", [P, 2, D + G], where=early)
        bproj = sb("bproj", [P, D], where=early)
        wTq = sb("wTq", [P, 2, PC], where=early)
        wTk = sb("wTk", [P, 2, P + 2 * DB], where=early)
        wTv = sb("wTv", [P, 2, PC], where=early)
        kAh = sb("kAh", [P, P + 2 * DB], F32R, early)
        kAl = sb("kAl", [P, P + 2 * DB], F32R, early)
        kB1 = sb("kB1", [P, P + 2 * DB], F32R, early)
        kB2 = sb("kB2", [DB + 2, P + 2 * DB], F32R, early)
        vAh = sb("vAh", [P, W2N], F32R, early)
        vAl = sb("vAl", [P, W2N], F32R, early)
        vB1 = sb("vB1", [P, W2N], F32R, early)
        vB2 = sb("vB2", [DB + 2, W2N], F32R, early)
        ids = sb("ids", [P, C + 2], I32, front)
        idsf = sb("idsf", [P, C + 2], where=front)
        idx = sb("idx", [P, NB * (KT + 1)], I32, front)
        links = sb("links", [P, NL], I32, front)
        linkf = sb("linkf", [P, NL], where=front)
        valid = sb("valid", [P, C], where=front)
        eq = sb("eq", [P, C, NL], where=front)
        maskP = sb("maskP", [P, C], where=front)
        mask = sb("mask", [P, NT], where=front)
        msum = sb("msum", [P, 1], where=front)
        ones = sb("ones", [P, P], where=front)
        cnt = sb("cnt", [P, 4], where=front)
        tok = sb("tok", [P, NB * (KT + 1), D], where=front)
        xh = sb("xh", [P, 3, P + 2 * DB], where=front)
        xm = sb("xm", [P, 3, D + 1], where=front)
        XH = sb("XH", [P, 2, NB * SLOTS * Q], F32R, front)
        XL = sb("XL", [P, 2, NB * SLOTS * Q], F32R, front)
        sq = sb("sq", [P, 2, HD], where=front)
        ss = sb("ss", [P, NT, HEADS], where=front)
        fac = sb("fac", [P, NT, HEADS], where=front)
        qe = sb("qe", [P, 2, HD], where=front)
        gam = sb("gam", [P, D], where=front)
        bet = sb("bet", [P, D], where=front)
        wp = sb("wp", [P, HP, D], where=front)
        wpt = sb("wpt", [P, HP, PC], where=front)
        wv = sb("wv", [P, HP, D], where=front)
        woA = sb("woA", [P, HD], where=front)
        woB = sb("woB", [DB, HD], where=front)
        vt = sb("vt", [P, HP, DT], where=front)
        wpAh = sb("wpAh", [P, HD], F32R, front)
        wpAl = sb("wpAl", [P, HD], F32R, front)
        wpB1 = sb("wpB1", [P, HD], F32R, front)
        wpB2 = sb("wpB2", [DB + 2, HD], F32R, front)
        wpT = sb("wpT", [P, 2, HD], where=front)
        wvT = sb("wvT", [P, 2, HD], where=front)
        woT = sb("woT", [P, HP, D], where=front)
        eyeP = sb("eyeP", [P, DT], where=front)
        cc = sb("cc", [P, 2, D], where=front)
        r1 = sb("r1", [P, HP, DT], where=front)
        bs = sq
        tt = sb("tt", [P, HP, DT], where=front)
        mm_ = qe[:].rearrange("p a b -> p (a b)")[:, 0:HP * D].rearrange("p (t c) -> p t c", t=HP)
        nAh = sb("nAh", [P, D], F32R, front)
        nAl = sb("nAl", [P, D], F32R, front)
        nB1 = sb("nB1", [P, D], F32R, front)
        nB2 = sb("nB2", [DB + 2, D], F32R, front)
        front.close()
        qAh = sb("qAh", [P, NT * P], F32R, late)
        qAl = sb("qAl", [P, NT * P], F32R, late)
        qB = sb("qB", [P, NT * P], F32R, late)
        gw = sb("gw", [P, NT, P], where=late)
        phsq = gw[:].rearrange("p i c -> p (i c)").rearrange("p (h n) -> p h n", h=2)
        gm = sb("gm", [P, NT], where=late)
        gs = sb("gs", [P, NT], where=late)
        gD = sb("gD", [P, NT * P], F32R, late)
        gL = sb("gL", [P, NT * P], F32R, late)
        gP = sb("gP", [P, NT * P], F32R, late)
        uP = sb("uP", [P, NB, D], F32R, late)
        zz = sb("zz", [P, 2, S], where=late)
        gws = sb("gws", [P, S], where=late)
        et = sb("et", [P, KT, P], where=late)
        nmx = sb("nmx", [P, NT], where=late)
        rsum = sb("rsum", [P, NT], where=late)
        rinv = sb("rinv", [P, NT], where=late)
        cn = sb("cn", [P, NT], where=late)
        phn = sb("phn", [NE, NP, P + 2 * DB], where=late)
        phT = sb("phT", [P, 2, NS], where=late)
        pss = sb("pss", [P, 2, NP], where=late)
        prs = sb("prs", [P, 2, NP], where=late)
        lnn = sb("lnn", [NE, 2, D], where=late)
        late.close()
        early.close()
        ec = sb("ec", [P, NT, NS])
        rsC = sb("rsC", [P, NT])
        riC = sb("riC", [P, NT])
        nmC = sb("nmC", [P, NT])
        xsT = sb("xsT", [DH + 1, 2, NE, NB, NP])
        RING = 4
        W1N, W2C = GE * 2 * HID, GE * HC * D
        XN = 1 + P + 2 * DB
        x2a = sb("x2a", [P, KT, XN], where=last_read, side="right")
        X2H = sb("X2H", [P, 2, 2, P], F32R, last_read, "right")
        X2L = sb("X2L", [P, 2, 2, P], F32R, last_read, "right")
        last_read.close()
        w1r = [sb("w1r0", [P, W1N]), sb("w1r1", [P, W1N])]
        w2r = [sb("w2r0", [P, W2C]), sb("w2r1", [P, W2C], side="right")]
        b2r = [sb("b2r0", [P, D]), sb("b2r1", [P, D], side="right")]
        w1r.append(sb("w1r2", [P, W1N], side="right"))
        LOW = KT // 2
        ls_high = sb("ls_high", [P, KT - LOW, NS], where=moe_in)
        ls_low = sb("ls_low", [P, LOW, NS], where=moe_in)
        top = sb("top", [P, NS], where=moe_in)
        ctop = sb("ctop", [P, NS], where=moe_in)
        x2b = sb("x2b", [P, KT, XN], where=moe_in)
        xs = sb("xs", [P, ST, D], where=moe_in)
        csq = sb("csq", [P, NB, ST], where=moe_in)
        xst6 = sb("xst6", [P, NB, ST, 6], where=moe_in)
        xmv = sb("xmv", [P, NB, ST, 2], where=moe_in)
        xve = sb("xve", [P, NB, ST], where=moe_in)
        moe_in.close()
        w2r.append(sb("w2r2", [P, W2C]))
        b2r.append(sb("b2r2", [P, D]))
        w1r.append(sb("w1r3", [P, W1N]))
        w2r.append(sb("w2r3", [P, W2C]))
        b2r.append(sb("b2r3", [P, D]))
        w1r = [w[0:DH + 1, 0:W1N].rearrange("p (e c h) -> p e c h", e=GE, c=2) for w in w1r]
        w2r = [w[:, 0:W2C].rearrange("p (e c d) -> p e c d", e=GE, c=HC) for w in w2r]
        hs = sb("hs", [P, 2, HID])
        hT = sb("hT", [P, 2, HC, P])
        ysb = sb("ysb", [P, YB, D])
        ys = sb("ys", [P, YR, NB, D])
        ct = sb("ct", [P, 2, KT, P])
        ys_dram = nc.dram_tensor("ys_dram", [NG, P, D], F32, kind="Internal").ap()

        ps = ctx.enter_context(nc.psum_tensor("ps", [P, 8, 512], F32))

        def bank(k, n=1):
            return ps[:, k:k + n, :].rearrange("p k c -> p (k c)")

        names = """in_ids in_tok in_mix in_attn in_phi barrier v_chain a_chain p_chain idsf_ready ids_permuted idx_ready
            maskp_ready mask_permuted mask_ready msum_ready count_ready cnt_ready wpt_ready setup_filled setup_taken
            ones_ready half_ready front_stats front_rstd xh_ready xT_filled xh_copied xl_ready q_filled q_squared
            q_normed q_fac qe_ready gram_done cprime_done cc_ready xm_ready update_done r1_ready traces_done
            tt_ready mix_done mm_ready xl_ones wn_ready h_filled h_stats h_rstd h_taken x1_ready x1T_filled
            x1h_ready x1l_ready pr_filled pr_taken g_gelu g_shifted g_exp gw_ready gwT_filled gwT_hi gwT_taken
            u_filled u_taken qp_filled qph_taken qpl_taken alpha_exp s_filled gw_filled gw_copied z_ready e_ready
            et_filled et_copied_a et_copied_v o_filled o_taken norm_ready ph_filled ph_copied ph_squared ph_summed
            ph_rsqrt ph_scaled ph_hi f_stats f_rstd x2_ready x2t_ready x2T_filled x2h_ready x2l_ready l_filled
            l_copied lmax_ready c_exp top_ready ctop_ready d_shifted d_shifted_v d_exp dispatched pair_done xs_stats
            xs_rstd xs_norm xsT_filled xsT_ready xsT_ones x2l_ones hid_filled hid_gelu hT_filled hT_ready y_filled
            y_ready cT_filled cT_copied yp_filled yp_taken stored""".split()
        m = {n: sem(n) for n in names}
        gathered = [sem(f"gathered{i}") for i in range(NB * (KT + 1))]
        ys_stored = [sem(f"ys_stored{i}") for i in range(YB)]
        ys_loaded = [sem(f"ys_loaded{i}") for i in range(YR)]
        w1_loaded = [sem(f"w1_loaded{r}") for r in range(RING)]
        w2_loaded = [sem(f"w2_loaded{r}") for r in range(RING)]

        def loaded(g):
            return 16 * 2 * (g // RING + 1)

        ENGINES = 5
        LAG = 4

        def meet(eng, n):
            eng.drain().then_inc(m["barrier"], 1)
            eng.wait_ge(m["barrier"], ENGINES * n)

        block = ctx.enter_context(nc.Block())

        AHEAD = 3
        INNER = KT - 3

        def logit_bank(i):
            return 4 if i < KT + AHEAD and i % 2 else 0

        def ls(b, k):
            return ls_low[:, k % LOW, :] if b or k < LOW else ls_high[:, k - LOW, :]

        def ls_free(eng, k):
            eng.wait_ge(m["dispatched"], k + 1 if k < LOW else INNER + k - LOW + 1)

        def on_pool(b, k):
            return k >= (6 if b else 2)

        def x2(i):
            return x2a[:, i, :] if i < KT else x2b[:, i - KT, :]

        SETUP = ["wpA", "wpB1", "wpB2", "wqT", "wkT", "wvT3", "kA", "kB1", "kB2", "vA", "vB1", "vB2",
                 "tvA", "tvB", "toA", "toB", "bpA", "bpB", "nA", "nB1", "nB2"]
        at = {n: k for k, n in enumerate(SETUP)}

        BESIDE = [None] + SETUP[3:16] + [None] * (NT + 3 - 14) + ["bpA", "bpB", None]
        FIRST, LAST = at["wqT"], at["bpB"]

        def setup_bank(name):
            return bank(7) if FIRST <= at[name] <= LAST else bank(6 + at[name] % 2)

        def q_bank(i):
            return bank((2, 3, 6)[i % 3])

        def h_bank(i):
            return bank((0, 1, 2, 7)[i % 4])

        def store_half(eng, jj):
            o4 = out.rearrange("b (q k j) d -> b q j k d", k=KT, j=2)
            for i in range(0, NT, 4):
                b, k = divmod(i, KT)
                eng.wait_ge(m["yp_taken"], NT * (ST - 1) + i + 4)
                eng.dma_start(o4[b, :, jj, k:k + 4, :], res[jj * Q:(jj + 1) * Q, i:i + 4, :]).then_inc(m["stored"], 16)

        @block.sync
        def _(sp):
            x_rows = a["x"].rearrange("b (q c) -> (b q) c", c=C)
            sp.dma_start(ids[:, 0:C], x_rows).then_inc(m["in_ids"], 16)
            sp.dma_start(ids[0:P - 1, C:C + 2], x_rows[1:P, 0:2]).then_inc(m["in_ids"], 16)
            sp.dma_start(ids[P - 1:P, C:C + 2], x_rows[P - 1:P, 0:2]).then_inc(m["in_ids"], 16)
            sp.dma_start(ident[:], a["c_ident"]).then_inc(m["in_ids"], 16)
            sp.dma_start(links[:], a["L0_tok_link_ids"].unsqueeze(0).broadcast_to([P, NL])).then_inc(m["in_tok"], 16)
            sp.dma_start(valid[:], a["c_valid"]).then_inc(m["in_tok"], 16)
            sp.dma_start(gam[:], a["L0_tok_gamma"].unsqueeze(0).broadcast_to([P, D])).then_inc(m["in_tok"], 16)
            sp.dma_start(bet[:], a["L0_tok_beta"].unsqueeze(0).broadcast_to([P, D])).then_inc(m["in_tok"], 16)
            sp.dma_start(wp[:], a["L0_tok_W_proj"].rearrange("(t p) d -> p t d", p=P)).then_inc(m["in_tok"], 16)
            sp.dma_start(wqkA[:], a["L0_attn_W_qkv"][0:P, :]).then_inc(m["in_attn"], 16)
            sp.dma_start(wqkB[:], a["L0_attn_W_qkv"][P:D, :]).then_inc(m["in_attn"], 16)
            bq = a["L0_attn_b_qkv"].rearrange("(y d) -> d y", y=3)
            sp.dma_start(bcol[:, 0, :], bq[0:P, :], allow_slow_non_contiguous=True).then_inc(m["in_attn"], 16)
            sp.dma_start(bcol[0:DB, 1, :], bq[P:D, :], allow_slow_non_contiguous=True).then_inc(m["in_attn"], 16)
            for c, (lo, n) in enumerate(((0, P), (P, DB))):
                sp.dma_start(wpg[0:n, c, 0:D], a["L0_attn_W_proj"][lo:lo + n, :]).then_inc(m["in_attn"], 16)
                sp.dma_start(wpg[0:n, c, D:D + G], a["L0_attn_W_gp"][lo:lo + n, :]).then_inc(m["in_attn"], 16)
            sp.dma_start(bproj[:], a["L0_attn_b_proj"].unsqueeze(0).broadcast_to([P, D])).then_inc(m["in_attn"], 16)
            sp.dma_start(aw[:, 0:1], a["L0_attn_alpha"].broadcast_to([P, 1])).then_inc(m["in_attn"], 16)
            sp.dma_start(wv[:], a["L0_tok_W_val"].rearrange("(t p) d -> p t d", p=P)).then_inc(m["in_mix"], 16)
            sp.dma_start(woA[:], a["L0_tok_W_out"][0:P, :]).then_inc(m["in_mix"], 16)
            sp.dma_start(woB[:], a["L0_tok_W_out"][P:D, :]).then_inc(m["in_mix"], 16)
            v4 = a["L0_tok_value_traces"].rearrange("(t r) p q -> r p t q", r=2)
            for r in range(2):
                sp.dma_start(vt[r * DT:(r + 1) * DT, :, :], v4[r]).then_inc(m["in_mix"], 16)
            meet(sp, 1)
            sp.dma_start(phn[:, :, 0:D], a["L0_ffn_phi"]).then_inc(m["in_phi"], 16)
            sp.dma_start(phn[:, :, D:D + DB], a["L0_ffn_phi"][:, :, P:D]).then_inc(m["in_phi"], 16)
            sp.dma_start(lnn[:, 0, :], a["L0_ffn_ln_g"]).then_inc(m["in_phi"], 16)
            sp.dma_start(lnn[:, 1, :], a["L0_ffn_ln_b"]).then_inc(m["in_phi"], 16)
            meet(sp, 2)

            def load_w1(g):
                r = g % RING
                e = slice(GE * g, GE * g + GE)
                if g:
                    sp.wait_ge(w1_loaded[(g - 1) % RING], loaded(g - 1))
                sp.dma_start(w1r[r][0:DH, :, :, :].rearrange("r e c h -> r e (c h)"),
                             a["L0_ffn_w1"][e].rearrange("e (r c) h -> r e (c h)", c=2)).then_inc(w1_loaded[r], 16)
                sp.dma_start(w1r[r][DH:DH + 1, :, 1, :], a["L0_ffn_b1"][e].unsqueeze(0)).then_inc(w1_loaded[r], 16)

            def load_w2(g):
                r = g % RING
                e = slice(GE * g, GE * g + GE)
                if g:
                    sp.wait_ge(w2_loaded[(g - 1) % RING], loaded(g - 1))
                sp.dma_start(w2r[r][:].rearrange("r e c d -> r e (c d)"),
                             a["L0_ffn_w2"][e].rearrange("e (r c) d -> r e (c d)", c=HC)).then_inc(w2_loaded[r], 16)
                sp.dma_start(b2r[r][:], a["L0_ffn_b2"][e].unsqueeze(1).broadcast_to([GE, 32, D])).then_inc(w2_loaded[r], 16)

            load_w1(0)
            load_w2(0)
            load_w1(1)
            sp.wait_ge(m["l_filled"], NT)
            load_w2(1)
            sp.wait_ge(m["pair_done"], PAIRS)
            load_w1(2)
            load_w2(2)
            meet(sp, 3)
            load_w1(3)
            load_w2(3)
            for g in range(NG - RING):
                sp.wait_ge(m["hid_filled"], g + 1)
                load_w1(g + RING)
                sp.wait_ge(m["y_ready"], g + 1)
                load_w2(g + RING)
            store_half(sp, 0)
            sp.wait_ge(m["stored"], 16 * 2 * NT // 4)

        @block.gpsimd
        def _(pool):
            pc = [0]

            def link(ins):
                pc[0] += 1
                ins.then_inc(m["p_chain"], 1)
                pool.wait_ge(m["p_chain"], pc[0])

            nc.gpsimd.memset(ones[:], 1.0).then_inc(m["ones_ready"], 1)
            link(nc.gpsimd.memset(mhalf[:], -0.5))
            nc.gpsimd.memset(XL[DB:P, 1, :].bitcast(F32), 1.0).then_inc(m["xl_ones"], 1)
            pool.wait_ge(m["idx_ready"], 1)

            def front_factors(b):
                t = slice(b * KT, (b + 1) * KT)
                pool.wait_ge(m["front_stats"], (b + 1) * KT)
                link(nc.gpsimd.tensor_scalar(ve[:, t], mv[:, t, 1], 1e-5, None, ALU.add))
                link(nc.gpsimd.tensor_tensor(rstd[:, t], ve[:, t], mhalf[:, 0:KT], ALU.pow))
                link(nc.gpsimd.tensor_tensor(nmr[:, t], mv[:, t, 0], rstd[:, t], ALU.mult))
                nc.gpsimd.tensor_scalar(nmr[:, t], nmr[:, t], -1.0, None, ALU.mult).then_inc(m["front_rstd"], 1)

            for i in range(NB * (KT + 1)):
                if i == 14:
                    pool.wait_ge(m["xl_ones"], 1)
                    front_factors(0)
                nc.gpsimd.indirect_dma_start(
                    tok[:, i, :], None, a["L0_tok_wte"], bass.IndirectOffsetOnAxis(ap=idx[:, i:i + 1], axis=0)
                ).then_inc(gathered[i], 16)
            front_factors(1)
            pool.wait_ge(m["front_rstd"], NB)
            nc.gpsimd.memset(X1L[DB:P, 1, :].bitcast(F32), 1.0).then_inc(m["xl_ones"], 1)
            pool.wait_ge(m["xl_ones"], 2)

            def rsqrt(i, eps):
                link(nc.gpsimd.tensor_scalar(ve[:, i:i + 1], mv[:, i, 1:2], eps, None, ALU.add))
                return nc.gpsimd.tensor_tensor(rstd[:, i:i + 1], ve[:, i:i + 1], mhalf[:, 0:1], ALU.pow)

            def head_factors(i):
                pool.wait_ge(m["q_normed"], i + 1)
                link(nc.gpsimd.tensor_scalar(fac[:, i, :], ss[:, i, :], 1e-16, None, ALU.max))
                link(nc.gpsimd.tensor_tensor(fac[:, i, :], fac[:, i, :], mhalf[:, 0:HEADS], ALU.pow))
                nc.gpsimd.tensor_scalar(fac[:, i, :], fac[:, i, :], mask[:, i:i + 1], None, ALU.mult).then_inc(m["q_fac"], 1)

            pool.wait_ge(m["mask_ready"], 1)
            for i in range(NT):
                head_factors(i)

            def ln_factors(i, eps, done):
                link(rsqrt(i, eps))
                nc.gpsimd.tensor_scalar(nmr[:, i:i + 1], mv[:, i, 0:1], rstd[:, i:i + 1], -1.0,
                                        ALU.mult, ALU.mult).then_inc(done, 1)

            for i in range(NT):
                pool.wait_ge(m["h_stats"], i + 1)
                ln_factors(i, 1e-5, m["h_rstd"])
            meet(pool, 1)
            nc.gpsimd.memset(gw[:], 0.0).then_inc(m["half_ready"], 1)
            pool.wait_ge(m["ph_summed"], 1)
            link(nc.gpsimd.tensor_scalar(prs[:], pss[:], 1e-6, None, ALU.add))
            nc.gpsimd.tensor_tensor(prs[:].rearrange("p c k -> p (c k)"), prs[:].rearrange("p c k -> p (c k)"),
                                    mhalf[:, 0:2 * NP], ALU.pow).then_inc(m["ph_rsqrt"], 1)
            for i in range(NT):
                pool.wait_ge(m["f_stats"], i + 1)
                ln_factors(i, 1e-5, m["f_rstd"])
            meet(pool, 2)
            for i in range(KT):
                pool.wait_ge(m["x2_ready"], i + 1)
                nc.gpsimd.tensor_copy(x2(i)[:, 1 + D:1 + D + DB], x2(i)[:, 1 + P:1 + D]).then_inc(m["x2t_ready"], 1)

            def all_tokens_top(b):
                pool.wait_ge(m["x2t_ready"], KT)
                pool.wait_ge(m["top_ready"], (KT - 1) * (b + 1))
                if b:
                    pool.wait_ge(m["d_shifted"], KT - 2)
                    pool.wait_ge(m["d_shifted_v"], 2)
                nc.gpsimd.partition_all_reduce(ctop[:], top[:], P, bass.bass_isa.ReduceOp.max).then_inc(m["ctop_ready"], 1)
                pool.wait_ge(m["ctop_ready"], b + 1)

            def xs_factors(b, j):
                pool.wait_ge(m["xs_stats"], PAIRS * b + j + 1)
                nc.gpsimd.tensor_tensor(xve[:, b, 2 * j:2 * j + 2], xve[:, b, 2 * j:2 * j + 2], mhalf[:, 0:2], ALU.pow
                                        ).then_inc(m["xs_rstd"], 1)

            all_tokens_top(0)
            for k in range(2, KT):
                nc.gpsimd.tensor_tensor(ls(0, k), ec[:, k, :], ctop[:], ALU.subtract).then_inc(m["d_shifted"], 1)
            pool.wait_ge(m["d_shifted"], KT - 2)
            nc.gpsimd.memset(xsT[DH:DH + 1, 1, :, :, :], 1.0).then_inc(m["xsT_ones"], 1)
            pool.wait_ge(m["xsT_ones"], 1)
            all_tokens_top(1)
            for j in range(PAIRS):
                xs_factors(0, j)
            for k in range(6, KT):
                ls_free(pool, k)
                nc.gpsimd.tensor_tensor(ls(1, k), ec[:, KT + k, :], ctop[:], ALU.subtract).then_inc(m["d_shifted"], 1)
            for j in range(PAIRS):
                xs_factors(1, j)
            meet(pool, 3)
            for g in range(NG):
                t = g // 2
                pool.wait_ge(ys_stored[g % YB], 16 * (g // YB + 1))
                if t >= YR and g % 2 == 0:
                    pool.wait_ge(m["yp_filled"], NT * (t - YR + 1))
                rows = slice((g % 2) * GE * NP, (g % 2 + 1) * GE * NP)
                y4 = ys_dram[g].rearrange("(j b s) d -> b j s d", b=NB, s=NP)
                for b in range(NB):
                    nc.gpsimd.dma_start(ys[rows, t % YR, b, :], y4[b]).then_inc(ys_loaded[t % YR], 16)

        @block.tensor
        def _(pe):
            mm = nc.tensor.matmul

            def fill(name):
                k = at[name]
                if FIRST <= k <= LAST + 1:
                    pe.wait_ge(m["setup_taken"], k)
                elif k >= 2:
                    pe.wait_ge(m["setup_taken"], k - 1)
                return setup_bank(name)

            def filled(ins):
                ins.then_inc(m["setup_filled"], 1)

            def permute(dst, src, n):
                for b in range(NB):
                    for jj in range(2):
                        last = mm(dst[jj * Q:(jj + 1) * Q, b * n:(b + 1) * n], ident[:, b * Q:(b + 1) * Q],
                                  src[:, jj:2 * n:2], start=True, stop=True)
                return last

            def product(dst, xH, xL, wAh, wAl, wB1, wB2):
                mm(dst, xH(0, P), wAh, start=True, stop=False)
                mm(dst, xH(0, P), wAl, start=False, stop=False)
                mm(dst, xL(0, P), wAh, start=False, stop=False)
                mm(dst, xH(1, P), wB1, start=False, stop=False)
                return mm(dst, xL(1, DB + 2), wB2, start=False, stop=True)

            pe.wait_ge(m["in_ids"], 64)
            pe.wait_ge(m["idsf_ready"], 1)
            permute(bank(5), idsf, KT + 1).then_inc(m["ids_permuted"], 1)
            pe.wait_ge(m["maskp_ready"], 1)
            permute(bank(4), maskP, KT).then_inc(m["mask_permuted"], 1)
            pe.wait_ge(m["msum_ready"], 1)
            pe.wait_ge(m["ones_ready"], 1)
            mm(bank(3)[:, 0:1], ones[:], msum[:], start=True, stop=True).then_inc(m["count_ready"], 1)

            pe.wait_ge(m["wpt_ready"], 1)
            for name, lo, n in (("wpA", 0, P), ("wpB1", CB1, P), ("wpB2", CB2, DB + 2)):
                d = fill(name)
                for t in range(HP):
                    last = nc.tensor.transpose(d[0:n, t * P:(t + 1) * P], wpt[:, t, lo:lo + n], ident[:])
                filled(last)
            def prepare(name):
                if name in ("wqT", "wkT", "wvT3"):
                    y = ("wqT", "wkT", "wvT3").index(name)
                    pe.wait_ge(m["in_attn"], 16 * 10)
                    d = fill(name)
                    for c, (lo, n) in enumerate(((0, P), (P, DB))):
                        cols = slice(y * D + lo, y * D + lo + n)
                        nc.tensor.transpose(d[0:n, c * D:c * D + P], wqkA[:, cols], ident[:])
                        last = nc.tensor.transpose(d[0:n, c * D + P:(c + 1) * D], wqkB[:, cols], ident[0:DB, 0:DB])
                elif name[0] in "kv":
                    lo, n = {"A": (0, P), "B1": (CB1, P), "B2": (CB2, DB + 2)}[name[1:]]
                    d = fill(name)
                    if name[0] == "k":
                        mm(d[0:n, 0:P + 2 * DB], wTq[:, 0, lo:lo + n], wTk[:, 0, :], start=True, stop=False)
                        last = mm(d[0:n, 0:P + 2 * DB], wTq[0:DB, 1, lo:lo + n], wTk[0:DB, 1, :], start=False, stop=True)
                    else:
                        mm(d[0:n, 0:D + G], wTv[:, 0, lo:lo + n], wpg[:, 0, :], start=True, stop=False)
                        mm(d[0:n, 0:D + G], wTv[0:DB, 1, lo:lo + n], wpg[0:DB, 1, :], start=False, stop=True)
                        mm(d[0:n, D + G:W2N], wTq[:, 0, lo:lo + n], bcol[:, 0, 1:2], start=True, stop=False)
                        last = mm(d[0:n, D + G:W2N], wTq[0:DB, 1, lo:lo + n], bcol[0:DB, 1, 1:2], start=False, stop=True)
                elif name in ("tvA", "tvB"):
                    lo, n = {"tvA": (0, P), "tvB": (P, DB)}[name]
                    pe.wait_ge(m["in_mix"], 16 * 5)
                    d = fill(name)
                    for t in range(HP):
                        last = nc.tensor.transpose(d[0:n, t * P:(t + 1) * P], wv[:, t, lo:lo + n], ident[:])
                elif name in ("toA", "toB"):
                    n, rows = {"toA": (P, woA), "toB": (DB, woB)}[name]
                    d = fill(name)
                    for t in range(HP):
                        last = nc.tensor.transpose(d[:, t * n:(t + 1) * n], rows[:, t * P:(t + 1) * P], ident[0:n, 0:n])
                else:
                    lo, n = {"bpA": (0, P), "bpB": (P, DB)}[name]
                    pe.wait_ge(m["cc_ready"], 1)
                    d = fill(name)
                    mm(d[0:n, :], cc[:, 0, lo:lo + n], wpT[:, 0, :], start=True, stop=False)
                    last = mm(d[0:n, :], cc[0:DB + 1, 1, lo:lo + n], wpT[0:DB + 1, 1, :], start=False, stop=True)
                filled(last)

            def slots(b, s):
                lo = (b * SLOTS + s) * Q
                return slice(lo, lo + P)

            gram = bank(4)[:, 0:HP * DT].rearrange("p (t c) -> p t c", t=HP)
            cpr = bank(5)

            def tok_T(i):
                pe.wait_ge(m["xh_ready"], i + 1)
                if i >= 2:
                    pe.wait_ge(m["xl_ready"], i - 1)
                d = bank(i % 2)
                nc.tensor.transpose(d[:, 0:P], xh[:, i % 3, 0:P], ident[:])
                nc.tensor.transpose(d[:, P:2 * P], xh[:, i % 3, P:P + 2 * DB], ident[:]).then_inc(m["xT_filled"], 1)

            def cprime(i):
                b, k = divmod(i, KT)
                nxt = b * (KT + 1) + k + 1
                pe.wait_ge(m["xm_ready"], i + 1)
                pe.wait_ge(gathered[nxt], 16)
                mm(cpr[:, 0:D], xm[:, i % 3, 0:P], tok[:, nxt, :], start=(i == 0), stop=False, skip_group_check=True)
                mm(cpr[0:DB + 1, 256:256 + D], xm[:, i % 3, P:D + 1], tok[:, nxt, :], start=False, stop=False,
                   skip_group_check=True).then_inc(m["cprime_done"], 1)

            def q_proj(i):
                b, k = divmod(i, KT)
                pe.wait_ge(m["xl_ready"], i + 1)
                if i >= 3:
                    pe.wait_ge(m["qe_ready"], i - 2)
                elif i == 2:
                    pe.wait_ge(m["setup_taken"], FIRST)
                c = slots(b, 2 * k + 1)
                product(q_bank(i), lambda h, n: XH[0:n, h, c], lambda h, n: XL[0:n, h, c],
                        wpAh[:], wpAl[:], wpB1[:], wpB2[:]).then_inc(m["q_filled"], 1)

            def grams(i):
                pe.wait_ge(m["qe_ready"], i + 1)
                for h in range(HEADS):
                    t, r = divmod(h, 2)
                    q = qe[:, i % 2, h * DT:(h + 1) * DT]
                    last = mm(gram[r * DT:(r + 1) * DT, t, :], q, q, start=(i == 0 and t == 0), stop=False,
                              skip_group_check=True)
                last.then_inc(m["gram_done"], 1)

            pe.wait_ge(m["cnt_ready"], 1)
            pe.wait_ge(m["xl_ones"], 1)
            for s in range(NT + 6):
                if 3 <= s < NT + 3:
                    q_proj(s - 3)
                if 6 <= s:
                    grams(s - 6)
                if 1 <= s < NT + 1:
                    tok_T(s - 1)
                if 2 <= s < NT + 2:
                    cprime(s - 2)
                if BESIDE[s]:
                    prepare(BESIDE[s])

            pe.wait_ge(m["setup_taken"], at["bpB"] + 1)
            for h in range(HEADS):
                t, r = divmod(h, 2)
                rows, cols = slice(r * DT, (r + 1) * DT), slice(h * DT, (h + 1) * DT)
                d = bank(0)[rows, t * DT:(t + 1) * DT]
                mm(d, wvT[:, 0, cols], bs[:, 0, cols], start=True, stop=False)
                last = mm(d, wvT[0:DB, 1, cols], bs[0:DB, 1, cols], start=False, stop=True)
            last.then_inc(m["update_done"], 1)
            pe.wait_ge(m["r1_ready"], 1)
            for r in range(2):
                rows = slice(r * DT, (r + 1) * DT)
                for t in range(HP):
                    last = mm(bank(1 + 2 * r)[rows, t * DT:(t + 1) * DT], vt[rows, t, :], r1[rows, t, :], start=True, stop=True)
            last.then_inc(m["traces_done"], 1)
            pe.wait_ge(m["tt_ready"], 1)
            for odd in range(2):
                for t in range(odd, HP, 2):
                    d = bank(2 * odd + t // 2)[:, 0:D]
                    for r in range(2):
                        rows = slice(r * DT, (r + 1) * DT)
                        last = mm(d[rows, :], tt[rows, t, :], woT[rows, t, :], start=True, stop=True)
                last.then_inc(m["mix_done"], 1)
            pe.wait_ge(m["mm_ready"], 2)
            for name, lo, n in (("nA", 0, P), ("nB1", CB1, P), ("nB2", CB2, DB + 2)):
                d = fill(name)
                for t in range(HP):
                    last = mm(d[0:n, 0:D], wpt[:, t, lo:lo + n], mm_[:, t, :], start=(t == 0), stop=(t == HP - 1))
                filled(last)
            pe.wait_ge(m["setup_taken"], len(SETUP))
            pe.wait_ge(m["wn_ready"], NB)

            def mixed(i):
                b, k = divmod(i, KT)
                if i >= 4:
                    pe.wait_ge(m["x1_ready"], i - 3)
                    pe.wait_ge(m["h_taken"], i - 3)
                c = slots(b, 2 * k)
                product(h_bank(i)[:, 0:D], lambda h, n: XH[0:n, h, c], lambda h, n: XL[0:n, h, c],
                        nAh[:], nAl[:], nB1[:], nB2[:]).then_inc(m["h_filled"], 1)

            def x1_T(i):
                pe.wait_ge(m["x1_ready"], i + 1)
                if i >= 2:
                    pe.wait_ge(m["x1l_ready"], i - 1)
                d = bank(3 + i % 2)
                nc.tensor.transpose(d[:, 0:P], x1t[:, i % 3, 0:P], ident[:])
                nc.tensor.transpose(d[:, P:2 * P], x1t[:, i % 3, P:P + 2 * DB], ident[:]).then_inc(m["x1T_filled"], 1)

            def value_proj(i):
                pe.wait_ge(m["x1l_ready"], i + 1)
                if i >= 2:
                    pe.wait_ge(m["pr_taken"], i - 1)
                c = slice(i * P, (i + 1) * P)
                product(bank(5 + i % 2)[:, 0:W2N], lambda h, n: X1H[0:n, h, c], lambda h, n: X1L[0:n, h, c],
                        vAh[:], vAl[:], vB1[:], vB2[:]).then_inc(m["pr_filled"], 1)

            pe.wait_ge(m["xl_ones"], 2)
            for s in range(NT + 5):
                if s < NT:
                    mixed(s)
                if 3 <= s < NT + 3:
                    x1_T(s - 3)
                if 5 <= s:
                    value_proj(s - 5)
            meet(pe, 1)

            j = 0
            for blk in range(NT * P // 512):
                for c0, w in ((0, slice(0, P)), (1, slice(P, P + 2 * DB))):
                    if j >= 4:
                        pe.wait_ge(m["qpl_taken"], j - 3)
                    d = bank(4 + j % 4)
                    n = slice(blk * 512, (blk + 1) * 512)
                    mm(d, kAh[:, w], X1H[:, 0, n], start=True, stop=False)
                    mm(d, kAl[:, w], X1H[:, 0, n], start=False, stop=False)
                    mm(d, kAh[:, w], X1L[:, 0, n], start=False, stop=False)
                    mm(d, kB1[:, w], X1H[:, 1, n], start=False, stop=False)
                    mm(d, kB2[:, w], X1L[0:DB + 2, 1, n], start=False, stop=True).then_inc(m["qp_filled"], 1)
                    j += 1
            pe.wait_ge(m["gw_ready"], 1)
            for j in range(NT // 4):
                for q in range(4):
                    last = nc.tensor.transpose(bank(j)[:, q * P:(q + 1) * P], gw[:, 4 * j + q, :], ident[:])
                last.then_inc(m["gwT_filled"], 1)

            def phi_T(j):
                half, p8 = divmod(j, 2)
                if j >= 2:
                    pe.wait_ge(m["ph_copied"], j - 1)
                d = bank(4 + j % 2)
                for q in range(8):
                    last = nc.tensor.transpose(d[:, q * NE:(q + 1) * NE], phn[:, 8 * p8 + q, half * P:(half + 1) * P],
                                               ident[0:NE, 0:NE])
                last.then_inc(m["ph_filled"], 1)

            def beside_scores():
                for j in range(4):
                    phi_T(j)
                for w in range(4):
                    last = nc.tensor.transpose(bank(6)[0:DH, 256 + w * NE:256 + (w + 1) * NE], lnn[:, w // 2, w % 2:D:2],
                                               ident[0:NE, 0:NE])
                for b in range(NB):
                    d = bank(6 + b)[:, 0:D]
                    for k in range(KT):
                        i = b * KT + k
                        last = mm(d, gw[:, i, :], pr[:, i, 0:D], start=(k == 0), stop=(k == KT - 1))
                    last.then_inc(m["u_filled"], 1)

            pe.wait_ge(m["in_phi"], 64)
            pe.wait_ge(m["qpl_taken"], 8)
            pe.wait_ge(m["gwT_taken"], NT // 4)

            def scores(i):
                b = i // KT
                n = slice(i * P, (i + 1) * P)
                if i >= 1:
                    pe.wait_ge(m["z_ready"], i)
                for hf in range(2):
                    d = bank(hf)
                    c = slice(b * S + hf * 512, b * S + (hf + 1) * 512)
                    mm(d, qAh[:, n], X1H[:, 0, c], start=True, stop=False)
                    mm(d, qAl[:, n], X1H[:, 0, c], start=False, stop=False)
                    mm(d, qAh[:, n], X1L[:, 0, c], start=False, stop=False)
                    mm(d, qB[:, n], X1H[:, 1, c], start=False, stop=False)
                    last = mm(d, qB[0:DB, n], X1L[0:DB, 1, c], start=False, stop=True)
                last.then_inc(m["s_filled"], 1)
                if i >= 1:
                    pe.wait_ge(m["gw_copied"], i)
                for hf in range(2):
                    d = bank(2 + hf)
                    c = slice(b * S + hf * 512, b * S + (hf + 1) * 512)
                    mm(d, gP[0:DB + G, n], gD[0:DB + G, c], start=True, stop=False)
                    last = mm(d, gP[0:G, n], gL[0:G, c], start=False, stop=True)
                last.then_inc(m["gw_filled"], 1)

            def attend(i):
                b = i // KT
                n = slice(i * P, (i + 1) * P)
                pe.wait_ge(m["e_ready"], i + 1)
                if i >= 1:
                    pe.wait_ge(m["et_copied_a"], i)
                    pe.wait_ge(m["et_copied_v"], i)
                else:
                    pe.wait_ge(m["ph_copied"], 4)
                    pe.wait_ge(m["u_taken"], NB)
                for k in range(KT):
                    last = nc.tensor.transpose(bank(4 + k // 4)[:, (k % 4) * P:(k % 4 + 1) * P],
                                               zz[:, i % 2, k * P:(k + 1) * P], ident[:])
                    if k % 4 == 3:
                        last.then_inc(m["et_filled"], 1)
                if i >= 2:
                    pe.wait_ge(m["o_taken"], i - 1)
                d = bank(6 + i % 2)
                mm(d[:, 256:256 + D], gD[0:DB + G, n], uP[0:DB + G, b, :], start=True, stop=False)
                mm(d[:, 256:256 + D], gL[0:G, n], uP[0:G, b, :], start=False, stop=True)
                for k in range(KT):
                    if k == 0:
                        pe.wait_ge(m["et_copied_a"], i + 1)
                    if k == KT // 2:
                        pe.wait_ge(m["et_copied_v"], i + 1)
                    last = mm(d[:, 0:D], et[:, k, :], pr[:, b * KT + k, 0:D], start=(k == 0), stop=(k == KT - 1))
                last.then_inc(m["o_filled"], 1)

            for s in range(NT + 1):
                if s < NT:
                    scores(s)
                if s == 0:
                    beside_scores()
                if s >= 1:
                    attend(s - 1)
            meet(pe, 2)

            def x2_T(i):
                pe.wait_ge(m["x2t_ready" if i < KT else "x2_ready"], i + 1)
                if i >= 2:
                    pe.wait_ge(m["x2l_ready"], i - 1)
                d = bank(2 + i % 2)
                nc.tensor.transpose(d[:, 0:P], x2(i)[:, 1:1 + P], ident[:])
                nc.tensor.transpose(d[:, P:2 * P], x2(i)[:, 1 + P:1 + P + 2 * DB], ident[:]).then_inc(m["x2T_filled"], 1)

            def logits(i):
                pe.wait_ge(m["x2l_ready"], i + 1)
                if i >= 1:
                    n = i if i >= KT + AHEAD else i - 1
                    if n:
                        pe.wait_ge(m["l_copied"], n)
                for hf in range(2):
                    d = bank(logit_bank(i) + hf)
                    c = slice(hf * 512, (hf + 1) * 512)
                    xHt, xLt = X2H[:, i % 2], X2L[:, i % 2]
                    mm(d, xHt[:, 0, :], phAh[:, c], start=True, stop=False)
                    mm(d, xHt[:, 0, :], phAl[:, c], start=False, stop=False)
                    mm(d, xLt[:, 0, :], phAh[:, c], start=False, stop=False)
                    mm(d, xHt[:, 1, :], phB[:, c], start=False, stop=False)
                    last = mm(d, xLt[0:DB, 1, :], phB[0:DB, c], start=False, stop=True)
                last.then_inc(m["l_filled"], 1)

            def dispatch(b, k, pairs):
                i = b * KT + k
                pe.wait_ge(m["d_exp"], i + 1)
                for j in pairs:
                    if k == 0:
                        if b:
                            pe.wait_ge(m["xs_norm"], j + 1)
                        elif j == 0:
                            pe.wait_ge(m["l_copied"], KT + AHEAD)
                    for t in (2 * j, 2 * j + 1):
                        d = bank(4 + j)[:, (t % 2) * 256:(t % 2) * 256 + 1 + D]
                        last = mm(d, ls(b, k)[:, t * P:(t + 1) * P], x2(i)[:, 0:1 + D], start=(k == 0 and t % 2 == 0),
                                  stop=(k == KT - 1), skip_group_check=True)
                return last

            def xs_T(b, j):
                pe.wait_ge(m["xs_norm"], PAIRS * b + j + 1)
                if b:
                    pe.wait_ge(m["xsT_ready"], j + 1)
                for half in range(2):
                    for t in (2 * j, 2 * j + 1):
                        last = nc.tensor.transpose(bank(j)[0:DH, half * 256 + (t % 2) * P:half * 256 + (t % 2 + 1) * P],
                                                   xs[:, t, half:D:2], ident[:])
                last.then_inc(m["xsT_filled"], 1)

            pe.wait_ge(m["x2l_ones"], 1)
            x2_T(0)
            for i in range(KT + AHEAD):
                x2_T(i + 1)
                logits(i)
            for i in range(KT + AHEAD, NT):
                dispatch(0, i - KT - AHEAD, range(PAIRS)).then_inc(m["dispatched"], 1)
                if i + 1 < NT:
                    x2_T(i + 1)
                logits(i)
            for j in range(PAIRS):
                for k in range(INNER, KT):
                    last = dispatch(0, k, (j,))
                last.then_inc(m["pair_done"], 1)
            dispatch(1, 0, range(PAIRS)).then_inc(m["dispatched"], 1)
            pe.wait_ge(m["l_copied"], NT)
            for j in range(PAIRS):
                xs_T(0, j)
            for k in range(1, INNER):
                dispatch(1, k, range(PAIRS)).then_inc(m["dispatched"], 1)
            for j in range(PAIRS):
                for k in range(INNER, KT):
                    last = dispatch(1, k, (j,))
                last.then_inc(m["pair_done"], 1)
                if j >= 2:
                    xs_T(1, j - 2)
            xs_T(1, PAIRS - 2)
            xs_T(1, PAIRS - 1)
            meet(pe, 3)

            def hidden(g):
                r = g % RING
                pe.wait_ge(w1_loaded[r], loaded(g))
                if g >= 1:
                    pe.wait_ge(m["hid_gelu"], g)
                for half in range(2):
                    n = DH + half
                    for j in range(GE):
                        last = mm(bank(0)[32 * j:32 * j + 32, 0:HID],
                                  xsT[0:n, half, GE * g + j, :, :].rearrange("d b s -> d (b s)"),
                                  w1r[r][0:n, j, half, :], start=(half == 0), stop=(half == 1),
                                  tile_position=(0, 32 * j))
                last.then_inc(m["hid_filled"], 1)

            def hidden_T(g):
                pe.wait_ge(m["hid_gelu"], g + 1)
                if g >= 1:
                    pe.wait_ge(m["hT_ready"], g)
                for c in range(HC):
                    last = nc.tensor.transpose(bank(1)[:, c * P:(c + 1) * P], hs[:, g % 2, c:HID:HC], ident[:])
                last.then_inc(m["hT_filled"], 1)

            def expert_out(g):
                r = g % RING
                pe.wait_ge(w2_loaded[r], loaded(g))
                pe.wait_ge(m["hT_ready"], g + 1)
                if g >= 1:
                    pe.wait_ge(m["y_ready"], g)
                for c in range(HC):
                    for j in range(GE):
                        last = mm(bank(2)[32 * j:32 * j + 32, 0:D], hT[:, g % 2, c, 32 * j:32 * j + 32],
                                  w2r[r][:, j, c, :], start=(c == 0), stop=(c == HC - 1), tile_position=(0, 32 * j))
                last.then_inc(m["y_filled"], 1)

            def combine_T(u):
                t, b = divmod(u, NB)
                if u >= 1:
                    pe.wait_ge(m["cT_copied"], u)
                for k in range(KT):
                    last = nc.tensor.transpose(bank(3 + k // 4)[:, (k % 4) * P:(k % 4 + 1) * P],
                                               ec[:, b * KT + k, t * P:(t + 1) * P], ident[:])
                last.then_inc(m["cT_filled"], 1)

            def combine(u):
                t, b = divmod(u, NB)
                pe.wait_ge(m["cT_copied"], u + 1)
                pe.wait_ge(ys_loaded[t % YR], 16 * 2 * NB * (t // YR + 1))
                for k in range(KT):
                    q = u * KT + k
                    if q >= 3:
                        pe.wait_ge(m["yp_taken"], q - 2)
                    mm(bank(5 + q % 3)[:, 0:D], ct[:, u % 2, k, :], ys[:, t % YR, b, :], start=True,
                       stop=True).then_inc(m["yp_filled"], 1)

            hidden(0)
            for s in range(NG + LAG):
                if s < NG:
                    hidden_T(s)
                if s + 1 < NG:
                    hidden(s + 1)
                if LAG - 1 <= s < NG + LAG - 1:
                    combine_T(s - LAG + 1)
                if s < NG:
                    expert_out(s)
                if s >= LAG:
                    combine(s - LAG)

        @block.scalar
        def _(act):
            sc = nc.scalar
            ac = [0]

            def link(ins):
                ac[0] += 1
                ins.then_inc(m["a_chain"], 1)
                act.wait_ge(m["a_chain"], ac[0])

            def normalise(i):
                b, k = divmod(i, KT)
                t = b * (KT + 1) + k
                act.wait_ge(m["front_rstd"], b + 1)
                act.wait_ge(gathered[t], 16)
                if i >= 3:
                    act.wait_ge(m["xT_filled"], i - 2)
                    act.wait_ge(m["xm_ready"], i - 2)
                sc.activation(xh[:, i % 3, 0:D], tok[:, t, :], ACT.Identity, bias=nmr[:, i:i + 1], scale=rstd[:, i:i + 1])
                sc.activation(xh[:, i % 3, D:D + DB], tok[:, t, P:D], ACT.Identity, bias=nmr[:, i:i + 1],
                              scale=rstd[:, i:i + 1]).then_inc(m["xh_ready"], 1)

            def masked(i):
                act.wait_ge(m["xh_ready"], i + 1)
                act.wait_ge(m["mask_ready"], 1)
                if i >= 3:
                    act.wait_ge(m["cprime_done"], i - 2)
                sc.activation(xm[:, i % 3, 0:D], xh[:, i % 3, 0:D], ACT.Copy, scale=mask[:, i:i + 1])
                sc.copy(xm[:, i % 3, D:D + 1], mask[:, i:i + 1]).then_inc(m["xm_ready"], 1)

            def hi_parts(i):
                b, k = divmod(i, KT)
                lo = (b * SLOTS + 2 * k + 1) * Q
                act.wait_ge(m["xT_filled"], i + 1)
                sc.copy(XH[:, :, lo:lo + P], bank(i % 2)[:, 0:2 * P].rearrange("p (h c) -> p h c", h=2)
                        ).then_inc(m["xh_copied"], 1)

            def squares(i):
                act.wait_ge(m["q_filled"], i + 1)
                if i >= 2:
                    act.wait_ge(m["q_normed"], i - 1)
                sc.activation(sq[:, i % 2, :], q_bank(i), ACT.Square).then_inc(m["q_squared"], 1)

            for s in range(NT + 3):
                if 2 <= s < NT + 2:
                    hi_parts(s - 2)
                if s < NT:
                    normalise(s)
                    masked(s)
                if 3 <= s:
                    squares(s - 3)

            act.wait_ge(m["mix_done"], 1)
            for t in range(0, HP, 2):
                last = sc.copy(mm_[:, t, :], bank(t // 2)[:, 0:D])
            last.then_inc(m["mm_ready"], 1)
            for s in range(NT + 6):
                if 4 <= s < NT + 4:
                    i = s - 4
                    act.wait_ge(m["x1T_filled"], i + 1)
                    sc.copy(X1H[:, :, i * P:(i + 1) * P], bank(3 + i % 2)[:, 0:2 * P].rearrange("p (h c) -> p h c", h=2)
                            ).then_inc(m["x1h_ready"], 1)
                if 2 <= s < NT + 2:
                    i = s - 2
                    act.wait_ge(m["h_rstd"], i + 1)
                    if i >= 3:
                        act.wait_ge(m["x1T_filled"], i - 2)
                    d = h_bank(i)
                    sc.activation(x1t[:, i % 3, 0:D], d[:, 0:D], ACT.Identity, bias=nmr[:, i:i + 1], scale=rstd[:, i:i + 1])
                    sc.activation(x1t[:, i % 3, D:D + DB], d[:, P:D], ACT.Identity, bias=nmr[:, i:i + 1],
                                  scale=rstd[:, i:i + 1]).then_inc(m["x1_ready"], 1)
                if s >= 6:
                    i = s - 6
                    act.wait_ge(m["pr_filled"], i + 1)
                    sc.copy(pr[:, i, :], bank(5 + i % 2)[:, 0:W2N]).then_inc(m["pr_taken"], 1)
            meet(act, 1)
            logit = pr[:, :, D:D + G]
            sc.activation(logit, logit, ACT.Gelu).then_inc(m["g_gelu"], 1)
            for j in range(2 * (NT * P // 512)):
                blk, c0 = divmod(j, 2)
                act.wait_ge(m["qp_filled"], j + 1)
                sc.copy((qB if c0 else qAh)[:, blk * 512:(blk + 1) * 512], bank(4 + j % 4)).then_inc(m["qph_taken"], 1)
                if j == 1:
                    act.wait_ge(m["g_shifted"], 1)
                    sc.activation(logit, logit, ACT.Exp).then_inc(m["g_exp"], 1)
                    sc.activation(aw[:, 1:2], aw[:, 0:1], ACT.Exp, scale=-1.0).then_inc(m["alpha_exp"], 1)
            for j in range(NT // 4):
                act.wait_ge(m["gwT_filled"], j + 1)
                c = slice(j * 512, (j + 1) * 512)
                sc.copy(gP[0:DB, c], bank(j)[0:DB, :])
                sc.copy(gD[:, c], bank(j)).then_inc(m["gwT_hi"], 1)

            def phi_parts(s):
                if s == 0:
                    for j in range(4):
                        half, p8 = divmod(j, 2)
                        act.wait_ge(m["ph_filled"], j + 1)
                        sc.copy(phT[:, half, :].rearrange("d (n p) -> d p n", p=NP)[:, 8 * p8:8 * p8 + 8, :],
                                bank(4 + j % 2).rearrange("d (p n) -> d p n", n=NE)).then_inc(m["ph_copied"], 1)
                if s == 1:
                    act.wait_ge(m["ph_copied"], 4)
                    act.wait_ge(m["u_filled"], NB)
                    sc.activation(phsq, phT[:], ACT.Square).then_inc(m["ph_squared"], 1)
                if s == 6:
                    act.wait_ge(m["ph_scaled"], 1)
                    sc.copy(phAh[:], phT[:, 0, :])
                if s == 7:
                    sc.copy(phB[:], phT[:, 1, :]).then_inc(m["ph_hi"], 1)

            def group_weights(i):
                act.wait_ge(m["gw_filled"], i + 1)
                if i >= 1:
                    act.wait_ge(m["z_ready"], i)
                sc.copy(gws[:], bank(2, 2)).then_inc(m["gw_copied"], 1)

            def exps(i):
                act.wait_ge(m["norm_ready"], i + 1)
                sc.activation(zz[:, i % 2, :], zz[:, i % 2, :], ACT.Exp, bias=nmx[:, i:i + 1],
                              accum_out=rsum[:, i:i + 1]).then_inc(m["e_ready"], 1)

            def turn(i):
                act.wait_ge(m["et_filled"], 2 * i + 1)
                if i >= 1:
                    act.wait_ge(m["o_filled"], i)
                sc.copy(et[:, 0:KT // 2, :].rearrange("p k c -> p (k c)"), bank(4)).then_inc(m["et_copied_a"], 1)

            for s in range(NT + 1):
                if s >= 1:
                    exps(s - 1)
                    turn(s - 1)
                if s < NT:
                    group_weights(s)
                phi_parts(s)
            meet(act, 2)

            def x2_tile(i):
                act.wait_ge(m["f_rstd"], i + 1)
                def part(lo, n, at):
                    return sc.activation(x2(i)[:, at:at + n], res[:, i, lo:lo + n], ACT.Identity, bias=nmr[:, i:i + 1],
                                         scale=rstd[:, i:i + 1])
                if i < KT:
                    part(0, D, 1).then_inc(m["x2_ready"], 1)
                else:
                    part(0, D, 1)
                    part(P, DB, 1 + D).then_inc(m["x2_ready"], 1)

            def x2_hi(i):
                act.wait_ge(m["x2T_filled"], i + 1)
                if i >= 2:
                    act.wait_ge(m["l_filled"], i - 1)
                sc.copy(X2H[:, i % 2, :, :], bank(2 + i % 2)[:, 0:2 * P].rearrange("p (h c) -> p h c", h=2)
                        ).then_inc(m["x2h_ready"], 1)

            def wait_shifted(b, k):
                if on_pool(b, k):
                    act.wait_ge(m["d_shifted"], (KT - 2) * b + k - (5 if b else 1))
                else:
                    act.wait_ge(m["d_shifted_v"], 2 * b + k + 1)

            def c_exps(i):
                act.wait_ge(m["lmax_ready"], i + 1)
                wait_shifted(*divmod(i, KT))
                sc.activation(ec[:, i, :], ec[:, i, :], ACT.Exp, bias=nmC[:, i:i + 1],
                              accum_out=rsC[:, i:i + 1]).then_inc(m["c_exp"], 1)

            def l_copy(i):
                act.wait_ge(m["l_filled"], i + 1)
                sc.copy(ec[:, i, :], bank(logit_bank(i), 2)).then_inc(m["l_copied"], 1)

            def d_exps(b, k):
                wait_shifted(b, k)
                sc.activation(ls(b, k), ls(b, k), ACT.Exp).then_inc(m["d_exp"], 1)

            x2_tile(0)
            x2_tile(1)
            x2_hi(0)
            for i in range(NT):
                if i == KT + AHEAD:
                    d_exps(0, 1)
                elif KT + AHEAD < i < NT - 1:
                    d_exps(0, 2 * (i - KT - AHEAD))
                    d_exps(0, 2 * (i - KT - AHEAD) + 1)
                if i + 2 < NT:
                    x2_tile(i + 2)
                if i + 1 < NT:
                    x2_hi(i + 1)
                l_copy(i)
                if i == KT + AHEAD - 1:
                    d_exps(0, 0)
                if i >= NT - 2:
                    c_exps(2 * (i - NT + 2))
                    c_exps(2 * (i - NT + 2) + 1)
            for k in range(4, KT):
                c_exps(k)
            for k in range(KT):
                d_exps(1, k)
                c_exps(KT + k)
            meet(act, 3)

            def gelus(g):
                act.wait_ge(m["hid_filled"], g + 1)
                if g >= 2:
                    act.wait_ge(m["hT_filled"], g - 1)
                sc.activation(hs[:, g % 2, :], bank(0)[:, 0:HID], ACT.Gelu).then_inc(m["hid_gelu"], 1)

            def c_turn(u):
                act.wait_ge(m["cT_filled"], u + 1)
                if u >= 2:
                    act.wait_ge(m["yp_filled"], KT * (u - 1))
                sc.copy(ct[:, u % 2].rearrange("p k c -> p (k c)"), bank(3, 2)).then_inc(m["cT_copied"], 1)

            gelus(0)
            for s in range(NG + LAG):
                if s + 1 < NG:
                    gelus(s + 1)
                if LAG - 1 <= s < NG + LAG - 1:
                    c_turn(s - LAG + 1)
                if s < NG:
                    act.wait_ge(m["y_ready"], s + 1)
                    sc.dma_start(ys_dram[s], ysb[:, s % YB, :]).then_inc(ys_stored[s % YB], 16)
            store_half(act, 1)

        @block.vector
        def _(dve):
            v = nc.vector
            vc = [0]

            def link(ins):
                vc[0] += 1
                ins.then_inc(m["v_chain"], 1)
                dve.wait_ge(m["v_chain"], vc[0])

            def bc(ap, shape):
                return ap.broadcast_to(shape)

            dve.wait_ge(m["in_ids"], 64)
            v.tensor_copy(idsf[:], ids[:]).then_inc(m["idsf_ready"], 1)
            dve.wait_ge(m["ids_permuted"], 1)
            v.tensor_copy(idx[:], bank(5)[:, 0:NB * (KT + 1)]).then_inc(m["idx_ready"], 1)
            dve.wait_ge(m["in_tok"], 16 * 5)
            link(v.tensor_copy(linkf[:], links[:]))
            link(v.tensor_tensor(eq[:], bc(idsf[:, 1:C + 1].unsqueeze(2), [P, C, NL]),
                                 bc(linkf[:].unsqueeze(1), [P, C, NL]), ALU.is_equal))
            link(v.tensor_reduce(maskP[:], eq[:], AX, ALU.max))
            v.tensor_tensor(maskP[:], maskP[:], valid[:], ALU.mult).then_inc(m["maskp_ready"], 1)
            dve.wait_ge(m["mask_permuted"], 1)
            v.tensor_copy(mask[:], bank(4)[:, 0:NT]).then_inc(m["mask_ready"], 1)
            dve.wait_ge(m["mask_ready"], 1)
            v.tensor_reduce(msum[:], mask[:], AX, ALU.add).then_inc(m["msum_ready"], 1)
            dve.wait_ge(m["count_ready"], 1)
            link(v.tensor_scalar(cnt[:, 0:1], bank(3)[:, 0:1], float(HEADS), 1.0, ALU.mult, ALU.max))
            link(v.reciprocal(cnt[:, 1:2], cnt[:, 0:1]))
            v.tensor_scalar(cnt[:, 2:3], cnt[:, 1:2], -TRACE_DECAY * ERASE_LR, None, ALU.mult)
            v.tensor_scalar(cnt[:, 3:4], cnt[:, 1:2], TRACE_LR, None, ALU.mult).then_inc(m["cnt_ready"], 1)

            v.tensor_tensor(wpt[:, :, 0:D], wp[:], bc(gam[:].unsqueeze(1), [P, HP, D]), ALU.mult)
            v.tensor_tensor(wpt[:, :, D:D + DB], wp[:, :, P:D], bc(gam[:, P:D].unsqueeze(1), [P, HP, DB]), ALU.mult)
            link(v.tensor_tensor(wpt[:, :, CB2:CB2 + DB], wp[:, :, P:D], bc(gam[:, P:D].unsqueeze(1), [P, HP, DB]), ALU.mult))
            link(v.tensor_tensor(wp[:], wp[:], bc(bet[:].unsqueeze(1), [P, HP, D]), ALU.mult))
            v.tensor_reduce(wpt[:, :, CB2 + DB:CB2 + DB + 1], wp[:].unsqueeze(2), AX, ALU.add)
            v.tensor_reduce(wpt[:, :, CB2 + DB + 1:PC], wp[:].unsqueeze(2), AX, ALU.add).then_inc(m["wpt_ready"], 1)

            def take(name):
                dve.wait_ge(m["setup_filled"], at[name] + 1)
                return setup_bank(name)

            def taken(ins):
                ins.then_inc(m["setup_taken"], 1)

            def f(ap):
                return ap.bitcast(F32)

            def form_p(name, Ah, Al, B1, B2, n, copies=(None, None)):
                d = take(name)
                part = name[-2:]
                if part == "B1":
                    link(v.tensor_copy(B1[:], d[:, 0:n]))
                    taken(v.tensor_tensor(B1[DB:P, :], d[DB:P, 0:n], f(B1[DB:P, :]), ALU.subtract))
                elif part == "B2":
                    link(v.tensor_copy(B2[:], d[0:DB + 2, 0:n]))
                    if copies[1] is not None:
                        v.tensor_copy(copies[1], d[0:DB + 1, 0:n])
                    link(v.tensor_tensor(B2[DB:DB + 2, :], d[DB:DB + 2, 0:n], f(B2[DB:DB + 2, :]), ALU.subtract))
                    taken(v.tensor_copy(B2[DB:DB + 1, :], d[DB:DB + 1, 0:n]))
                else:
                    link(v.tensor_copy(Ah[:], d[:, 0:n]))
                    if copies[0] is not None:
                        v.tensor_copy(copies[0], d[:, 0:n])
                    taken(v.tensor_tensor(Al[:], d[:, 0:n], f(Ah[:]), ALU.subtract))

            def receive(name):
                if name in ("wqT", "wkT", "wvT3"):
                    y = ("wqT", "wkT", "wvT3").index(name)
                    w = (wTq, wTk, wTv)[y]
                    dve.wait_ge(m["in_attn"], 16 * 10)
                    d = take(name)
                    scale = SCALE if y == 0 else 1.0
                    for c, n in enumerate((P, DB)):
                        v.tensor_scalar(w[0:n, c, 0:D], d[0:n, c * D:(c + 1) * D], scale, None, ALU.mult)
                        last = v.tensor_scalar(w[0:n, c, D:D + DB], d[0:n, c * D + P:(c + 1) * D], scale, None, ALU.mult)
                        if y != 1:
                            v.tensor_scalar(w[0:n, c, CB2:CB2 + DB], d[0:n, c * D + P:(c + 1) * D], scale, None, ALU.mult)
                            last = v.tensor_scalar(w[0:n, c, CB2 + DB:PC], bc(bcol[0:n, c, y:y + 1], [n, 2]), scale, None,
                                                   ALU.mult)
                    taken(last)
                elif name[0] == "k":
                    form_p(name, kAh, kAl, kB1, kB2, P + 2 * DB)
                elif name[0] == "v":
                    form_p(name, vAh, vAl, vB1, vB2, W2N)
                elif name == "tvA":
                    taken(v.tensor_copy(wvT[:, 0, :], take(name)))
                elif name == "tvB":
                    taken(v.tensor_copy(wvT[0:DB, 1, :], take(name)[0:DB, :]))
                elif name == "toA":
                    taken(v.tensor_copy(woT[:, :, 0:P], take(name).rearrange("p (t c) -> p t c", t=HP)))
                elif name == "toB":
                    taken(v.tensor_copy(woT[:, :, P:D], take(name)[:, 0:HP * DB].rearrange("p (t c) -> p t c", t=HP)))
                elif name == "bpA":
                    taken(v.tensor_scalar(bs[:, 0, :], take(name), cnt[:, 3:4], None, ALU.mult))
                else:
                    taken(v.tensor_scalar(bs[0:DB, 1, :], take(name)[0:DB, :], cnt[0:DB, 3:4], None, ALU.mult))

            def stats(i):
                t = (i // KT) * (KT + 1) + i % KT
                dve.wait_ge(gathered[t], 16)
                link(v.bn_stats(st6[:, i, :], tok[:, t, :]))
                v.bn_aggr(mv[:, i, :], st6[:, i, :]).then_inc(m["front_stats"], 1)

            for i in range(KT):
                stats(i)
            for name in SETUP[0:3]:
                form_p(name, wpAh, wpAl, wpB1, wpB2, HD, (wpT[:, 0, :], wpT[0:DB + 1, 1, :]))
            for r in range(2):
                rows = slice(r * DT, (r + 1) * DT)
                v.tensor_scalar(eyeP[rows, :], ident[rows, rows], TRACE_DECAY, None, ALU.mult)

            def lo_parts(i):
                b, k = divmod(i, KT)
                lo = (b * SLOTS + 2 * k + 1) * Q
                dve.wait_ge(m["xh_copied"], i + 1)
                d = bank(i % 2)
                v.tensor_tensor(XL[:, 0, lo:lo + P], d[:, 0:P], f(XH[:, 0, lo:lo + P]), ALU.subtract)
                ins = v.tensor_tensor(XL[0:DB, 1, lo:lo + P], d[0:DB, P:2 * P], f(XH[0:DB, 1, lo:lo + P]), ALU.subtract)
                ins.then_inc(m["xl_ready"], 1)
                if k == KT - 1:
                    dve.wait_ge(m["xl_ready"], i + 1)
                    z, e = b * SLOTS * Q, (b * SLOTS + SLOTS - 1) * Q
                    v.tensor_copy(XH[:, :, z + 1:z + Q], f(XH[:, :, e:e + Q - 1]))
                    v.tensor_copy(XL[:, :, z + 1:z + Q], f(XL[:, :, e:e + Q - 1]))
                    v.memset(f(XH[:, :, z:z + 1]), 0.0)
                    v.memset(f(XL[:, :, z:z + 1]), 0.0).then_inc(m["wn_ready"], 1)

            def norms(i):
                dve.wait_ge(m["q_squared"], i + 1)
                v.tensor_reduce(ss[:, i, :], sq[:, i % 2, :].rearrange("p (h c) -> p h c", h=HEADS), AX,
                                ALU.add).then_inc(m["q_normed"], 1)

            def erase_q(i):
                dve.wait_ge(m["q_fac"], i + 1)
                if i >= 2:
                    dve.wait_ge(m["gram_done"], i - 1)
                v.tensor_tensor(qe[:, i % 2, :].rearrange("p (h c) -> p h c", h=HEADS),
                                q_bank(i).rearrange("p (h c) -> p h c", h=HEADS),
                                bc(fac[:, i, :].unsqueeze(2), [P, HEADS, DT]), ALU.mult).then_inc(m["qe_ready"], 1)

            for i in range(KT, NT):
                stats(i)
            dve.wait_ge(m["xl_ones"], 1)
            for s in range(NT + 6):
                if 2 <= s < NT + 2:
                    lo_parts(s - 2)
                if 4 <= s < NT + 4:
                    norms(s - 4)
                if 5 <= s < NT + 5:
                    erase_q(s - 5)
                if s == NT + 2:
                    dve.wait_ge(m["cprime_done"], NT)
                    v.tensor_copy(cc[:, 0, :], bank(5)[:, 0:D])
                    v.tensor_copy(cc[0:DB + 1, 1, :], bank(5)[0:DB + 1, 256:256 + D]).then_inc(m["cc_ready"], 1)
                if s == NT + 5:
                    dve.wait_ge(m["gram_done"], NT)
                    dve.wait_ge(m["cnt_ready"], 1)
                    v.scalar_tensor_tensor(r1[:], bank(4)[:, 0:HP * DT].rearrange("p (t c) -> p t c", t=HP), cnt[:, 2:3],
                                           bc(eyeP[:].unsqueeze(1), [P, HP, DT]), ALU.mult, ALU.add
                                           ).then_inc(m["r1_ready"], 1)
                if BESIDE[s]:
                    receive(BESIDE[s])

            def traces(k):
                return bank(k)[:, 0:HP * DT].rearrange("p (t c) -> p t c", t=HP)

            dve.wait_ge(m["update_done"], 1)
            link(v.tensor_copy(tt[:], traces(0)))
            dve.wait_ge(m["traces_done"], 1)
            v.tensor_tensor(tt[0:DT], traces(1)[0:DT], tt[0:DT], ALU.add)
            v.tensor_tensor(tt[DT:P], traces(3)[DT:P], tt[DT:P], ALU.add).then_inc(m["tt_ready"], 1)
            dve.wait_ge(m["mix_done"], 2)
            for t in range(1, HP, 2):
                last = v.tensor_copy(mm_[:, t, :], bank(2 + t // 2)[:, 0:D])
            last.then_inc(m["mm_ready"], 1)
            for name in SETUP[-3:]:
                form_p(name, nAh, nAl, nB1, nB2, D)

            dve.wait_ge(m["xl_ones"], 2)
            for s in range(NT + 4):
                if s >= 4:
                    i = s - 4
                    c = slice(i * P, (i + 1) * P)
                    dve.wait_ge(m["x1h_ready"], i + 1)
                    d = bank(3 + i % 2)
                    v.tensor_tensor(X1L[:, 0, c], d[:, 0:P], f(X1H[:, 0, c]), ALU.subtract)
                    v.tensor_tensor(X1L[0:DB, 1, c], d[0:DB, P:2 * P], f(X1H[0:DB, 1, c]), ALU.subtract
                                    ).then_inc(m["x1l_ready"], 1)
                if s < NT:
                    i = s
                    dve.wait_ge(m["h_filled"], i + 1)
                    link(v.bn_stats(st6[:, i, :], h_bank(i)[:, 0:D]))
                    v.tensor_tensor(res[:, i, :], h_bank(i)[:, 0:D], bproj[:], ALU.add).then_inc(m["h_taken"], 1)
                    v.bn_aggr(mv[:, i, :], st6[:, i, :]).then_inc(m["h_stats"], 1)
            meet(dve, 1)
            logit = pr[:, :, D:D + G]
            dve.wait_ge(m["g_gelu"], 1)
            link(v.tensor_reduce(gm[:], logit, AX, ALU.max))
            v.tensor_tensor(logit, logit, bc(gm[:].unsqueeze(2), [P, NT, G]), ALU.subtract).then_inc(m["g_shifted"], 1)
            def q_lo(j):
                blk, c0 = divmod(j, 2)
                n = slice(blk * 512, (blk + 1) * 512)
                dve.wait_ge(m["qph_taken"], j + 1)
                if c0:
                    v.tensor_tensor(qB[DB:P, n], bank(4 + j % 4)[DB:P, :], f(qB[DB:P, n]), ALU.subtract).then_inc(m["qpl_taken"], 1)
                else:
                    v.tensor_tensor(qAl[:, n], bank(4 + j % 4), f(qAh[:, n]), ALU.subtract).then_inc(m["qpl_taken"], 1)

            for j in range(2):
                q_lo(j)
            dve.wait_ge(m["g_exp"], 1)
            link(v.tensor_reduce(gs[:], logit, AX, ALU.add))
            link(v.reciprocal(gs[:], gs[:]))
            dve.wait_ge(m["half_ready"], 1)
            v.tensor_tensor(gw[:, :, 0:G], logit, bc(gs[:].unsqueeze(2), [P, NT, G]), ALU.mult)
            v.tensor_tensor(gw[:, :, DB:DB + G], logit, bc(gs[:].unsqueeze(2), [P, NT, G]), ALU.mult).then_inc(m["gw_ready"], 1)
            dve.wait_ge(m["alpha_exp"], 1)
            link(v.tensor_scalar(aw[:, 2:3], aw[:, 1:2], 1.0, None, ALU.add))
            link(v.reciprocal(aw[:, 2:3], aw[:, 2:3]))
            link(v.tensor_tensor(aw[:, 3:4], aw[:, 1:2], aw[:, 2:3], ALU.mult))
            for j in range(2, 2 * (NT * P // 512)):
                q_lo(j)
            for j in range(NT // 4):
                c = slice(j * 512, (j + 1) * 512)
                d = bank(j)
                dve.wait_ge(m["gwT_hi"], j + 1)
                v.tensor_tensor(gL[:, c], d, f(gD[:, c]), ALU.subtract)
                v.tensor_tensor(gP[DB:P, c], d[DB:P, :], f(gD[DB:P, c]), ALU.subtract).then_inc(m["gwT_taken"], 1)

            def beside(s):
                if s == 0:
                    for b in range(NB):
                        d = bank(6 + b)[:, 0:D]
                        dve.wait_ge(m["u_filled"], b + 1)
                        if b == 0:
                            v.tensor_copy(lnT[:], bank(6)[0:DH, 256:256 + 4 * NE].rearrange("d (w e) -> d w e", w=4))
                        link(v.tensor_scalar(uP[:, b, :], d, aw[:, 2:3], None, ALU.mult))
                        v.scalar_tensor_tensor(uP[DB:P, b, :], d[DB:P, :], aw[DB:P, 2:3], f(uP[DB:P, b, :]), ALU.mult,
                                               ALU.subtract).then_inc(m["u_taken"], 1)
                if s == 2:
                    dve.wait_ge(m["ph_squared"], 1)
                    v.tensor_reduce(pss[:], phsq.rearrange("d c (n p) -> d c p n", p=NP), AX, ALU.add
                                    ).then_inc(m["ph_summed"], 1)
                if s in (4, 5):
                    if s == 4:
                        dve.wait_ge(m["ph_rsqrt"], 1)
                    w = phT[:, s - 4, :].rearrange("d (n p) -> d n p", p=NP)
                    last = v.tensor_tensor(w, w, bc(prs[:, s - 4, :].unsqueeze(1), [P, NE, NP]), ALU.mult)
                    if s == 5:
                        last.then_inc(m["ph_scaled"], 1)
                if s == 8:
                    dve.wait_ge(m["ph_hi"], 1)
                    v.tensor_tensor(phAl[:], phT[:, 0, :], f(phAh[:]), ALU.subtract)
                if s == 9:
                    v.tensor_tensor(phB[DB:P, :], phT[DB:P, 1, :], f(phB[DB:P, :]), ALU.subtract)

            def z_tile(i):
                dve.wait_ge(m["gw_copied"], i + 1)
                dve.wait_ge(m["s_filled"], i + 1)
                if i >= 2:
                    dve.wait_ge(m["et_filled"], 2 * (i - 1))
                v.scalar_tensor_tensor(zz[:, i % 2, :], bank(0, 2), pr[:, i, W2N - 1:W2N], gws[:], ALU.add,
                                       ALU.mult).then_inc(m["z_ready"], 1)
                dve.wait_ge(m["z_ready"], i + 1)
                v.tensor_reduce(nmx[:, i:i + 1], zz[:, i % 2, :], AX, ALU.max, negate=True).then_inc(m["norm_ready"], 1)

            def turn(i):
                dve.wait_ge(m["et_filled"], 2 * i + 2)
                if i >= 1:
                    dve.wait_ge(m["o_filled"], i)
                v.tensor_copy(et[:, KT // 2:KT, :].rearrange("p k c -> p (k c)"), bank(5)).then_inc(m["et_copied_v"], 1)

            def weight(i):
                dve.wait_ge(m["e_ready"], i + 1)
                link(v.reciprocal(rinv[:, i:i + 1], rsum[:, i:i + 1]))
                link(v.tensor_scalar(cn[:, i:i + 1], rinv[:, i:i + 1], aw[:, 3:4], None, ALU.mult))

            def finish(i):
                d = bank(6 + i % 2)
                dve.wait_ge(m["o_filled"], i + 1)
                link(v.tensor_tensor(res[:, i, :], d[:, 256:256 + D], res[:, i, :], ALU.add))
                v.scalar_tensor_tensor(res[:, i, :], d[:, 0:D], cn[:, i:i + 1], res[:, i, :], ALU.mult,
                                       ALU.add).then_inc(m["o_taken"], 1)
                dve.wait_ge(m["o_taken"], i + 1)
                link(v.bn_stats(st6[:, i, :], res[:, i, :]))
                v.bn_aggr(mv[:, i, :], st6[:, i, :]).then_inc(m["f_stats"], 1)

            for s in range(NT + 1):
                if s >= 1:
                    weight(s - 1)
                    turn(s - 1)
                if s < NT:
                    z_tile(s)
                if s >= 1:
                    finish(s - 1)
                beside(s)
            meet(dve, 2)

            v.memset(f(X2L[DB:P, :, 1, :]), 1.0)
            v.memset(x2a[:, :, 0:1], 1.0)
            v.memset(x2b[:, :, 0:1], 1.0).then_inc(m["x2l_ones"], 1)

            def x2_lo(i):
                dve.wait_ge(m["x2h_ready"], i + 1)
                d = bank(2 + i % 2)
                if i >= 2:
                    dve.wait_ge(m["l_filled"], i - 1)
                v.tensor_tensor(X2L[:, i % 2, 0, :], d[:, 0:P], f(X2H[:, i % 2, 0, :]), ALU.subtract)
                v.tensor_tensor(X2L[0:DB, i % 2, 1, :], d[0:DB, P:2 * P], f(X2H[0:DB, i % 2, 1, :]), ALU.subtract
                                ).then_inc(m["x2l_ready"], 1)

            def l_max(i):
                dve.wait_ge(m["l_copied"], i + 1)
                v.tensor_reduce(nmC[:, i:i + 1], ec[:, i, :], AX, ALU.max, negate=True).then_inc(m["lmax_ready"], 1)

            def l_top(i):
                b, k = divmod(i, KT)
                if k == 0:
                    return
                dve.wait_ge(m["l_copied"], i + 1)
                if k == 1:
                    if b:
                        dve.wait_ge(m["ctop_ready"], b)
                    before = ec[:, i - 1, :]
                else:
                    dve.wait_ge(m["top_ready"], (KT - 1) * b + k - 1)
                    before = top[:]
                v.tensor_tensor(top[:], before, ec[:, i, :], ALU.max).then_inc(m["top_ready"], 1)

            def shift(b, k):
                dve.wait_ge(m["ctop_ready"], b + 1)
                if b:
                    ls_free(dve, k)
                v.tensor_tensor(ls(b, k), ec[:, b * KT + k, :], ctop[:], ALU.subtract).then_inc(m["d_shifted_v"], 1)

            acc = bank(4, 4).rearrange("p (t c) -> p t c", c=256)

            def xs_stats(b, j):
                t = slice(2 * j, 2 * j + 2)
                dve.wait_ge(m["pair_done"], PAIRS * b + j + 1)
                v.tensor_copy(csq[:, b, t], acc[:, t, 0])
                for q in (2 * j, 2 * j + 1):
                    last = v.bn_stats(xst6[:, b, q, :], acc[:, q, 1:1 + D])
                link(last)
                v.tensor_tensor(csq[:, b, t], csq[:, b, t], csq[:, b, t], ALU.mult)
                for q in (2 * j, 2 * j + 1):
                    last = v.bn_aggr(xmv[:, b, q, :], xst6[:, b, q, :])
                link(last)
                v.scalar_tensor_tensor(xve[:, b, t], csq[:, b, t], 1e-5, xmv[:, b, t, 1], ALU.mult, ALU.add
                                       ).then_inc(m["xs_stats"], 1)

            def xs_norm(b, j):
                dve.wait_ge(m["xs_rstd"], PAIRS * b + j + 1)
                if b:
                    dve.wait_ge(m["xsT_filled"], j + 1)
                for q in (2 * j, 2 * j + 1):
                    last = v.tensor_scalar(xs[:, q, :], acc[:, q, 1:1 + D], xmv[:, b, q, 0:1], xve[:, b, q:q + 1],
                                           ALU.subtract, ALU.mult)
                last.then_inc(m["xs_norm"], 1)

            def xsT_tiles(b, j):
                dve.wait_ge(m["xsT_filled"], PAIRS * b + j + 1)
                e = slice(2 * EPT * j, 2 * EPT * (j + 1))
                shape = [DH, 2 * EPT, NP]
                for half in range(2):
                    src = bank(j)[0:DH, half * 256:(half + 1) * 256].rearrange("d (e s) -> d e s", s=NP)
                    last = v.tensor_tensor(xsT[0:DH, half, e, b, :], src, bc(lnT[:, half, e].unsqueeze(2), shape), ALU.mult)
                link(last)
                for half in range(2):
                    dst = xsT[0:DH, half, e, b, :]
                    last = v.tensor_tensor(dst, dst, bc(lnT[:, 2 + half, e].unsqueeze(2), shape), ALU.add)
                last.then_inc(m["xsT_ready"], 1)

            x2_lo(0)
            for i in range(NT):
                if i + 1 < NT:
                    x2_lo(i + 1)
                if i == KT + 1:
                    shift(0, 0)
                if i == KT + 2:
                    shift(0, 1)
                l_top(i)
                if i >= KT:
                    l_max(2 * (i - KT))
                    l_max(2 * (i - KT) + 1)
            for j in range(PAIRS - 1):
                xs_stats(0, j)
            shift(1, 0)
            xs_norm(0, 0)
            xs_stats(0, PAIRS - 1)
            xs_norm(0, 1)
            shift(1, 1)
            xs_norm(0, 2)
            xs_norm(0, 3)
            for j in range(PAIRS):
                shift(1, 2 + j)
                xsT_tiles(0, j)
            xs_stats(1, 0)
            for j in range(1, PAIRS):
                xs_stats(1, j)
                xs_norm(1, j - 1)
                if j >= 2:
                    xsT_tiles(1, j - 2)
            xs_norm(1, PAIRS - 1)
            for j in (PAIRS - 2, PAIRS - 1):
                xsT_tiles(1, j)
            dve.wait_ge(m["c_exp"], NT)
            v.reciprocal(riC[:], rsC[:])
            meet(dve, 3)

            def h_turn(g):
                dve.wait_ge(m["hT_filled"], g + 1)
                if g >= 2:
                    dve.wait_ge(m["y_filled"], g - 1)
                v.tensor_copy(hT[:, g % 2].rearrange("p c r -> p (c r)"), bank(1)[:, 0:HC * P]).then_inc(m["hT_ready"], 1)

            def y_bias(g):
                dve.wait_ge(m["y_filled"], g + 1)
                if g >= YB:
                    dve.wait_ge(ys_stored[g % YB], 16 * (g // YB))
                v.tensor_tensor(ysb[:, g % YB, :], bank(2)[:, 0:D], b2r[g % RING][:], ALU.add).then_inc(m["y_ready"], 1)

            def add_up(u):
                t, b = divmod(u, NB)
                for k in range(KT):
                    q, i = u * KT + k, b * KT + k
                    dve.wait_ge(m["yp_filled"], q + 1)
                    if t:
                        dve.wait_ge(m["yp_taken"], NT * (t - 1) + i + 1)
                    v.scalar_tensor_tensor(res[:, i, :], bank(5 + q % 3)[:, 0:D], riC[:, i:i + 1], res[:, i, :],
                                           ALU.mult, ALU.add).then_inc(m["yp_taken"], 1)

            for s in range(NG + LAG):
                if s < NG:
                    h_turn(s)
                    dve.wait_ge(w2_loaded[s % RING], loaded(s))
                    y_bias(s)
                if s >= LAG:
                    add_up(s - LAG)


INPUTS = ["x", "L0_tok_link_ids", "L0_tok_wte", "L0_tok_gamma", "L0_tok_beta", "L0_tok_W_proj", "L0_tok_W_val",
          "L0_tok_W_out", "L0_tok_value_traces", "L0_attn_W_qkv", "L0_attn_b_qkv", "L0_attn_W_proj",
          "L0_attn_b_proj", "L0_attn_W_gp", "L0_attn_alpha", "L0_ffn_phi", "L0_ffn_ln_g", "L0_ffn_ln_b",
          "L0_ffn_w1", "L0_ffn_b1", "L0_ffn_w2", "L0_ffn_b2"]


def kernel(**inputs):
    import numpy as np
    import concourse.bacc as bacc
    from concourse.bass_utils import run_bass_kernel_spmd as run

    nc = bacc.Bacc("TRN2", target_bir_lowering=False, num_devices=1)
    arrays, args = {}, {}
    data = {n: np.ascontiguousarray(inputs[n]) for n in INPUTS}
    data["L0_attn_alpha"] = data["L0_attn_alpha"].reshape(1, 1)
    nb, s = data["x"].shape
    d = data["L0_tok_wte"].shape[1]
    data["c_ident"] = np.eye(P, dtype=np.float32)
    per = nb * s // P
    data["c_valid"] = ((np.arange(nb * s) % s) < s - 2).astype(np.float32).reshape(P, per)
    for n, v in data.items():
        arrays[f"in_{n}"] = v
        args[n] = nc.dram_tensor(f"in_{n}", v.shape, mybir.dt.from_np(v.dtype), kind="ExternalInput").ap()
    out = nc.dram_tensor("out", [nb, s, d], F32, kind="ExternalOutput").ap()
    build(nc, args, out)
    r = run(nc, [arrays], core_ids=[0])
    return r.results[0]["out"]
```
